# Optimizing a Trainium2 kernel written in Bass

```python
import numpy as np
import jax
import jax.numpy as jnp

def _softmax(x, axis=-1):
    return jax.nn.softmax(x, axis=axis)

def _gelu(x):
    return jax.nn.gelu(x, approximate=True)

def _silu(x):
    return jax.nn.silu(x)

def _sigmoid(x):
    return jax.nn.sigmoid(x)

def _layernorm(x, axis=-1, eps=1e-05):
    m = jnp.mean(x, axis=axis, keepdims=True)
    v = jnp.var(x, axis=axis, keepdims=True)
    return (x - m) / jnp.sqrt(v + eps)

def _scatter_add(tgt, idx, src, axis=0):
    return tgt.at[idx].add(src)

def _segment_sum(src, seg, n):
    return jax.ops.segment_sum(src, seg, n)
kernel_name = 'mk_decoder_postln_d1_seqx_r2_18be3a'

def setup_inputs(seed: int=0):
    np.random.seed(seed)
    _w = jnp.asarray

    def _rec_inputs():
        import jax
        import jax.numpy as jnp
        _rk = jax.random.key(seed)
        x = 0.0001212 + 1 * jax.random.normal(jax.random.fold_in(_rk, 1), (16, 256, 2048), jnp.float32)
        _lenS = 256 - jax.random.randint(jax.random.fold_in(_rk, 7), (16,), 0, max(1, 256 // 4) + 1, jnp.int32)
        _lenS2 = 256 - jax.random.randint(jax.random.fold_in(_rk, 8), (16,), 0, max(1, 256 // 4) + 1, jnp.int32)
        _ctx_4096P = jax.random.normal(jax.random.fold_in(_rk, 11), (16, 16, 2048), jnp.float32)
        _ctx_4096c = jax.random.dirichlet(jax.random.fold_in(_rk, 511), 0.3 * jnp.ones((16,), jnp.float32), (16, 256))
        _ctx_4096t = jnp.einsum('bsk,bkd->bsd', _ctx_4096c, _ctx_4096P)
        _ctx_4096t = _ctx_4096t * jax.lax.rsqrt(jnp.mean(jnp.square(_ctx_4096t)) + 1e-12) * 0.953939
        ctx_4096 = -0.000125008 + 0.999885 * (_ctx_4096t + 0.3 * jax.random.normal(jax.random.fold_in(_rk, 611), (16, 256, 2048), jnp.float32))
        return (x, ctx_4096)
    x, ctx_4096 = _rec_inputs()

    def _L0_attn_setup():
        import jax, jax.numpy as jnp
        import numpy as np
        import math
        FACTOR = 1
        key = jax.random.key(seed)
        x = jax.random.normal(key, (8, 256, 2048), dtype=jnp.float32)
        return {'x': x}
    _L0_attn_all = _L0_attn_setup()
    _L0_attn_in = {k: v for k, v in _L0_attn_all.items() if k in ()}
    del _L0_attn_all

    def _L0_xattn_setup():
        import jax, jax.numpy as jnp
        import numpy as np
        N, C, S = (16, 256, 2048)
        rng = jax.random.key(seed)
        k1, k2, k3 = jax.random.split(rng, 3)
        return {'key': jax.random.normal(k1, (N, C, S), dtype=jnp.float32), 'value': jax.random.normal(k2, (N, C, S), dtype=jnp.float32), 'query': jax.random.normal(k3, (N, C, S), dtype=jnp.float32)}
    _L0_xattn_all = _L0_xattn_setup()
    _L0_xattn_in = {k: v for k, v in _L0_xattn_all.items() if k in ()}
    del _L0_xattn_all

    def _L0_ffn_setup():
        import jax, jax.numpy as jnp
        import numpy as np
        E = 8
        R = 8
        DIN = 2048
        DOUT = 2048
        TOP_K = 2
        SCALING = 2.0

        def _moe_lora(xf, gate_W, A, B):
            gate_probs = jax.nn.softmax(xf @ gate_W.T, axis=-1)
            weights, sel = jax.lax.top_k(gate_probs, TOP_K)
            weights = weights / jnp.sum(weights, axis=-1, keepdims=True)
            T = xf.shape[0]
            w_dense = jnp.zeros((T, E), xf.dtype).at[jnp.arange(T)[:, None], sel].add(weights)
            h = jnp.einsum('td,erd->ter', xf, A)
            h = h * (w_dense[:, :, None] * SCALING)
            return jnp.einsum('ter,eor->to', h, B)
        key = jax.random.key(seed)
        k0, k1, k2, k3, k4 = jax.random.split(key, 5)
        x = jax.random.normal(k0, (4, 1024, DIN), jnp.float32)
        W_base = jax.random.normal(k1, (DOUT, DIN), jnp.float32) * 0.02
        gate_W = jax.random.normal(k2, (E, DIN), jnp.float32) * 0.02
        A = jax.random.normal(k3, (E, R, DIN), jnp.float32) * 0.02
        B = jax.random.normal(k4, (E, DOUT, R), jnp.float32) * 0.02
        return {'x': x, 'W_base': W_base, 'gate_W': gate_W, 'A': A, 'B': B}
    _L0_ffn_all = _L0_ffn_setup()
    _L0_ffn_in = {k: v for k, v in _L0_ffn_all.items() if k in ('W_base', 'gate_W', 'A', 'B')}
    del _L0_ffn_all
    return {'x': x, 'ctx_4096': ctx_4096, 'L0_ffn_W_base': _L0_ffn_in['W_base'], 'L0_ffn_gate_W': _L0_ffn_in['gate_W'], 'L0_ffn_A': _L0_ffn_in['A'], 'L0_ffn_B': _L0_ffn_in['B']}

def reference(x, ctx_4096, L0_ffn_W_base, L0_ffn_gate_W, L0_ffn_A, L0_ffn_B):
    import jax
    import jax.numpy as jnp

    def _L0_attn_ref(x):
        import jax, jax.numpy as jnp
        import numpy as np
        import math
        FACTOR = 1
        B, C, L = x.shape
        xh = x[:, None]
        f = jnp.fft.rfft(xh, axis=-1)
        corr = jnp.fft.irfft(f * jnp.conj(f), n=L, axis=-1)
        top_k = int(FACTOR * math.log(L))
        weights, delay = jax.lax.top_k(corr, top_k)
        tmp_corr = jax.nn.softmax(weights, axis=-1)
        init_index = jnp.arange(L)
        idx = (init_index[None, None, None, None, :] + delay[..., None]) % L
        pattern = jnp.take_along_axis(xh[:, :, :, None, :], idx, axis=-1)
        delays_agg = jnp.sum(pattern * tmp_corr[..., None], axis=-2)
        return delays_agg[:, 0]

    def _L0_xattn_ref(key, value, query):
        import jax, jax.numpy as jnp
        import numpy as np
        N, C, S = (16, 256, 2048)
        KC = key.shape[1]
        sim = jnp.einsum('ncs,nds->ncd', key, query) * KC ** (-0.5)
        sim = jax.nn.softmax(sim, axis=1)
        context = jnp.einsum('ncd,nds->ncs', sim, value)
        return context

    def _L0_ffn_ref(x, W_base, gate_W, A, B):
        import jax, jax.numpy as jnp
        import numpy as np
        E = 8
        R = 8
        DIN = 2048
        DOUT = 2048
        TOP_K = 2
        SCALING = 2.0

        def _moe_lora(xf, gate_W, A, B):
            gate_probs = jax.nn.softmax(xf @ gate_W.T, axis=-1)
            weights, sel = jax.lax.top_k(gate_probs, TOP_K)
            weights = weights / jnp.sum(weights, axis=-1, keepdims=True)
            T = xf.shape[0]
            w_dense = jnp.zeros((T, E), xf.dtype).at[jnp.arange(T)[:, None], sel].add(weights)
            h = jnp.einsum('td,erd->ter', xf, A)
            h = h * (w_dense[:, :, None] * SCALING)
            return jnp.einsum('ter,eor->to', h, B)
        xf = x.reshape(-1, x.shape[-1])
        out = xf @ W_base.T + _moe_lora(xf, gate_W, A, B)
        return out.reshape(*x.shape[:-1], DOUT)
    x = _layernorm(x + _L0_attn_ref(x), axis=-1)
    x = _layernorm(x + _L0_xattn_ref(ctx_4096, ctx_4096, x), axis=-1)
    x = _layernorm(x + _L0_ffn_ref(x, L0_ffn_W_base, L0_ffn_gate_W, L0_ffn_A, L0_ffn_B), axis=-1)
    return x

_drawn_inputs = setup_inputs


def setup_inputs(seed=0):
    import zlib

    import numpy as np

    out = dict(_drawn_inputs(seed))
    spreads = {}
    factors = {}
    for name, (base, spread) in spreads.items():
        noise = np.random.default_rng([zlib.crc32(name.encode()), seed]).standard_normal(out[name].shape)
        drawn = base * np.exp(spread * noise) if base else spread * noise
        out[name] = jnp.asarray(drawn.astype(out[name].dtype))
    for name, factor in factors.items():
        out[name] = (out[name] * factor).astype(out[name].dtype)
    return out
```

```python
from contextlib import ExitStack

import numpy as np

import concourse.bass as bass
from concourse import mybir

F32 = mybir.dt.float32
F16 = mybir.dt.float16
BF16 = mybir.dt.bfloat16
I32 = mybir.dt.int32
U32 = mybir.dt.uint32
ALU = mybir.AluOpType
ACT = mybir.ActivationFunctionType
AX = mybir.AxisListType

P = 128
L = 2048
C = 256
R = C // P
KT = L // P
BANK = 512
NBANK = L // BANK
EPS = 1e-5
EXPERTS, RANK = 8, 8
ER = EXPERTS * RANK
AG = ER + EXPERTS
WROW = L + ER
GUARD_GAP = 110.0
PAIRS = 256
HALF = L // 2


def after(eng, sem, value):
    if isinstance(value, int) and value <= 0:
        return
    eng.wait_ge(sem, value)


class Chain:

    def __init__(self, nc, eng, sem, pad):
        self.eng, self.sem, self.base, self.count = eng, sem, 0, 0
        self.pad_memset, self.pad = nc.vector.memset, pad[:]

    def link(self, instruction):
        self.count += 1
        instruction.then_inc(self.sem, 1)
        self.eng.wait_ge(self.sem, self.base + self.count)

    def settle(self):
        self.pad_memset(self.pad, 0.0)

    def mark(self):
        done, self.count = self.count, 0
        self.base = self.base + done
        return done


def batch_slots(eng, chain, nb, slot, links):
    for n in (-2, -1, 0, 1):
        slot(n, n // 2, n % 2)
        if chain:
            chain.mark()
    if nb > 4:
        start = chain.base - 2 * links if chain else 0
        with eng.Fori(1, (nb - 2) // 2) as m:
            for parity in range(2):
                n = 2 * m + parity
                if chain:
                    chain.base, chain.count = n * links + start, 0
                slot(n, m, parity)
                if chain:
                    assert chain.count == links, (chain.count, links)
        if chain:
            chain.base, chain.count = start + (nb - 2) * links, 0
    for n in (nb - 2, nb - 1):
        slot(n, n // 2, n % 2)
        if chain:
            chain.mark()


def is_batch(n, nb):
    return not isinstance(n, int) or 0 <= n < nb


def rsqrt_steps(nc, chain, rstd, var, eps, tmp, tmp2):
    v = nc.vector
    chain.link(v.tensor_scalar(tmp, var, eps, None, ALU.add))
    chain.link(v.tensor_scalar(tmp2.bitcast(I32), tmp.bitcast(I32), 1, None, ALU.arith_shift_right))
    chain.link(v.tensor_scalar(rstd.bitcast(I32), tmp2.bitcast(I32), -1.0, float(0x5F3759DF), ALU.mult, ALU.add))
    for _ in range(3):
        chain.link(v.tensor_tensor(tmp2, rstd, tmp, ALU.mult))
        chain.link(v.scalar_tensor_tensor(tmp2, tmp2, -0.5, rstd, ALU.mult, ALU.mult))
        chain.link(v.scalar_tensor_tensor(rstd, tmp2, 1.5, rstd, ALU.add, ALU.mult))


def scale_steps(nc, chain, scale, inverse, total, tmp):
    v = nc.vector
    chain.link(v.tensor_scalar(tmp.bitcast(U32), total.bitcast(U32), 24, None, ALU.logical_shift_right))
    v.tensor_scalar(scale.bitcast(I32), tmp.bitcast(I32), -float(1 << 23), float(204 << 23), ALU.mult, ALU.add)
    chain.link(v.tensor_scalar(inverse.bitcast(I32), tmp.bitcast(I32), float(1 << 23), float(50 << 23), ALU.mult, ALU.add))


def attention_pass(nc, src, ctx_in, x2_out, consts, eps1, tag, x_scale=1.0):
    nb = src.shape[0] // C
    with ExitStack() as st:
        def sb(name, shape, dt):
            return st.enter_context(nc.sbuf_tensor(f"{name}_{tag}", shape, dt))

        def sem(name):
            return st.enter_context(nc.semaphore(f"{name}_{tag}"))

        xbuf = [sb(f"xbuf{i}", [P, R, L], F32) for i in range(2)]
        cbuf = [sb(f"cbuf{i}", [P, R, L], F32) for i in range(2)]
        x2buf = sb("x2buf", [P, R, L], F32)
        v_hi, v_lo = sb("v_hi", [P, R, L], F16), sb("v_lo", [P, R, L], F16)
        q_hi, q_lo = sb("q_hi", [P, KT, C], F16), sb("q_lo", [P, KT, C], F16)
        k_hi, k_lo = sb("k_hi", [P, KT, C], F16), sb("k_lo", [P, KT, C], F16)
        p_hi, p_lo = sb("p_hi", [P, R, C], F16), sb("p_lo", [P, R, C], F16)
        expd = sb("expd", [P, R, C], F32)
        u_rows = sb("u_rows", [P, R, HALF], BF16)
        u_t = sb("u_t", [P, HALF // P, C], BF16)
        power = sb("power", [P, 4, C], BF16)
        fwd = sb("fwd", [P, HALF // P, 2 * PAIRS], BF16)
        inv = sb("inv", [P, 4, BANK], BF16)
        junk = sb("junk", [P, L], BF16)
        stats = sb("stats", [P, R, NBANK, 6], F32)
        stats2 = sb("stats2", [P, R, NBANK, 6], F32)
        mv1 = [sb(f"mv1_{i}", [P, R, 2], F32) for i in range(2)]
        mv2 = sb("mv2", [P, R, 2], F32)
        rs1, nb1 = sb("rs1", [P, R], F32), sb("nb1", [P, R], F32)
        rs2, nb2 = sb("rs2", [P, R], F32), sb("nb2", [P, R], F32)
        tmp, tmp2 = sb("tmp", [P, R], F32), sb("tmp2", [P, R], F32)
        sumsq = [sb(f"sumsq{i}", [P, R], F32) for i in range(2)]
        sumall = [sb(f"sumall{i}", [P, R], F32) for i in range(2)]
        scale = [sb(f"scale{i}", [P, 1], F32) for i in range(2)]
        iscale = [sb(f"iscale{i}", [P, 1], F32) for i in range(2)]
        lscale = [sb(f"lscale{i}", [P, 1], F32) for i in range(2)]
        nlscale = [sb(f"nlscale{i}", [P, 1], F32) for i in range(2)]
        rowmax, nmax = sb("rowmax", [P, R], F32), sb("nmax", [P, R], F32)
        psum_e, rinv = sb("psum_e", [P, R], F32), sb("rinv", [P, R], F32)
        gmax, gval = sb("gmax", [P, R], F32), sb("gval", [P, R], F32)
        energy = sb("energy", [P, R], F32)
        ident = consts["ident"]
        ident16 = consts["ident_bf16"]
        worst = consts["worst"]

        ps_t = [st.enter_context(nc.psum_tensor(f"ps_t{i}_{tag}", [P, BANK], F32)) for i in range(3)]
        ps_c = [st.enter_context(nc.psum_tensor(f"ps_c{i}_{tag}", [P, BANK], F32)) for i in range(2)]
        ps_s = [st.enter_context(nc.psum_tensor(f"ps_s{i}_{tag}", [P, BANK], F32)) for i in range(R)]
        ps_g = [st.enter_context(nc.psum_tensor(f"ps_g_{tag}", [P, BANK], F32)), ps_t[2]]

        x_loaded = [[sem(f"x_loaded{i}{r}") for r in range(R)] for i in range(2)]
        c_loaded = [[sem(f"c_loaded{i}{r}") for r in range(R)] for i in range(2)]
        stored = [sem(f"stored{r}") for r in range(R)]
        tables_loaded = sem("tables_loaded")
        folded, x1_ready, ln1_ready = sem("folded"), sem("x1_ready"), sem("ln1_ready")
        sumsq_done, sumall_done, scale_ready = sem("sumsq_done"), sem("sumall_done"), sem("scale_ready")
        t_filled, hi_done, t_free = sem("t_filled"), sem("hi_done"), sem("t_free")
        sim_done, nmax_ready, exp_done, p_ready = sem("sim_done"), sem("nmax_ready"), sem("exp_done"), sem("p_ready")
        vhi_done, vlo_done = sem("vhi_done"), sem("vlo_done")
        fwd_done, sq_done, inv_done, g_free = sem("fwd_done"), sem("sq_done"), sem("inv_done"), sem("g_free")
        context_done, ctx_added = sem("context_done"), sem("ctx_added")
        ln2_ready, x2_ready = sem("ln2_ready"), sem("x2_ready")
        dve_step = sem("dve_step")

        TB = 18
        CG = R * NBANK

        with nc.Block() as block:
            @block.sync
            def _(sp):
                sp.dma_start(fwd[:], consts["fwd_dram"]).then_inc(tables_loaded, 16)
                sp.dma_start(inv[:], consts["inv_dram"]).then_inc(tables_loaded, 16)

                def slot(n, half, parity):
                    if is_batch(n + 2, nb):
                        after(sp, ctx_added, CG * (n + 1))
                        for r in range(R):
                            sp.dma_start(xbuf[parity][:, r], src[bass.ds((n + 2) * C + r * P, P), :]).then_inc(x_loaded[parity][r], 16)
                        after(sp, vlo_done, R * (n + 1))
                        for r in range(R):
                            sp.dma_start(cbuf[parity][:, r], ctx_in[bass.ds((n + 2) * C + r * P, P), :]).then_inc(c_loaded[parity][r], 16)
                    if is_batch(n, nb):
                        for r in range(R):
                            sp.wait_ge(x2_ready, R * n + r + 1)
                            sp.dma_start(x2_out[bass.ds(n * C + r * P, P), :], x2buf[:, r]).then_inc(stored[r], 16)

                batch_slots(sp, None, nb, slot, 0)
                for r in range(R):
                    sp.wait_ge(stored[r], 16 * nb)

            @block.gpsimd
            def _(pool):
                def slot(n, half, parity):
                    b = n + 2
                    if is_batch(b, nb):
                        for r in range(R):
                            pool.wait_ge(x_loaded[parity][r], 16 * (half + 2))
                            if r == 0:
                                after(pool, t_filled, TB * b)
                            else:
                                pool.wait_ge(sumsq_done, R * (b + 1))
                            nc.gpsimd.tensor_tensor(u_rows[:, r], xbuf[parity][:, r, 0:HALF], xbuf[parity][:, r, HALF:L],
                                                    ALU.subtract).then_inc(folded, 1)
                        nc.gpsimd.partition_all_reduce(sumall[parity][:], sumsq[parity][:], P,
                                                       bass.bass_isa.ReduceOp.add).then_inc(sumall_done, 1)

                batch_slots(pool, None, nb, slot, 0)

            @block.scalar
            def _(act):
                def slot(n, half, parity):
                    cur, nxt, n2 = is_batch(n, nb), is_batch(n + 1, nb), is_batch(n + 2, nb)
                    other = 1 - parity
                    if nxt:
                        for q in range(2 * CG):
                            after(act, t_filled, TB * (n + 1) + q + 1)
                            r, kk = (q // 4) % 2, 4 * (q % 4)
                            bank = ps_t[q % 3][:].rearrange("p (k c) -> p k c", k=4)
                            if q < CG:
                                nc.scalar.activation(q_hi[:, kk:kk + 4, r * P:(r + 1) * P], bank, ACT.Copy).then_inc(hi_done, 1)
                            else:
                                if q == CG:
                                    act.wait_ge(scale_ready, n + 2)
                                nc.scalar.activation(k_hi[:, kk:kk + 4, r * P:(r + 1) * P], bank, ACT.Copy,
                                                     scale=scale[other][:]).then_inc(hi_done, 1)
                        after(act, context_done, CG * (n + 1))
                        for r in range(R):
                            nc.scalar.activation(v_hi[:, r], cbuf[other][:, r], ACT.Copy, scale=scale[other][:]).then_inc(vhi_done, 1)

                    def apply2(r):
                        if cur:
                            act.wait_ge(ln2_ready, n + 1)
                            nc.scalar.activation(x2buf[:, r], x2buf[:, r], ACT.Identity, bias=nb2[:, r:r + 1],
                                                 scale=rs2[:, r:r + 1]).then_inc(x2_ready, 1)

                    def softmax_exp(r):
                        if nxt:
                            after(act, p_ready, R * n + r + 1)
                            act.wait_ge(nmax_ready, R * (n + 1) + r + 1)
                            nc.scalar.activation(expd[:, r], ps_s[r][:, 0:C], ACT.Exp, bias=nmax[:, r:r + 1],
                                                 scale=lscale[other][:], accum_out=psum_e[:, r:r + 1]).then_inc(exp_done, 1)

                    apply2(0)
                    softmax_exp(0)
                    apply2(1)
                    softmax_exp(1)
                    if nxt:
                        after(act, inv_done, R * (n + 1))
                        for m in range(4):
                            act.wait_ge(fwd_done, 4 * (n + 1) + m + 1)
                            nc.scalar.activation(power[:, m], ps_t[m % 2][:, 0:C], ACT.Square).then_inc(sq_done, 1)
                    if n2:
                        for r in range(R):
                            act.wait_ge(c_loaded[parity][r], 16 * (half + 2))
                            after(act, sumsq_done, R * (n + 2) + r)
                            nc.scalar.activation(junk[:], cbuf[parity][:, r], ACT.Square,
                                                 accum_out=sumsq[parity][:, r:r + 1]).then_inc(sumsq_done, 1)
                        act.wait_ge(ln1_ready, n + 3)
                        for r in range(R):
                            act.wait_ge(folded, R * (n + 2) + r + 1)
                            nc.scalar.activation(xbuf[parity][:, r], xbuf[parity][:, r], ACT.Identity, bias=nb1[:, r:r + 1],
                                                 scale=rs1[:, r:r + 1]).then_inc(x1_ready, 1)

                batch_slots(act, None, nb, slot, 0)

            @block.vector
            def _(dve):
                v = nc.vector
                chain = Chain(nc, dve, dve_step, consts["pad"])

                def slot(n, half, parity):
                    cur, nxt, n2 = is_batch(n, nb), is_batch(n + 1, nb), is_batch(n + 2, nb)
                    other = 1 - parity

                    def x2_stats(j):
                        dve.wait_ge(ctx_added, CG * n + j + 1)
                        r, b = j // NBANK, j % NBANK
                        return v.bn_stats(stats2[:, r, b], x2buf[:, r, b * BANK:(b + 1) * BANK])

                    for j in range(CG):
                        if cur:
                            r, b = j // NBANK, j % NBANK
                            if b == 0:
                                after(dve, stored[r], 16 * n)
                            dve.wait_ge(context_done, CG * n + j + 1)
                            v.scalar_tensor_tensor(x2buf[:, r, b * BANK:(b + 1) * BANK], ps_c[j % 2][:], iscale[parity][:],
                                                   xbuf[parity][:, r, b * BANK:(b + 1) * BANK], ALU.mult,
                                                   ALU.add).then_inc(ctx_added, 1)
                            if j:
                                x2_stats(j - 1)
                        if nxt:
                            for q in (2 * j, 2 * j + 1):
                                r, kk = (q // 4) % 2, 4 * (q % 4)
                                at = (slice(None), slice(kk, kk + 4), slice(r * P, (r + 1) * P))
                                bank = ps_t[q % 3][:].rearrange("p (k c) -> p k c", k=4)
                                after(dve, hi_done, 2 * CG * (n + 1) + q + 1)
                                if q < CG:
                                    v.tensor_tensor(q_lo[at], bank, q_hi[at], ALU.subtract).then_inc(t_free, 1)
                                else:
                                    v.scalar_tensor_tensor(k_lo[at], bank, scale[other][:], k_hi[at], ALU.mult,
                                                           ALU.subtract).then_inc(t_free, 1)
                    if cur:
                        chain.link(x2_stats(CG - 1))
                    if nxt:
                        for r in range(R):
                            dve.wait_ge(t_filled, TB * (n + 1) + 16 + r + 1)
                            bank = ps_t[(16 + r) % 3][:].bitcast(BF16).rearrange("p (k c) -> p k c", c=P)
                            v.tensor_copy(u_t[:, :, r * P:(r + 1) * P], bank).then_inc(t_free, 1)
                    if cur:
                        chain.settle()
                        chain.link(v.bn_aggr(mv2[:, 0], stats2[:, 0].rearrange("p a b -> p (a b)")))
                        chain.settle()
                        chain.link(v.bn_aggr(mv2[:, 1], stats2[:, 1].rearrange("p a b -> p (a b)")))
                        rsqrt_steps(nc, chain, rs2[:], mv2[:, :, 1], EPS, tmp[:], tmp2[:])
                        v.scalar_tensor_tensor(nb2[:], mv2[:, :, 0], -1.0, rs2[:], ALU.mult, ALU.mult).then_inc(ln2_ready, 1)

                    def value_low(r):
                        if nxt:
                            dve.wait_ge(vhi_done, R * (n + 1) + r + 1)
                            v.scalar_tensor_tensor(v_lo[:, r], cbuf[other][:, r], scale[other][:], v_hi[:, r], ALU.mult,
                                                   ALU.subtract).then_inc(vlo_done, 1)

                    def softmax_max(r):
                        if nxt:
                            dve.wait_ge(sim_done, R * (n + 1) + r + 1)
                            dve.wait_ge(scale_ready, n + 2)
                            chain.link(v.tensor_reduce(rowmax[:, r:r + 1], ps_s[r][:, 0:C], AX.X, ALU.max))
                            v.tensor_tensor(nmax[:, r:r + 1], rowmax[:, r:r + 1], nlscale[other][:],
                                            ALU.mult).then_inc(nmax_ready, 1)

                    def softmax_norm(r):
                        if nxt:
                            dve.wait_ge(exp_done, R * (n + 1) + r + 1)
                            chain.link(v.reciprocal(rinv[:, r:r + 1], psum_e[:, r:r + 1]))
                            chain.link(v.tensor_scalar(p_hi[:, r], expd[:, r], rinv[:, r:r + 1], None, ALU.mult))
                            v.scalar_tensor_tensor(p_lo[:, r], expd[:, r], rinv[:, r:r + 1], p_hi[:, r], ALU.mult,
                                                   ALU.subtract).then_inc(p_ready, 1)

                    def x_stats(r):
                        if n2:
                            dve.wait_ge(x_loaded[parity][r], 16 * (half + 2))
                            for b in range(NBANK):
                                ins = v.bn_stats(stats[:, r, b], xbuf[parity][:, r, b * BANK:(b + 1) * BANK])
                            chain.link(ins)
                            chain.settle()
                            chain.link(v.bn_aggr(mv1[parity][:, r], stats[:, r].rearrange("p a b -> p (a b)")))

                    value_low(0)
                    softmax_max(0)
                    value_low(1)
                    x_stats(0)
                    softmax_norm(0)
                    softmax_max(1)
                    x_stats(1)
                    softmax_norm(1)
                    if n2:
                        after(dve, x1_ready, R * (n + 2))
                        rsqrt_steps(nc, chain, rs1[:], mv1[parity][:, :, 1], eps1, tmp[:], tmp2[:])
                        v.scalar_tensor_tensor(nb1[:], mv1[parity][:, :, 0], -1.0, rs1[:], ALU.mult, ALU.mult).then_inc(ln1_ready, 1)
                        dve.wait_ge(sumall_done, n + 3)
                        chain.link(v.tensor_tensor(tmp[:, 0:1], sumall[parity][:, 0:1], sumall[parity][:, 1:2], ALU.add))
                        scale_steps(nc, chain, scale[parity][:], iscale[parity][:], tmp[:, 0:1], tmp2[:, 0:1])
                        v.tensor_scalar(lscale[parity][:], iscale[parity][:], C ** -0.5, None, ALU.mult)
                        v.tensor_scalar(nlscale[parity][:], iscale[parity][:], -(C ** -0.5), None, ALU.mult).then_inc(scale_ready, 1)
                    if nxt:
                        for r in range(R):
                            dve.wait_ge(inv_done, R * (n + 1) + r + 1)
                            chain.link(v.tensor_reduce(gmax[:, r:r + 1], ps_g[r][:, 1:BANK], AX.X, ALU.max, apply_absolute_value=True))
                            v.tensor_tensor(gval[:, r:r + 1], gmax[:, r:r + 1], ps_g[r][:, 0:1], ALU.subtract).then_inc(g_free, 1)
                        dve.wait_ge(g_free, R * (n + 2))
                        chain.link(v.tensor_tensor(energy[:], mv1[other][:, :, 0], mv1[other][:, :, 0], ALU.mult))
                        chain.link(v.tensor_tensor(energy[:], energy[:], mv1[other][:, :, 1], ALU.add))
                        chain.link(v.scalar_tensor_tensor(gval[:], energy[:], L / 32.0, gval[:], ALU.mult, ALU.add))
                        chain.link(v.tensor_tensor(worst[:], worst[:], gval[:], ALU.max))

                batch_slots(dve, chain, nb, slot, 46)

            @block.tensor
            def _(pe):
                pe.wait_ge(tables_loaded, 32)

                def slot(n, half, parity):
                    cur, nxt = is_batch(n, nb), is_batch(n + 1, nb)
                    other = 1 - parity

                    def transposed_bank(q):
                        g = TB * (n + 1) + q
                        after(pe, t_free, g - 2)
                        if q == 2:
                            after(pe, g_free, R * (n + 1))
                        r, kk = (q // 4) % 2, 4 * (q % 4)
                        bank = ps_t[q % 3]
                        if q < CG and q % 4 == 0:
                            pe.wait_ge(x1_ready, R * (n + 1) + r + 1)
                        if CG <= q < 2 * CG and q % 4 == 0:
                            pe.wait_ge(c_loaded[other][r], 16 * (half + parity + 1))
                        if q < 2 * CG:
                            rows = xbuf[other] if q < CG else cbuf[other]
                            for i in range(4):
                                ins = nc.tensor.transpose(bank[:, i * P:(i + 1) * P], rows[:, r, (kk + i) * P:(kk + i + 1) * P], ident[:])
                        else:
                            r = q - 2 * CG
                            pe.wait_ge(folded, R * (n + 1) + r + 1)
                            out = bank[:].bitcast(BF16)
                            for i in range(HALF // P):
                                ins = nc.tensor.transpose(out[:, i * P:(i + 1) * P], u_rows[:, r, i * P:(i + 1) * P], ident16[:])
                        ins.then_inc(t_filled, 1)

                    for j in range(CG):
                        if cur:
                            if j == 0:
                                pe.wait_ge(p_ready, R * (n + 1))
                                pe.wait_ge(vlo_done, R * (n + 1))
                            after(pe, ctx_added, CG * n + j - 1)
                            r, b = j // NBANK, j % NBANK
                            terms = [(p_hi, v_hi), (p_hi, v_lo), (p_lo, v_hi)]
                            for i in range(3 * R):
                                pp, vv = terms[i % 3]
                                d = i // 3
                                ins = nc.tensor.matmul(ps_c[j % 2][:], pp[:, d, r * P:(r + 1) * P], vv[:, d, b * BANK:(b + 1) * BANK],
                                                       start=(i == 0), stop=(i == 3 * R - 1))
                            ins.then_inc(context_done, 1)
                        if nxt:
                            transposed_bank(2 * j)
                            transposed_bank(2 * j + 1)
                    if nxt:
                        transposed_bank(16)
                        transposed_bank(17)
                        after(pe, exp_done, R * (n + 1))
                        pe.wait_ge(t_free, TB * (n + 2))
                        for r in range(R):
                            terms = [(q_hi, k_hi), (q_hi, k_lo), (q_lo, k_hi)]
                            for i in range(3 * KT):
                                qq, kk = terms[i % 3]
                                k = i // 3
                                ins = nc.tensor.matmul(ps_s[r][:, 0:C], qq[:, k, r * P:(r + 1) * P], kk[:, k, :],
                                                       start=(i == 0), stop=(i == 3 * KT - 1))
                            ins.then_inc(sim_done, 1)
                        for m in range(4):
                            if m >= 2:
                                pe.wait_ge(sq_done, 4 * (n + 1) + m - 1)
                            for k in range(HALF // P):
                                ins = nc.tensor.matmul(ps_t[m % 2][:, 0:C], fwd[:, k, m * P:(m + 1) * P], u_t[:, k, :],
                                                       start=(k == 0), stop=(k == HALF // P - 1))
                            ins.then_inc(fwd_done, 1)
                        pe.wait_ge(sq_done, 4 * (n + 2))
                        for r in range(R):
                            for m in range(4):
                                ins = nc.tensor.matmul(ps_g[r][:], power[:, m, r * P:(r + 1) * P], inv[:, m, :],
                                                       start=(m == 0), stop=(m == 3))
                            ins.then_inc(inv_done, 1)

                batch_slots(pe, None, nb, slot, 0)


def guard_tables():
    order = (np.arange(L // 4) * 197 + 61) % (L // 4)
    freq = np.sort(2 * order[:PAIRS] + 1).astype(np.int64)
    pos = np.arange(HALF, dtype=np.int64)
    angle = 2 * np.pi * ((pos[:, None] * freq[None, :]) % L) / L
    fwd = np.concatenate([np.cos(angle), np.sin(angle)], 1) / np.sqrt(L / 2)
    lag = np.arange(BANK, dtype=np.int64)
    both = np.concatenate([freq, freq])
    inv = np.cos(2 * np.pi * ((both[:, None] * lag[None, :]) % L) / L)
    return (fwd.reshape(HALF // P, P, 2 * PAIRS).transpose(1, 0, 2).copy(), inv.reshape(4, P, BANK).transpose(1, 0, 2).copy())


def prepare_weights(nc, W, A, gate, B, consts, w_scratch, iscale_scratch):
    NO = W.shape[0] // P
    with ExitStack() as st:
        def sb(name, shape, dt):
            return st.enter_context(nc.sbuf_tensor(f"{name}_w", shape, dt))

        def sem(name):
            return st.enter_context(nc.semaphore(f"{name}_w"))

        rows = [sb(f"rows{i}", [P, WROW], F32) for i in range(2)]
        halves = [sb(f"halves{i}", [P, 2, KT, P], F16) for i in range(2)]
        b_rows = [sb(f"b_rows{i}", [P, 4, ER], F16) for i in range(2)]
        junk = sb("junk", [P, WROW], BF16)
        total = [sb(f"total{i}", [P, 1], F32) for i in range(2)]
        scale = [sb(f"scale{i}", [P, 1], F32) for i in range(2)]
        inverse = [sb(f"inverse{i}", [P, 1], F32) for i in range(2)]
        tmp = sb("tmp", [P, 1], F32)
        ident, ident16 = consts["ident"], consts["ident_f16"]
        b_stack, ag_t = consts["b_stack"], consts["ag_t"]
        ps_t = [st.enter_context(nc.psum_tensor(f"ps_t{i}_w", [P, BANK], F32)) for i in range(4)]
        ps_b = [st.enter_context(nc.psum_tensor(f"ps_b{i}_w", [P, 2, BANK], F16)) for i in range(2)]

        loaded = [sem(f"loaded{i}") for i in range(2)]
        stored = [sem(f"stored{i}") for i in range(2)]
        istored = [sem(f"istored{i}") for i in range(2)]
        squared, scale_ready, scaled = sem("squared"), sem("scale_ready"), sem("scaled")
        t_filled, hi_done, t_free = sem("t_filled"), sem("hi_done"), sem("t_free")
        bhi_done, b_split, b_filled, b_free = sem("bhi_done"), sem("b_split"), sem("b_filled"), sem("b_free")
        dve_step = sem("dve_step")

        def tiles(slot, chain, links):
            for n in (-1, 0, 1):
                slot(n, n // 2, n % 2)
            with (chain.eng if chain else slot.eng).Fori(1, (NO - 2) // 2) as m:
                for parity in range(2):
                    n = 2 * m + parity
                    if chain:
                        chain.base, chain.count = n * links + links, 0
                    slot(n, m, parity)
                    if chain:
                        assert chain.count == links, (chain.count, links)
            if chain:
                chain.base, chain.count = (NO - 1) * links, 0
            for n in (NO - 2, NO - 1, NO):
                slot(n, n // 2, n % 2)

        def is_last(n):
            return isinstance(n, int) and n == NO

        def is_tile(n):
            return not isinstance(n, int) or 0 <= n <= NO

        with nc.Block() as block:
            @block.sync
            def _(sp):
                def load(n, half, parity):
                    if is_last(n):
                        after(sp, t_filled, 4 * (n - 1))
                        after(sp, b_filled, n - 1)
                        sp.dma_start(rows[parity][0:ER, 0:L], A).then_inc(loaded[parity], 16)
                        sp.dma_start(rows[parity][ER:AG, 0:L], gate).then_inc(loaded[parity], 16)
                    elif is_tile(n):
                        after(sp, t_filled, 4 * (n - 1))
                        after(sp, b_filled, n - 1)
                        sp.dma_start(rows[parity][:, 0:L], W[bass.ds(n * P, P), :]).then_inc(loaded[parity], 16)
                        sp.dma_start(rows[parity][:, L:WROW], B[bass.ds(n * P, P), :]).then_inc(loaded[parity], 16)

                def slot(n, half, parity):
                    if isinstance(n, int) and n == -1:
                        load(0, 0, 0)
                    load(n + 2, half + 1, parity)
                    if is_tile(n):
                        rows_used = AG if is_last(n) else P
                        sp.wait_ge(scale_ready, n + 1)
                        sp.dma_start(iscale_scratch[bass.ds(n * P, rows_used), :], inverse[parity][0:rows_used, :]).then_inc(istored[parity], 16)
                        if not is_last(n):
                            sp.wait_ge(hi_done, 4 * (n + 1))
                            sp.wait_ge(t_free, 4 * (n + 1))
                            sp.dma_start(w_scratch[n], halves[parity][:].rearrange("p h k c -> p (h k c)")).then_inc(stored[parity], 16)

                slot.eng = sp
                tiles(slot, None, 0)
                sp.wait_ge(istored[0], 16 * (NO // 2 + 1))
                sp.wait_ge(istored[1], 16 * (NO // 2))
                for i in range(2):
                    sp.wait_ge(stored[i], 16 * (NO // 2))

            @block.gpsimd
            def _(pool):
                def slot(n, half, parity):
                    if is_tile(n + 1):
                        used = slice(0, AG) if is_last(n + 1) else slice(0, P)
                        cols = slice(0, L) if is_last(n + 1) else slice(0, WROW)
                        other = 1 - parity
                        pool.wait_ge(scale_ready, n + 2)
                        target = rows[other][used, cols]
                        nc.gpsimd.tensor_tensor(target, target, scale[other][used, :].to_broadcast(list(target.shape)),
                                                ALU.mult).then_inc(scaled, 1)

                slot.eng = pool
                tiles(slot, None, 0)

            @block.scalar
            def _(act):
                def slot(n, half, parity):
                    other = 1 - parity
                    if is_tile(n + 1):
                        used = slice(0, AG) if is_last(n + 1) else slice(0, P)
                        cols = slice(0, L) if is_last(n + 1) else slice(0, WROW)
                        act.wait_ge(loaded[other], 32 * (half + parity + 1))
                        after(act, squared, n + 1)
                        after(act, scale_ready, n)
                        nc.scalar.activation(junk[used, cols], rows[other][used, cols], ACT.Square,
                                             accum_out=total[other][used, :]).then_inc(squared, 1)
                    if is_tile(n) and not is_last(n):
                        act.wait_ge(scaled, n + 1)
                        after(act, b_filled, n - 1)
                        for i in range(3):
                            nc.scalar.activation(b_rows[parity][:, i], rows[parity][:, L:WROW], ACT.Copy).then_inc(bhi_done, 1)
                        after(act, stored[parity], 16 * half)
                        for q in range(4):
                            act.wait_ge(t_filled, 4 * n + q + 1)
                            nc.scalar.activation(halves[parity][:, 0, 4 * q:4 * q + 4, :],
                                                 ps_t[q][:].rearrange("p (k c) -> p k c", k=4), ACT.Copy).then_inc(hi_done, 1)
                    if is_last(n):
                        for q in range(4):
                            act.wait_ge(t_filled, 4 * n + q + 1)
                            nc.scalar.activation(ag_t[:, 4 * q:4 * q + 4, 0:AG],
                                                 ps_t[q][:].rearrange("p (k c) -> p k c", k=4)[:, :, 0:AG], ACT.Copy).then_inc(hi_done, 1)

                slot.eng = act
                tiles(slot, None, 0)

            @block.vector
            def _(dve):
                v = nc.vector
                chain = Chain(nc, dve, dve_step, consts["pad"])

                def slot(n, half, parity):
                    other = 1 - parity
                    if is_tile(n + 1):
                        used = slice(0, AG) if is_last(n + 1) else slice(0, P)
                        dve.wait_ge(squared, n + 2)
                        after(dve, scaled, n)
                        after(dve, istored[other], 16 * (half + parity))
                        scale_steps(nc, chain, scale[other][used, :], inverse[other][used, :], total[other][used, :], tmp[used, :])
                        v.tensor_copy(tmp[used, :], inverse[other][used, :]).then_inc(scale_ready, 1)
                        dve.wait_ge(scale_ready, n + 2)
                    if is_tile(n) and not is_last(n):
                        dve.wait_ge(bhi_done, 3 * (n + 1))
                        v.tensor_tensor(b_rows[parity][:, 3], rows[parity][:, L:WROW], b_rows[parity][:, 0],
                                        ALU.subtract).then_inc(b_split, 1)
                        dve.wait_ge(hi_done, 4 * n + 1)
                        after(dve, stored[parity], 16 * half)
                        for q in range(4):
                            dve.wait_ge(hi_done, 4 * n + q + 1)
                            v.tensor_tensor(halves[parity][:, 1, 4 * q:4 * q + 4, :], ps_t[q][:].rearrange("p (k c) -> p k c", k=4),
                                            halves[parity][:, 0, 4 * q:4 * q + 4, :], ALU.subtract).then_inc(t_free, 1)
                        dve.wait_ge(b_filled, n + 1)
                        v.tensor_copy(b_stack[:, :, bass.ds(n * P, P)], ps_b[parity][:, :, 0:P]).then_inc(b_free, 1)
                    if is_last(n):
                        for q in range(4):
                            dve.wait_ge(hi_done, 4 * n + q + 1)
                            v.tensor_tensor(ag_t[:, 4 * q:4 * q + 4, AG:2 * AG],
                                            ps_t[q][:].rearrange("p (k c) -> p k c", k=4)[:, :, 0:AG],
                                            ag_t[:, 4 * q:4 * q + 4, 0:AG], ALU.subtract).then_inc(t_free, 1)

                tiles(slot, chain, 2)

            @block.tensor
            def _(pe):
                def slot(n, half, parity):
                    if is_tile(n):
                        used = AG if is_last(n) else P
                        pe.wait_ge(scaled, n + 1)
                        for q in range(4):
                            after(pe, t_free, 4 * (n - 1) + q + 1)
                            for i in range(4):
                                k = 4 * q + i
                                ins = nc.tensor.transpose(ps_t[q][:, i * P:i * P + used], rows[parity][0:used, k * P:(k + 1) * P],
                                                          ident[0:used, 0:used])
                            ins.then_inc(t_filled, 1)
                        if not is_last(n):
                            pe.wait_ge(b_split, n + 1)
                            after(pe, b_free, n - 1)
                            for i in range(2):
                                ins = nc.tensor.transpose(ps_b[parity][:, i, 0:P],
                                                          b_rows[parity][:, 2 * i:2 * i + 2].rearrange("p a b -> p (a b)"), ident16[:])
                            ins.then_inc(b_filled, 1)

                slot.eng = pe
                tiles(slot, None, 0)


def feed_forward(nc, x2, out, consts, w_scratch, iscale_scratch):
    NT = x2.shape[0] // P
    with ExitStack() as st:
        def sb(name, shape, dt):
            return st.enter_context(nc.sbuf_tensor(f"{name}_f", shape, dt))

        def sem(name):
            return st.enter_context(nc.semaphore(f"{name}_f"))

        NO = L // P
        w = sb("w", [P, NO, 2, KT, P], F16)
        irow = sb("irow", [P, L + AG], F32)
        xn = [sb(f"xn{i}", [P, L], F32) for i in range(2)]
        x_hi = [sb(f"x_hi{i}", [P, KT, P], F16) for i in range(2)]
        x_lo = [sb(f"x_lo{i}", [P, KT, P], F16) for i in range(2)]
        y = [sb(f"y{i}", [P, L], F32) for i in range(2)]
        stats, mv = sb("stats", [P, NBANK, 6], F32), sb("mv", [P, 2], F32)
        rs, nb_ = sb("rs", [P, 1], F32), sb("nb", [P, 1], F32)
        tmp, tmp2 = sb("tmp", [P, 1], F32), sb("tmp2", [P, 1], F32)
        ag, ag2 = sb("ag", [P, AG], F32), sb("ag2", [P, AG], F32)
        nmax = sb("nmax", [P, 1], F32)
        probs = sb("probs", [P, EXPERTS], F32)
        top, top_i = sb("top", [P, 8], F32), sb("top_i", [P, 8], U32)
        top_f = sb("top_f", [P, 2], F32)
        pair, wtop = sb("pair", [P, 1], F32), sb("wtop", [P, 2], F32)
        dense, dense2 = sb("dense", [P, EXPERTS], F32), sb("dense2", [P, EXPERTS], F32)
        h, h_rest = sb("h", [P, ER], F32), sb("h_rest", [P, ER], F32)
        h_parts = sb("h_parts", [P, 4, ER], BF16)
        h_t = sb("h_t", [P, 2, P], BF16)
        ident, ident16 = consts["ident"], consts["ident_bf16"]
        expert_ids, b_stack, ag_t = consts["expert_ids"], consts["b_stack"], consts["ag_t"]

        def pb(name, shape, dt):
            return st.enter_context(nc.psum_tensor(f"{name}_f", shape, dt))

        ps_y = [pb(f"ps_y{j}", [P, BANK], F32) for j in range(NBANK)]
        ps_a, ps_h = pb("ps_a", [P, BANK], F32), pb("ps_h", [P, 2, BANK], BF16)
        ps_t = [pb(f"ps_t{i}", [P, BANK], F32) for i in range(2)]

        w_loaded = [sem(f"w_loaded{j}") for j in range(NBANK)]
        irow_loaded = sem("irow_loaded")
        x_loaded = [sem(f"x_loaded{i}") for i in range(2)]
        stored = [sem(f"stored{i}") for i in range(2)]
        t_filled, hi_done, t_free = sem("t_filled"), sem("hi_done"), sem("t_free")
        a_done, a_read, nmax_ready, exp_done, h_ready = sem("a_done"), sem("a_read"), sem("nmax_ready"), sem("exp_done"), sem("h_ready")
        ht_done, ht_copied = sem("ht_done"), sem("ht_copied")
        bank_done, evacuated, res_added = sem("bank_done"), sem("evacuated"), sem("res_added")
        ln_ready, out_ready, dve_step = sem("ln_ready"), sem("out_ready"), sem("dve_step")

        def tiles(eng, slot, chain, links):
            for t in (-1, 0, 1):
                slot(t, t // 2, t % 2)
            with eng.Fori(1, (NT - 2) // 2) as m:
                for parity in range(2):
                    t = 2 * m + parity
                    if chain:
                        chain.base, chain.count = t * links, 0
                    slot(t, m, parity)
                    if chain:
                        assert chain.count == links, (chain.count, links)
            if chain:
                chain.base, chain.count = (NT - 2) * links, 0
            for t in (NT - 2, NT - 1):
                slot(t, t // 2, t % 2)

        with nc.Block() as block:
            @block.sync
            def _(sp):
                def load(t, half, parity):
                    if is_batch(t, NT):
                        after(sp, res_added, NBANK * (t - 1))
                        sp.dma_start(xn[parity][:], x2[bass.ds(t * P, P), :]).then_inc(x_loaded[parity], 16)

                def slot(t, half, parity):
                    if isinstance(t, int) and t == -1:
                        load(0, 0, 0)
                        sp.dma_start(w[:, 0:4].rearrange("p n h k c -> p n (h k c)"), w_scratch[0:4].rearrange("n p c -> p n c")).then_inc(w_loaded[0], 16)
                        sp.dma_start(irow[:], iscale_scratch[0:L + AG, :].rearrange("c o -> (o c)").partition_broadcast(P)).then_inc(irow_loaded, 16)
                        for j in range(1, NBANK):
                            sp.dma_start(w[:, 4 * j:4 * j + 4].rearrange("p n h k c -> p n (h k c)"),
                                         w_scratch[4 * j:4 * j + 4].rearrange("n p c -> p n c")).then_inc(w_loaded[j], 16)
                    if is_batch(t, NT):
                        load(t + 2, half + 1, parity)
                        sp.wait_ge(out_ready, t + 1)
                        sp.dma_start(out[bass.ds(t * P, P), :], y[parity][:]).then_inc(stored[parity], 16)
                    else:
                        load(1, 0, 1)

                tiles(sp, slot, None, 0)
                for i in range(2):
                    sp.wait_ge(stored[i], 16 * (NT // 2))

            @block.gpsimd
            def _(pool):
                def slot(t, half, parity):
                    if is_batch(t, NT):
                        pool.wait_ge(x_loaded[parity], 16 * (half + 1))
                        for j in range(NBANK):
                            pool.wait_ge(evacuated, NBANK * t + j + 1)
                            at = slice(j * BANK, (j + 1) * BANK)
                            nc.gpsimd.tensor_tensor(y[parity][:, at], y[parity][:, at], xn[parity][:, at], ALU.add).then_inc(res_added, 1)

                tiles(pool, slot, None, 0)

            @block.scalar
            def _(act):
                def slot(t, half, parity):
                    cur, nxt = is_batch(t, NT), is_batch(t + 1, NT)
                    if cur:
                        act.wait_ge(nmax_ready, t + 1)
                        nc.scalar.activation(probs[:], ag[:, ER:AG], ACT.Exp, bias=nmax[:]).then_inc(exp_done, 1)
                        act.wait_ge(ht_done, t + 1)
                        nc.scalar.activation(h_t[:], ps_h[:, :, 0:P], ACT.Copy).then_inc(ht_copied, 1)
                    if nxt:
                        for q in range(4):
                            act.wait_ge(t_filled, 4 * (t + 1) + q + 1)
                            nc.scalar.activation(x_hi[1 - parity][:, 4 * q:4 * q + 4, :],
                                                 ps_t[q % 2][:].rearrange("p (k c) -> p k c", k=4), ACT.Copy).then_inc(hi_done, 1)
                    if cur:
                        act.wait_ge(ln_ready, t + 1)
                        nc.scalar.activation(y[parity][:], y[parity][:], ACT.Identity, bias=nb_[:], scale=rs[:]).then_inc(out_ready, 1)

                tiles(act, slot, None, 0)

            @block.vector
            def _(dve):
                v = nc.vector
                chain = Chain(nc, dve, dve_step, consts["pad"])

                def slot(t, half, parity):
                    cur, nxt = is_batch(t, NT), is_batch(t + 1, NT)

                    def bank_out(j):
                        if j == 0:
                            after(dve, stored[parity], 16 * half)
                        dve.wait_ge(bank_done, NBANK * t + j + 1)
                        v.tensor_tensor(y[parity][:, j * BANK:(j + 1) * BANK], ps_y[j][:], irow[:, j * BANK:(j + 1) * BANK],
                                        ALU.mult).then_inc(evacuated, 1)

                    def low_half(q):
                        if nxt:
                            dve.wait_ge(hi_done, 4 * (t + 1) + q + 1)
                            v.tensor_tensor(x_lo[1 - parity][:, 4 * q:4 * q + 4, :], ps_t[q % 2][:].rearrange("p (k c) -> p k c", k=4),
                                            x_hi[1 - parity][:, 4 * q:4 * q + 4, :], ALU.subtract).then_inc(t_free, 1)

                    if not cur:
                        for q in range(4):
                            low_half(q)
                        return
                    dve.wait_ge(a_done, t + 1)
                    if isinstance(t, int) and t == 0:
                        dve.wait_ge(irow_loaded, 16)
                    chain.link(v.tensor_copy(ag2[:], ps_a[:, AG:2 * AG]))
                    v.tensor_tensor(ag[:], ps_a[:, 0:AG], ag2[:], ALU.add).then_inc(a_read, 1)
                    dve.wait_ge(a_read, t + 1)
                    chain.link(v.tensor_tensor(ag[:], ag[:], irow[:, L:L + AG], ALU.mult))
                    chain.link(v.tensor_reduce(tmp[:], ag[:, ER:AG], AX.X, ALU.max))
                    v.tensor_scalar(nmax[:], tmp[:], -1.0, None, ALU.mult).then_inc(nmax_ready, 1)
                    dve.wait_ge(exp_done, t + 1)
                    chain.settle()
                    chain.link(v.max(top[:], probs[:]))
                    chain.settle()
                    chain.link(v.max_index(top_i[:], top[:], probs[:]))
                    chain.link(v.tensor_tensor(pair[:], top[:, 0:1], top[:, 1:2], ALU.add))
                    chain.link(v.tensor_copy(top_f[:], top_i[:, 0:2]))
                    chain.link(v.reciprocal(pair[:], pair[:]))
                    chain.link(v.tensor_scalar(wtop[:], top[:, 0:2], pair[:], 2.0, ALU.mult, ALU.mult))
                    chain.link(v.tensor_scalar(dense[:], expert_ids[:], top_f[:, 0:1], wtop[:, 0:1], ALU.is_equal, ALU.mult))
                    chain.link(v.tensor_scalar(dense2[:], expert_ids[:], top_f[:, 1:2], wtop[:, 1:2], ALU.is_equal, ALU.mult))
                    chain.link(v.tensor_tensor(dense[:], dense[:], dense2[:], ALU.add))
                    chain.link(v.tensor_tensor(h[:].rearrange("p (e r) -> p e r", e=EXPERTS), ag[:, 0:ER].rearrange("p (e r) -> p e r", e=EXPERTS),
                                               dense[:].unsqueeze(2).to_broadcast([P, EXPERTS, RANK]), ALU.mult))
                    after(dve, ht_done, t)
                    chain.link(v.tensor_copy(h_parts[:, 0], h[:]))
                    chain.link(v.tensor_tensor(h_rest[:], h[:], h_parts[:, 0], ALU.subtract))
                    v.tensor_copy(h_parts[:, 3], h_parts[:, 0])
                    chain.link(v.tensor_copy(h_parts[:, 1], h_rest[:]))
                    v.tensor_tensor(h_parts[:, 2], h_rest[:], h_parts[:, 1], ALU.subtract).then_inc(h_ready, 1)
                    bank_out(0)
                    bank_out(1)
                    for q in range(4):
                        low_half(q)
                    bank_out(2)
                    bank_out(3)
                    for j in range(NBANK):
                        dve.wait_ge(res_added, NBANK * t + j + 1)
                        ins = v.bn_stats(stats[:, j], y[parity][:, j * BANK:(j + 1) * BANK])
                    chain.link(ins)
                    chain.settle()
                    chain.link(v.bn_aggr(mv[:], stats[:].rearrange("p a b -> p (a b)")))
                    after(dve, out_ready, t)
                    rsqrt_steps(nc, chain, rs[:], mv[:, 1:2], EPS, tmp[:], tmp2[:])
                    v.scalar_tensor_tensor(nb_[:], mv[:, 0:1], -1.0, rs[:], ALU.mult, ALU.mult).then_inc(ln_ready, 1)

                tiles(dve, slot, chain, 30)

            @block.tensor
            def _(pe):
                def slot(t, half, parity):
                    cur, nxt = is_batch(t, NT), is_batch(t + 1, NT)
                    other = 1 - parity

                    def transposed_bank(q):
                        if nxt:
                            if q == 0:
                                pe.wait_ge(x_loaded[other], 16 * (half + parity + 1))
                            after(pe, t_free, 4 * (t + 1) + q - 1)
                            for i in range(4):
                                k = 4 * q + i
                                ins = nc.tensor.transpose(ps_t[q % 2][:, i * P:(i + 1) * P], xn[other][:, k * P:(k + 1) * P], ident[:])
                            ins.then_inc(t_filled, 1)

                    if not cur:
                        for q in range(4):
                            transposed_bank(q)
                        return

                    def main(j):
                        if isinstance(t, int) and t == 0:
                            pe.wait_ge(w_loaded[j], 16)
                        after(pe, evacuated, NBANK * (t - 1) + j + 1)
                        for k in range(KT):
                            for xx, hh in ((x_hi, 0), (x_hi, 1), (x_lo, 0)):
                                nc.tensor.matmul(ps_y[j][:].rearrange("p (n c) -> p n c", c=P), xx[parity][:, k], w[:, 4 * j:4 * j + 4, hh, k, :],
                                                 start=(k == 0 and xx is x_hi and hh == 0), stop=False)

                    def lora(j):
                        nc.tensor.matmul(ps_y[j][:], h_t[:, 0], b_stack[:, 0, j * BANK:(j + 1) * BANK], start=False, stop=False)
                        nc.tensor.matmul(ps_y[j][:], h_t[:, 1], b_stack[:, 1, j * BANK:(j + 1) * BANK], start=False,
                                         stop=True).then_inc(bank_done, 1)

                    pe.wait_ge(t_free, 4 * (t + 1))
                    after(pe, a_read, t)
                    for k in range(KT):
                        nc.tensor.matmul(ps_a[:, 0:2 * AG], x_hi[parity][:, k], ag_t[:, k, :], start=(k == 0), stop=False)
                        ins = nc.tensor.matmul(ps_a[:, 0:AG], x_lo[parity][:, k], ag_t[:, k, 0:AG], start=False, stop=(k == KT - 1))
                    ins.then_inc(a_done, 1)
                    main(0)
                    pe.wait_ge(h_ready, t + 1)
                    after(pe, ht_copied, t)
                    for i in range(2):
                        ins = nc.tensor.transpose(ps_h[:, i, 0:P], h_parts[:, 2 * i:2 * i + 2].rearrange("p a b -> p (a b)"), ident16[:])
                    ins.then_inc(ht_done, 1)
                    main(1)
                    pe.wait_ge(ht_copied, t + 1)
                    lora(0)
                    lora(1)
                    transposed_bank(0)
                    transposed_bank(1)
                    main(2)
                    lora(2)
                    transposed_bank(2)
                    transposed_bank(3)
                    main(3)
                    lora(3)

                tiles(pe, slot, None, 0)


def setup(nc, consts):
    with ExitStack() as st:
        loaded, made = st.enter_context(nc.semaphore("ident_loaded")), st.enter_context(nc.semaphore("ident_made"))
        with nc.Block() as block:
            @block.sync
            def _(sp):
                sp.dma_start(consts["ident"][:], consts["ident_dram"]).then_inc(loaded, 16)
                sp.dma_start(consts["expert_ids"][:], consts["expert_dram"]).then_inc(loaded, 16)

            @block.vector
            def _(dve):
                nc.vector.memset(consts["worst"][:], -3e38).then_inc(made, 1)
                dve.wait_ge(loaded, 32)
                nc.vector.tensor_copy(consts["ident_bf16"][:], consts["ident"][:]).then_inc(made, 1)
                nc.vector.tensor_copy(consts["ident_f16"][:], consts["ident"][:]).then_inc(made, 1)
                dve.wait_ge(made, 3)


def autocorrelation(nc, x, z, forward_dram, inverse_dram, consts):
    nb = x.shape[0] // C
    TOP = 7
    BITS = L.bit_length() - 1
    with ExitStack() as st:
        def sb(name, shape, dt):
            return st.enter_context(nc.sbuf_tensor(f"{name}_c", shape, dt))

        def sem(name):
            return st.enter_context(nc.semaphore(f"{name}_c"))

        rows = sb("rows", [P, R, L], F32)
        x_t = sb("x_t", [P, KT, C], F32)
        table = [sb(f"table{i}", [P, KT, P], F32) for i in range(2)]
        lags = sb("lags", [P, KT, BANK], F32)
        power = sb("power", [P, KT, C], F32)
        corr = sb("corr", [P, R, L], F32)
        turn = [sb(f"turn{i}", [P, 2 * L], F32) for i in range(2)]
        acc = sb("acc", [P, L], F32)
        top, top_i = sb("top", [P, 8], F32), sb("top_i", [P, 8], U32)
        bit_u, bit, nbit = sb("bit_u", [P, BITS, 8], U32), sb("bit", [P, BITS, 8], F32), sb("nbit", [P, BITS, 8], F32)
        ntop, total, weight = sb("ntop", [P, 1], F32), sb("total", [P, 1], F32), sb("weight", [P, 8], F32)
        ident = consts["ident"]
        ps_t = [st.enter_context(nc.psum_tensor(f"ps_t{i}_c", [P, BANK], F32)) for i in range(2)]
        ps_f = [st.enter_context(nc.psum_tensor(f"ps_f{i}_c", [P, BANK], F32)) for i in range(2)]
        ps_c = [st.enter_context(nc.psum_tensor(f"ps_c{i}_c", [P, BANK], F32)) for i in range(2)]

        x_loaded, lags_loaded = sem("x_loaded"), sem("lags_loaded")
        table_loaded = [sem(f"table_loaded{i}") for i in range(2)]
        stored = sem("stored")
        t_filled, t_copied, fwd_done, squared = sem("t_filled"), sem("t_copied"), sem("fwd_done"), sem("squared")
        corr_done, corr_copied, ntop_ready, exp_done = sem("corr_done"), sem("corr_copied"), sem("ntop_ready"), sem("exp_done")
        z_ready, dve_step = sem("z_ready"), sem("dve_step")
        NBNK = R * NBANK

        def every_batch(eng, batch):
            batch(0)
            with eng.Fori(1, nb) as n:
                batch(n)

        with nc.Block() as block:
            @block.sync
            def _(sp):
                def batch(n):
                    after(sp, z_ready, R * n)
                    sp.dma_start(rows[:], x[bass.ds(n * C, C), :].rearrange("(r p) l -> p r l", p=P)).then_inc(x_loaded, 16)
                    for m in range(KT):
                        after(sp, fwd_done, KT * n + max(m - 1, 0))
                        sp.dma_start(table[m % 2][:], forward_dram[m]).then_inc(table_loaded[m % 2], 16)
                    for c in range(NBANK):
                        after(sp, corr_done, NBNK * n + R * c)
                        sp.dma_start(lags[:], inverse_dram[c]).then_inc(lags_loaded, 16)
                    for r in range(R):
                        sp.wait_ge(z_ready, R * n + r + 1)
                        sp.dma_start(z[bass.ds(n * C + r * P, P), :], acc[:]).then_inc(stored, 16)

                every_batch(sp, batch)
                sp.wait_ge(stored, 16 * R * nb)

            @block.gpsimd
            def _(pool):
                pool.wait_ge(z_ready, 1)

            @block.tensor
            def _(pe):
                def batch(n):
                    pe.wait_ge(x_loaded, 16 * (n + 1))
                    for q in range(NBNK):
                        after(pe, t_copied, NBNK * n + max(q - 1, 0))
                        for i in range(4):
                            k = 4 * (q % 4) + i
                            ins = nc.tensor.transpose(ps_t[q % 2][:, i * P:(i + 1) * P], rows[:, q // 4, k * P:(k + 1) * P], ident[:])
                        ins.then_inc(t_filled, 1)
                    pe.wait_ge(t_copied, NBNK * (n + 1))
                    for m in range(KT):
                        pe.wait_ge(table_loaded[m % 2], 16 * (KT // 2 * n + m // 2 + 1))
                        after(pe, squared, KT * n + max(m - 1, 0))
                        for k in range(KT):
                            ins = nc.tensor.matmul(ps_f[m % 2][:, 0:C], table[m % 2][:, k, :], x_t[:, k, :], start=(k == 0), stop=(k == KT - 1))
                        ins.then_inc(fwd_done, 1)
                    pe.wait_ge(squared, KT * (n + 1))
                    for c in range(NBANK):
                        pe.wait_ge(lags_loaded, 16 * (NBANK * n + c + 1))
                        for r in range(R):
                            after(pe, corr_copied, NBNK * n + max(R * c + r - 1, 0))
                            for m in range(KT):
                                ins = nc.tensor.matmul(ps_c[r][:], power[:, m, r * P:(r + 1) * P], lags[:, m, :], start=(m == 0), stop=(m == KT - 1))
                            ins.then_inc(corr_done, 1)

                every_batch(pe, batch)

            @block.scalar
            def _(act):
                def batch(n):
                    for q in range(NBNK):
                        act.wait_ge(t_filled, NBNK * n + q + 1)
                        r, kk = q // 4, 4 * (q % 4)
                        nc.scalar.activation(x_t[:, kk:kk + 4, r * P:(r + 1) * P], ps_t[q % 2][:].rearrange("p (k c) -> p k c", k=4),
                                             ACT.Copy).then_inc(t_copied, 1)
                    for m in range(KT):
                        act.wait_ge(fwd_done, KT * n + m + 1)
                        nc.scalar.activation(power[:, m], ps_f[m % 2][:, 0:C], ACT.Square).then_inc(squared, 1)
                    after(act, z_ready, R * n)
                    for c in range(NBANK):
                        for r in range(R):
                            act.wait_ge(corr_done, NBNK * n + R * c + r + 1)
                            nc.scalar.activation(corr[:, r, c * BANK:(c + 1) * BANK], ps_c[r][:], ACT.Copy).then_inc(corr_copied, 1)
                    for r in range(R):
                        act.wait_ge(ntop_ready, R * n + r + 1)
                        nc.scalar.activation(weight[:, 0:TOP], top[:, 0:TOP], ACT.Exp, bias=ntop[:], accum_out=total[:]).then_inc(exp_done, 1)

                every_batch(act, batch)

            @block.vector
            def _(dve):
                v = nc.vector
                chain = Chain(nc, dve, dve_step, consts["pad"])
                HEAD, LAG = 8, 2 * BITS + 3
                def batch(n):
                    for r in range(R):
                        chain.base, chain.count = (n * R + r) * (HEAD + TOP * LAG), 0
                        if r == 0:
                            dve.wait_ge(corr_copied, NBNK * (n + 1))
                        chain.settle()
                        chain.link(v.max(top[:], corr[:, r]))
                        chain.settle()
                        chain.link(v.max_index(top_i[:], top[:], corr[:, r]))
                        v.tensor_scalar(ntop[:], top[:, 0:1], -1.0, None, ALU.mult).then_inc(ntop_ready, 1)
                        for b in range(BITS):
                            ins = v.tensor_scalar(bit_u[:, b], top_i[:], b, 1, ALU.logical_shift_right, ALU.bitwise_and)
                        chain.link(ins)
                        chain.link(v.tensor_copy(bit[:], bit_u[:]))
                        chain.link(v.tensor_scalar(nbit[:], bit[:], -1.0, 1.0, ALU.mult, ALU.add))
                        dve.wait_ge(exp_done, R * n + r + 1)
                        chain.link(v.reciprocal(total[:], total[:]))
                        chain.link(v.tensor_scalar(weight[:, 0:TOP], weight[:, 0:TOP], total[:], None, ALU.mult))
                        after(dve, stored, 16 * (R * n + r))
                        chain.link(v.tensor_copy(acc[:], rows[:, r]))
                        assert chain.count == HEAD, chain.count
                        chain.settle()
                        with dve.Fori(0, TOP) as lag:
                            chain.base, chain.count = (n * R + r) * (HEAD + TOP * LAG) + HEAD + lag * LAG, 0
                            v.tensor_copy(turn[0][:, 0:L], rows[:, r])
                            chain.link(v.tensor_copy(turn[0][:, L:2 * L], rows[:, r]))
                            for i in range(BITS):
                                b = BITS - 1 - i
                                step, width = 1 << b, L + (1 << b) - 1
                                a, c = turn[i % 2], turn[1 - i % 2]
                                chain.link(v.tensor_scalar(c[:, 0:width], a[:, step:step + width], bit[:, b, bass.ds(lag, 1)], None, ALU.mult))
                                chain.link(v.scalar_tensor_tensor(c[:, 0:width], a[:, 0:width], nbit[:, b, bass.ds(lag, 1)],
                                                                  c[:, 0:width], ALU.mult, ALU.add))
                            chain.link(v.scalar_tensor_tensor(acc[:], turn[BITS % 2][:, 0:L], weight[:, bass.ds(lag, 1)], acc[:],
                                                              ALU.mult, ALU.add))
                            chain.link(v.tensor_copy(ntop[:], total[:]))
                            assert chain.count == LAG, chain.count
                        v.tensor_copy(ntop[:], total[:]).then_inc(z_ready, 1)

                every_batch(dve, batch)


def correlation_tables():
    j = np.arange(L, dtype=np.int64)
    cosine = np.cos(2 * np.pi * np.minimum(j, L - j) / L)
    sine = np.sin(2 * np.pi * j / L)
    freq = np.concatenate([np.arange(L // 2 + 1), np.arange(1, L // 2)]).astype(np.int64)
    is_sine = j > L // 2
    phase = (j[:, None] * freq[None, :]) % L
    fwd = np.where(is_sine[None, :], sine[phase], cosine[phase]) / np.sqrt(L / 2)
    once = (freq == 0) | (freq == L // 2)
    inv = cosine[phase.T] * np.where(once, 0.5, 1.0)[:, None]
    fwd = fwd.reshape(KT, P, KT, P).transpose(2, 1, 0, 3)
    inv = inv.reshape(KT, P, NBANK, BANK).transpose(2, 1, 0, 3)
    return np.ascontiguousarray(fwd, np.float32), np.ascontiguousarray(inv, np.float32)


def guard_flag(nc, consts, flag):
    with ExitStack() as st:
        most = st.enter_context(nc.sbuf_tensor("most", [P, R], F32))
        worst = st.enter_context(nc.sbuf_tensor("worst_all", [P, 1], F32))
        reduced, step = st.enter_context(nc.semaphore("reduced")), st.enter_context(nc.semaphore("flag_step"))
        with nc.Block() as block:
            @block.gpsimd
            def _(pool):
                nc.gpsimd.partition_all_reduce(most[:], consts["worst"][:], P, bass.bass_isa.ReduceOp.max).then_inc(reduced, 1)

            @block.vector
            def _(dve):
                dve.wait_ge(reduced, 1)
                nc.vector.tensor_reduce(worst[:], most[:], AX.X, ALU.max).then_inc(step, 1)
                dve.wait_ge(step, 1)
                nc.vector.tensor_scalar(flag[:], worst[:], -GUARD_GAP, None, ALU.is_gt).then_inc(step, 1)
                dve.wait_ge(step, 2)


def decoder_layer(nc, x, ctx_in, W, A, gate, B, fwd_dram, inv_dram, ident_dram, expert_dram, forward_dram, inverse_dram, out):
    rows = x.shape[0]
    x2 = nc.dram_tensor("x2_scratch", (rows, L), F32, kind="Internal").ap()
    z = nc.dram_tensor("z_scratch", (rows, L), F32, kind="Internal").ap()
    w_scratch = nc.dram_tensor("w_scratch", (L // P, P, 2 * L), F16, kind="Internal").ap()
    iscale_scratch = nc.dram_tensor("iscale_scratch", (L + P, 1), F32, kind="Internal").ap()
    with ExitStack() as st:
        def sb(name, shape, dt):
            return st.enter_context(nc.sbuf_tensor(name, shape, dt))

        consts = dict(
            ident=sb("ident", [P, P], F32), ident_bf16=sb("ident_bf16", [P, P], BF16), ident_f16=sb("ident_f16", [P, P], F16),
            worst=sb("worst", [P, R], F32), pad=sb("pad", [P, 1], F32), expert_ids=sb("expert_ids", [P, EXPERTS], F32),
            b_stack=sb("b_stack", [P, 2, L], F16),
            ag_t=sb("ag_t", [P, KT, 2 * AG], F16),
            fwd_dram=fwd_dram, inv_dram=inv_dram, ident_dram=ident_dram, expert_dram=expert_dram)
        setup(nc, consts)
        prepare_weights(nc, W, A, gate, B, consts, w_scratch, iscale_scratch)
        attention_pass(nc, x, ctx_in, x2, consts, EPS / 4, "fast")
        flag = sb("flag", [P, 1], I32)
        guard_flag(nc, consts, flag)
        some_row_needs_it = nc.values_load(flag[0:1, 0:1], min_val=0, max_val=1)
        with nc.If(some_row_needs_it):
            autocorrelation(nc, x, z, forward_dram, inverse_dram, consts)
            attention_pass(nc, z, ctx_in, x2, consts, EPS, "full")
        feed_forward(nc, x2, out, consts, w_scratch, iscale_scratch)


def kernel(x, ctx_4096, L0_ffn_W_base, L0_ffn_gate_W, L0_ffn_A, L0_ffn_B):
    import ml_dtypes
    import concourse.bacc as bacc
    from concourse.bass_utils import run_bass_kernel_spmd

    shape = x.shape
    fwd, inv = guard_tables()
    forward, inverse = correlation_tables()
    arrays = {
        "x": np.ascontiguousarray(x).reshape(-1, L),
        "ctx_in": np.ascontiguousarray(ctx_4096).reshape(-1, L),
        "W": np.ascontiguousarray(L0_ffn_W_base),
        "A": np.ascontiguousarray(L0_ffn_A).reshape(ER, L),
        "gate": np.ascontiguousarray(L0_ffn_gate_W),
        "B": np.ascontiguousarray(np.transpose(L0_ffn_B, (1, 0, 2))).reshape(L, ER),
        "fwd_dram": fwd.astype(ml_dtypes.bfloat16),
        "inv_dram": inv.astype(ml_dtypes.bfloat16),
        "forward_dram": forward,
        "inverse_dram": inverse,
        "ident_dram": np.eye(P, dtype=np.float32),
        "expert_dram": np.tile(np.arange(EXPERTS, dtype=np.float32), (P, 1)),
    }
    nc = bacc.Bacc("TRN2", target_bir_lowering=False, num_devices=1)
    aps = {n: nc.dram_tensor(n, a.shape, mybir.dt.from_np(a.dtype), kind="ExternalInput").ap() for n, a in arrays.items()}
    out = nc.dram_tensor("out", arrays["x"].shape, F32, kind="ExternalOutput").ap()
    decoder_layer(nc, out=out, **aps)
    r = run_bass_kernel_spmd(nc, [arrays], core_ids=[0])
    return r.results[0]["out"].reshape(shape)
```

```python
from contextlib import ExitStack

import numpy as np

import concourse.bass as bass
from concourse import mybir

F32 = mybir.dt.float32
F16 = mybir.dt.float16
BF16 = mybir.dt.bfloat16
I32 = mybir.dt.int32
U32 = mybir.dt.uint32
ALU = mybir.AluOpType
ACT = mybir.ActivationFunctionType
AX = mybir.AxisListType

P = 128
L = 2048
C = 256
R = C // P
KT = L // P
BANK = 512
NBANK = L // BANK
EPS = 1e-5
EXPERTS, RANK = 8, 8
ER = EXPERTS * RANK
AG = ER + EXPERTS
EPS4_AT, EPS_AT, MINUS_ONE, MINUS_HALF = range(4)
GUARD_GAP = 110.0
PAIRS = 256
HALF = L // 2


def after(eng, sem, value):
    if isinstance(value, int) and value <= 0:
        return
    eng.wait_ge(sem, value)


class Chain:

    def __init__(self, nc, eng, sem, pad):
        self.eng, self.sem, self.base, self.count = eng, sem, 0, 0
        self.pad_memset, self.pad = nc.vector.memset, pad[:]

    def link(self, instruction):
        self.count += 1
        instruction.then_inc(self.sem, 1)
        self.eng.wait_ge(self.sem, self.base + self.count)

    def settle(self):
        self.pad_memset(self.pad, 0.0)

    def mark(self):
        done, self.count = self.count, 0
        self.base = self.base + done
        return done


def batch_slots(eng, chain, nb, slot, links):
    for n in (-2, -1, 0, 1):
        slot(n, n // 2, n % 2)
        if chain:
            chain.mark()
    if nb > 4:
        start = chain.base - 2 * links if chain else 0
        with eng.Fori(1, (nb - 2) // 2) as m:
            for parity in range(2):
                n = 2 * m + parity
                if chain:
                    chain.base, chain.count = n * links + start, 0
                slot(n, m, parity)
                if chain:
                    assert chain.count == links, (chain.count, links)
        if chain:
            chain.base, chain.count = start + (nb - 2) * links, 0
    for n in (nb - 2, nb - 1):
        slot(n, n // 2, n % 2)
        if chain:
            chain.mark()


def is_batch(n, nb):
    return not isinstance(n, int) or 0 <= n < nb


def rsqrt_steps(nc, chain, rstd, var, eps, tmp, tmp2):
    v = nc.vector
    chain.link(v.tensor_scalar(tmp, var, eps, None, ALU.add))
    chain.link(v.tensor_scalar(tmp2.bitcast(I32), tmp.bitcast(I32), 1, None, ALU.arith_shift_right))
    chain.link(v.tensor_scalar(rstd.bitcast(I32), tmp2.bitcast(I32), -1.0, float(0x5F3759DF), ALU.mult, ALU.add))
    for _ in range(3):
        chain.link(v.tensor_tensor(tmp2, rstd, tmp, ALU.mult))
        chain.link(v.scalar_tensor_tensor(tmp2, tmp2, -0.5, rstd, ALU.mult, ALU.mult))
        chain.link(v.scalar_tensor_tensor(rstd, tmp2, 1.5, rstd, ALU.add, ALU.mult))


def scale_steps(nc, chain, scale, inverse, total, tmp):
    v = nc.vector
    chain.link(v.tensor_scalar(tmp.bitcast(U32), total.bitcast(U32), 24, None, ALU.logical_shift_right))
    v.tensor_scalar(scale.bitcast(I32), tmp.bitcast(I32), -float(1 << 23), float(204 << 23), ALU.mult, ALU.add)
    chain.link(v.tensor_scalar(inverse.bitcast(I32), tmp.bitcast(I32), float(1 << 23), float(50 << 23), ALU.mult, ALU.add))


def attention_pass(nc, src, ctx_in, x2_out, w_rows, b_rows, consts, eps_column, tag):
    nb = src.shape[0] // C
    with ExitStack() as st:
        def sb(name, shape, dt):
            return st.enter_context(nc.sbuf_tensor(f"{name}_{tag}", shape, dt))

        def sem(name):
            return st.enter_context(nc.semaphore(f"{name}_{tag}"))

        xbuf = [sb(f"xbuf{i}", [P, R, L], F32) for i in range(2)]
        cbuf = [sb(f"cbuf{i}", [P, R, L], F32) for i in range(2)]
        x2buf = sb("x2buf", [P, R, L], F32)
        v_hi, v_lo = sb("v_hi", [P, R, L], F16), sb("v_lo", [P, R, L], F16)
        q_hi, q_lo = sb("q_hi", [P, KT, C], F16), sb("q_lo", [P, KT, C], F16)
        k_hi, k_lo = sb("k_hi", [P, KT, C], F16), sb("k_lo", [P, KT, C], F16)
        p_hi, p_lo = sb("p_hi", [P, R, C], F16), sb("p_lo", [P, R, C], F16)
        expd = sb("expd", [P, R, C], F32)
        u_rows = sb("u_rows", [P, R, HALF], BF16)
        u_t = sb("u_t", [P, HALF // P, C], BF16)
        power = sb("power", [P, 4, C], BF16)
        fwd = sb("fwd", [P, HALF // P, 2 * PAIRS], BF16)
        inv = sb("inv", [P, 4, BANK], BF16)
        junk = sb("junk", [P, L], BF16)
        stats = sb("stats", [P, R, NBANK, 6], F32)
        stats2 = sb("stats2", [P, R, NBANK, 6], F32)
        mv1 = sb("mv1", [P, R, 2], F32)
        mv2 = sb("mv2", [P, R, 2], F32)
        rs1, nb1 = sb("rs1", [P, R], F32), sb("nb1", [P, R], F32)
        rs2, nb2 = sb("rs2", [P, R], F32), sb("nb2", [P, R], F32)
        tmp, tmp2 = sb("tmp", [P, R], F32), sb("tmp2", [P, R], F32)
        var_eps = [sb(f"var_eps{i}", [P, R], F32) for i in range(2)]
        nmean = [sb(f"nmean{i}", [P, R], F32) for i in range(2)]
        mean_sq = sb("mean_sq", [P, R], F32)
        pool_pad = sb("pool_pad", [P, R], F32)
        w_tile = sb("w_tile", [P, L], F32)
        w_sumsq = sb("w_sumsq", [P, L // P + 1], F32)
        w_total, w_total_all = sb("w_total", [P, 1], F32), sb("w_total_all", [P, 1], F32)
        sumsq = [sb(f"sumsq{i}", [P, R], F32) for i in range(2)]
        sumall = [sb(f"sumall{i}", [P, R], F32) for i in range(2)]
        scale = [sb(f"scale{i}", [P, 1], F32) for i in range(2)]
        iscale = [sb(f"iscale{i}", [P, 1], F32) for i in range(2)]
        lscale = [sb(f"lscale{i}", [P, 1], F32) for i in range(2)]
        rowmax, nmax = sb("rowmax", [P, R], F32), sb("nmax", [P, R], F32)
        psum_e, rinv = sb("psum_e", [P, R], F32), sb("rinv", [P, R], F32)
        gmax = sb("gmax", [P, R], F32)
        ident = consts["ident"]
        ident16 = consts["ident_bf16"]
        g_lags, g_energy, columns = consts["g_lags"], consts["g_energy"], consts["columns"]

        ps_t = [st.enter_context(nc.psum_tensor(f"ps_t{i}_{tag}", [P, BANK], F32)) for i in range(3)]
        ps_c = [st.enter_context(nc.psum_tensor(f"ps_c{i}_{tag}", [P, BANK], F32)) for i in range(2)]
        ps_s = [st.enter_context(nc.psum_tensor(f"ps_s{i}_{tag}", [P, BANK], F32)) for i in range(R)]
        ps_g = [st.enter_context(nc.psum_tensor(f"ps_g_{tag}", [P, BANK], F32)), ps_t[2]]

        x_loaded = [[sem(f"x_loaded{i}{r}") for r in range(R)] for i in range(2)]
        c_loaded = [[sem(f"c_loaded{i}{r}") for r in range(R)] for i in range(2)]
        stored = [sem(f"stored{r}") for r in range(R)]
        tables_loaded = sem("tables_loaded")
        folded, x1_ready, ln1_ready = sem("folded"), sem("x1_ready"), sem("ln1_ready")
        sumsq_done, sumall_done, scale_ready = sem("sumsq_done"), sem("sumall_done"), sem("scale_ready")
        t_filled, hi_done, t_free = sem("t_filled"), sem("hi_done"), sem("t_free")
        sim_done, nmax_ready, exp_done, p_ready = sem("sim_done"), sem("nmax_ready"), sem("exp_done"), sem("p_ready")
        vhi_done, vlo_done = sem("vhi_done"), sem("vlo_done")
        fwd_done, sq_done, inv_done, g_free = sem("fwd_done"), sem("sq_done"), sem("inv_done"), sem("g_free")
        context_done, ctx_added = sem("context_done"), sem("ctx_added")
        ln2_ready, x2_ready = sem("ln2_ready"), sem("x2_ready")
        dve_step, pool_step = sem("dve_step"), sem("pool_step")
        u_copied, c_scaled = sem("u_copied"), sem("c_scaled")
        w_cleared, w_scaled = sem("w_cleared"), sem("w_scaled")
        w_loaded, w_squared, w_summed, w_reduced = sem("w_loaded"), sem("w_squared"), sem("w_summed"), sem("w_reduced")
        mv1_ready, mv2_ready, mv1_free = sem("mv1_ready"), sem("mv2_ready"), sem("mv1_free")

        TB = 18
        TS = 16
        W_TILES = L // P + 1
        assert nb == L // P
        CG = R * NBANK

        with nc.Block() as block:
            @block.sync
            def _(sp):
                sp.dma_start(fwd[:], consts["fwd_dram"]).then_inc(tables_loaded, 16)
                sp.dma_start(inv[:], consts["inv_dram"]).then_inc(tables_loaded, 16)

                def slot(n, half, parity):
                    if is_batch(n + 2, nb):
                        after(sp, ctx_added, CG * (n + 1))
                        for r in range(R):
                            sp.dma_start(xbuf[parity][:, r], src[bass.ds((n + 2) * C + r * P, P), :]).then_inc(x_loaded[parity][r], 16)
                        after(sp, vlo_done, R * (n + 1))
                        for r in range(R):
                            sp.dma_start(cbuf[parity][:, r], ctx_in[bass.ds((n + 2) * C + r * P, P), :]).then_inc(c_loaded[parity][r], 16)
                    if is_batch(n + 2, W_TILES):
                        after(sp, w_squared, n + 2)
                        if isinstance(n, int) and n == -2:
                            sp.dma_start(w_tile[0:ER, :], b_rows).then_inc(w_loaded, 16)
                        else:
                            sp.dma_start(w_tile[:], w_rows[bass.ds((n + 1) * P, P), :]).then_inc(w_loaded, 16)
                    if is_batch(n, nb):
                        for r in range(R):
                            sp.wait_ge(x2_ready, R * n + r + 1)
                            sp.dma_start(x2_out[bass.ds(n * C + r * P, P), :], x2buf[:, r]).then_inc(stored[r], 16)

                batch_slots(sp, None, nb, slot, 0)
                for r in range(R):
                    sp.wait_ge(stored[r], 16 * nb)

            @block.gpsimd
            def _(pool):
                g = nc.gpsimd
                chain = Chain(nc, pool, pool_step, consts["pad"])

                def settle():
                    g.tensor_tensor(pool_pad[:], columns[:, MINUS_ONE], columns[:, MINUS_ONE], ALU.mult)

                def norm_steps(i, mv, eps_at, rstd, nbias, ready):
                    g.tensor_tensor(var_eps[i][:], mv[:, :, 1], columns[:, eps_at], ALU.add)
                    chain.link(g.tensor_tensor(nmean[i][:], mv[:, :, 0], columns[:, MINUS_ONE], ALU.mult))
                    chain.link(g.tensor_tensor(rstd, var_eps[i][:], columns[:, MINUS_HALF], ALU.pow))
                    g.tensor_tensor(nbias, nmean[i][:], rstd, ALU.mult).then_inc(ready, 1)

                def slot(n, half, parity):
                    cur, nxt, n2 = is_batch(n, nb), is_batch(n + 1, nb), is_batch(n + 2, nb)
                    other = 1 - parity
                    if cur:
                        pool.wait_ge(mv2_ready, n + 1)
                        after(pool, x2_ready, R * n)
                        norm_steps(1, mv2, EPS_AT, rs2[:], nb2[:], ln2_ready)
                    if nxt:
                        for r in range(R):
                            pool.wait_ge(vhi_done, R * (n + 1) + r + 1)
                            g.tensor_tensor(v_lo[:, r], cbuf[other][:, r], v_hi[:, r], ALU.subtract).then_inc(vlo_done, 1)
                    if n2:
                        for r in range(R):
                            pool.wait_ge(x_loaded[parity][r], 16 * (half + 2))
                            if r == 0:
                                after(pool, t_filled, TB * (n + 2))
                            g.tensor_tensor(u_rows[:, r], xbuf[parity][:, r, 0:HALF], xbuf[parity][:, r, HALF:L],
                                            ALU.subtract).then_inc(folded, 1)
                        pool.wait_ge(mv1_ready, n + 3)
                        after(pool, x1_ready, R * (n + 2))
                        g.tensor_tensor(mean_sq[:], mv1[:, :, 0], mv1[:, :, 0], ALU.mult)
                        norm_steps(0, mv1, eps_column, rs1[:], nb1[:], ln1_ready)
                        pool.wait_ge(ln1_ready, n + 3)
                        g.tensor_tensor(g_energy[:, bass.ds((n + 2) * R, R)], mean_sq[:], mv1[:, :, 1], ALU.add).then_inc(mv1_free, 1)
                        pool.wait_ge(sumsq_done, R * (n + 3))
                        settle()
                        g.partition_all_reduce(sumall[parity][:], sumsq[parity][:], P,
                                               bass.bass_isa.ReduceOp.add).then_inc(sumall_done, 1)
                        pool.wait_ge(scale_ready, n + 3)
                        settle()
                        for r in range(R):
                            g.tensor_scalar(cbuf[parity][:, r], cbuf[parity][:, r], scale[parity][:], 1.0, ALU.mult,
                                            ALU.mult).then_inc(c_scaled, 1)
                    if isinstance(n, int) and n == nb - 1:
                        pool.wait_ge(w_summed, 1)
                        g.partition_all_reduce(w_total_all[:], w_total[:], P, bass.bass_isa.ReduceOp.add).then_inc(w_reduced, 1)

                batch_slots(pool, chain, nb, slot, 4)

            @block.scalar
            def _(act):
                def slot(n, half, parity):
                    cur, nxt, n2 = is_batch(n, nb), is_batch(n + 1, nb), is_batch(n + 2, nb)
                    other = 1 - parity
                    if nxt:
                        for q in range(2 * CG):
                            after(act, t_filled, TB * (n + 1) + q + 1)
                            r, kk = (q // 4) % 2, 4 * (q % 4)
                            bank = ps_t[q % 3][:].rearrange("p (k c) -> p k c", k=4)
                            if q < CG:
                                nc.scalar.activation(q_hi[:, kk:kk + 4, r * P:(r + 1) * P], bank, ACT.Copy).then_inc(hi_done, 1)
                            else:
                                nc.scalar.activation(k_hi[:, kk:kk + 4, r * P:(r + 1) * P], bank, ACT.Copy).then_inc(hi_done, 1)
                        for r in range(R):
                            act.wait_ge(t_filled, TB * (n + 1) + TS + r + 1)
                            bank = ps_t[(TS + r) % 3][:].bitcast(BF16).rearrange("p (k c) -> p k c", c=P)
                            nc.scalar.activation(u_t[:, :, r * P:(r + 1) * P], bank, ACT.Copy).then_inc(u_copied, 1)
                        after(act, context_done, CG * (n + 1))
                        for r in range(R):
                            nc.scalar.activation(v_hi[:, r], cbuf[other][:, r], ACT.Copy).then_inc(vhi_done, 1)

                    def apply2(r):
                        if cur:
                            act.wait_ge(ln2_ready, n + 1)
                            nc.scalar.activation(x2buf[:, r], x2buf[:, r], ACT.Identity, bias=nb2[:, r:r + 1],
                                                 scale=rs2[:, r:r + 1]).then_inc(x2_ready, 1)

                    def softmax_exp(r):
                        if nxt:
                            after(act, p_ready, R * n + r + 1)
                            act.wait_ge(nmax_ready, R * (n + 1) + r + 1)
                            nc.scalar.activation(expd[:, r], ps_s[r][:, 0:C], ACT.Exp, bias=nmax[:, r:r + 1],
                                                 scale=lscale[other][:], accum_out=psum_e[:, r:r + 1]).then_inc(exp_done, 1)

                    softmax_exp(0)
                    apply2(0)
                    softmax_exp(1)
                    apply2(1)
                    if nxt:
                        after(act, inv_done, R * (n + 1))
                        for m in range(4):
                            act.wait_ge(fwd_done, 4 * (n + 1) + m + 1)
                            nc.scalar.activation(power[:, m], ps_t[m % 2][:, 0:C], ACT.Square).then_inc(sq_done, 1)
                    if n2:
                        for r in range(R):
                            act.wait_ge(c_loaded[parity][r], 16 * (half + 2))
                            after(act, sumsq_done, R * (n + 2) + r)
                            after(act, w_squared, n + 2)
                            nc.scalar.activation(junk[:], cbuf[parity][:, r], ACT.Square,
                                                 accum_out=sumsq[parity][:, r:r + 1]).then_inc(sumsq_done, 1)
                        act.wait_ge(ln1_ready, n + 3)
                        for r in range(R):
                            act.wait_ge(folded, R * (n + 2) + r + 1)
                            nc.scalar.activation(xbuf[parity][:, r], xbuf[parity][:, r], ACT.Identity, bias=nb1[:, r:r + 1],
                                                 scale=rs1[:, r:r + 1]).then_inc(x1_ready, 1)
                    if is_batch(n + 2, W_TILES):
                        act.wait_ge(w_loaded, 16 * (n + 3))
                        act.wait_ge(sumsq_done, R * (n + 3) if n2 else R * nb)
                        if isinstance(n, int) and n == -2:
                            act.wait_ge(w_cleared, 1)
                            nc.scalar.activation(junk[0:ER, :], w_tile[0:ER, :], ACT.Square, accum_out=w_sumsq[0:ER, 0:1]).then_inc(w_squared, 1)
                        else:
                            nc.scalar.activation(junk[:], w_tile[:], ACT.Square,
                                                 accum_out=w_sumsq[:, bass.ds(n + 2, 1)]).then_inc(w_squared, 1)

                batch_slots(act, None, nb, slot, 0)

            @block.vector
            def _(dve):
                v = nc.vector
                chain = Chain(nc, dve, dve_step, consts["pad"])
                v.memset(w_sumsq[:], 0.0).then_inc(w_cleared, 1)

                def slot(n, half, parity):
                    cur, nxt, n2 = is_batch(n, nb), is_batch(n + 1, nb), is_batch(n + 2, nb)
                    other = 1 - parity

                    def x2_stats(j):
                        dve.wait_ge(ctx_added, CG * n + j + 1)
                        r, b = j // NBANK, j % NBANK
                        return v.bn_stats(stats2[:, r, b], x2buf[:, r, b * BANK:(b + 1) * BANK])

                    for j in range(CG):
                        if cur:
                            r, b = j // NBANK, j % NBANK
                            if b == 0:
                                after(dve, stored[r], 16 * n)
                            dve.wait_ge(context_done, CG * n + j + 1)
                            v.scalar_tensor_tensor(x2buf[:, r, b * BANK:(b + 1) * BANK], ps_c[j % 2][:], iscale[parity][:],
                                                   xbuf[parity][:, r, b * BANK:(b + 1) * BANK], ALU.mult,
                                                   ALU.add).then_inc(ctx_added, 1)
                            if j:
                                x2_stats(j - 1)
                        if nxt:
                            for q in (2 * j, 2 * j + 1):
                                r, kk = (q // 4) % 2, 4 * (q % 4)
                                at = (slice(None), slice(kk, kk + 4), slice(r * P, (r + 1) * P))
                                bank = ps_t[q % 3][:].rearrange("p (k c) -> p k c", k=4)
                                hi, lo = (q_hi, q_lo) if q < CG else (k_hi, k_lo)
                                after(dve, hi_done, TS * (n + 1) + q + 1)
                                v.tensor_tensor(lo[at], bank, hi[at], ALU.subtract).then_inc(t_free, 1)
                    if cur:
                        chain.link(x2_stats(CG - 1))
                    if cur:
                        after(dve, ln2_ready, n)
                        chain.settle()
                        chain.link(v.bn_aggr(mv2[:, 0], stats2[:, 0].rearrange("p a b -> p (a b)")))
                        chain.settle()
                        v.bn_aggr(mv2[:, 1], stats2[:, 1].rearrange("p a b -> p (a b)")).then_inc(mv2_ready, 1)

                    def softmax_max(r):
                        if nxt:
                            dve.wait_ge(sim_done, R * (n + 1) + r + 1)
                            dve.wait_ge(scale_ready, n + 2)
                            chain.link(v.tensor_reduce(rowmax[:, r:r + 1], ps_s[r][:, 0:C], AX.X, ALU.max))
                            v.tensor_scalar(nmax[:, r:r + 1], rowmax[:, r:r + 1], iscale[other][:], -(C ** -0.5), ALU.mult,
                                            ALU.mult).then_inc(nmax_ready, 1)

                    def softmax_norm(r):
                        if nxt:
                            dve.wait_ge(exp_done, R * (n + 1) + r + 1)
                            chain.link(v.reciprocal(rinv[:, r:r + 1], psum_e[:, r:r + 1]))
                            chain.link(v.tensor_scalar(p_hi[:, r], expd[:, r], rinv[:, r:r + 1], None, ALU.mult))
                            v.scalar_tensor_tensor(p_lo[:, r], expd[:, r], rinv[:, r:r + 1], p_hi[:, r], ALU.mult,
                                                   ALU.subtract).then_inc(p_ready, 1)

                    def x_stats(r):
                        if n2:
                            dve.wait_ge(x_loaded[parity][r], 16 * (half + 2))
                            for b in range(NBANK):
                                ins = v.bn_stats(stats[:, r, b], xbuf[parity][:, r, b * BANK:(b + 1) * BANK])
                            chain.link(ins)
                            if r == 0:
                                after(dve, mv1_free, n + 2)
                            chain.settle()
                            ins = v.bn_aggr(mv1[:, r], stats[:, r].rearrange("p a b -> p (a b)"))
                            if r == 0:
                                chain.link(ins)
                            else:
                                ins.then_inc(mv1_ready, 1)

                    softmax_max(0)
                    x_stats(0)
                    softmax_norm(0)
                    softmax_max(1)
                    x_stats(1)
                    softmax_norm(1)
                    if n2:
                        dve.wait_ge(sumall_done, n + 3)
                        chain.link(v.tensor_tensor(tmp[:, 0:1], sumall[parity][:, 0:1], sumall[parity][:, 1:2], ALU.add))
                        scale_steps(nc, chain, scale[parity][:], iscale[parity][:], tmp[:, 0:1], tmp2[:, 0:1])
                        v.tensor_scalar(lscale[parity][:], iscale[parity][:], C ** -0.5, None, ALU.mult).then_inc(scale_ready, 1)
                    if nxt:
                        for r in range(R):
                            dve.wait_ge(inv_done, R * (n + 1) + r + 1)
                            chain.link(v.tensor_reduce(gmax[:, r:r + 1], ps_g[r][:, 1:BANK], AX.X, ALU.max, apply_absolute_value=True))
                            v.tensor_tensor(g_lags[:, bass.ds((n + 1) * R + r, 1)], gmax[:, r:r + 1], ps_g[r][:, 0:1],
                                            ALU.subtract).then_inc(g_free, 1)
                    if isinstance(n, int) and n == nb - 1:
                        dve.wait_ge(w_squared, W_TILES)
                        v.tensor_reduce(w_total[:], w_sumsq[:], AX.X, ALU.add).then_inc(w_summed, 1)
                        dve.wait_ge(w_reduced, 1)
                        scale_steps(nc, chain, consts["w_scale"][:], consts["w_iscale"][:], w_total_all[:], tmp[:, 0:1])

                batch_slots(dve, chain, nb, slot, 16)

            @block.tensor
            def _(pe):
                pe.wait_ge(tables_loaded, 32)

                def slot(n, half, parity):
                    cur, nxt = is_batch(n, nb), is_batch(n + 1, nb)
                    other = 1 - parity

                    def transposed_bank(q):
                        after(pe, t_free, TS * (n + 1) + max(q - 2, 0))
                        if q in (1, 2):
                            after(pe, u_copied, R * (n + 1))
                        if q == 2:
                            after(pe, g_free, R * (n + 1))
                        r, kk = (q // 4) % 2, 4 * (q % 4)
                        bank = ps_t[q % 3]
                        if q < CG and q % 4 == 0:
                            pe.wait_ge(x1_ready, R * (n + 1) + r + 1)
                        if CG <= q < 2 * CG and q % 4 == 0:
                            pe.wait_ge(c_scaled, R * (n + 1) + r + 1)
                        if q < 2 * CG:
                            rows = xbuf[other] if q < CG else cbuf[other]
                            for i in range(4):
                                ins = nc.tensor.transpose(bank[:, i * P:(i + 1) * P], rows[:, r, (kk + i) * P:(kk + i + 1) * P], ident[:])
                        else:
                            r = q - 2 * CG
                            pe.wait_ge(folded, R * (n + 1) + r + 1)
                            out = bank[:].bitcast(BF16)
                            for i in range(HALF // P):
                                ins = nc.tensor.transpose(out[:, i * P:(i + 1) * P], u_rows[:, r, i * P:(i + 1) * P], ident16[:])
                        ins.then_inc(t_filled, 1)

                    for j in range(CG):
                        if cur:
                            if j == 0:
                                pe.wait_ge(p_ready, R * (n + 1))
                                pe.wait_ge(vlo_done, R * (n + 1))
                            after(pe, ctx_added, CG * n + j - 1)
                            r, b = j // NBANK, j % NBANK
                            terms = [(p_hi, v_hi), (p_hi, v_lo), (p_lo, v_hi)]
                            for i in range(3 * R):
                                pp, vv = terms[i % 3]
                                d = i // 3
                                ins = nc.tensor.matmul(ps_c[j % 2][:], pp[:, d, r * P:(r + 1) * P], vv[:, d, b * BANK:(b + 1) * BANK],
                                                       start=(i == 0), stop=(i == 3 * R - 1))
                            ins.then_inc(context_done, 1)
                        if nxt:
                            transposed_bank(2 * j)
                            transposed_bank(2 * j + 1)
                    if nxt:
                        transposed_bank(16)
                        transposed_bank(17)
                        after(pe, exp_done, R * (n + 1))
                        pe.wait_ge(t_free, TS * (n + 2))
                        for r in range(R):
                            terms = [(q_hi, k_hi), (q_hi, k_lo), (q_lo, k_hi)]
                            for i in range(3 * KT):
                                qq, kk = terms[i % 3]
                                k = i // 3
                                ins = nc.tensor.matmul(ps_s[r][:, 0:C], qq[:, k, r * P:(r + 1) * P], kk[:, k, :],
                                                       start=(i == 0), stop=(i == 3 * KT - 1))
                            ins.then_inc(sim_done, 1)
                        pe.wait_ge(u_copied, R * (n + 2))
                        for m in range(4):
                            if m >= 2:
                                pe.wait_ge(sq_done, 4 * (n + 1) + m - 1)
                            for k in range(HALF // P):
                                ins = nc.tensor.matmul(ps_t[m % 2][:, 0:C], fwd[:, k, m * P:(m + 1) * P], u_t[:, k, :],
                                                       start=(k == 0), stop=(k == HALF // P - 1))
                            ins.then_inc(fwd_done, 1)
                        pe.wait_ge(sq_done, 4 * (n + 2))
                        for r in range(R):
                            for m in range(4):
                                ins = nc.tensor.matmul(ps_g[r][:], power[:, m, r * P:(r + 1) * P], inv[:, m, :],
                                                       start=(m == 0), stop=(m == 3))
                            ins.then_inc(inv_done, 1)

                batch_slots(pe, None, nb, slot, 0)


def guard_tables():
    order = (np.arange(L // 4) * 197 + 61) % (L // 4)
    freq = np.sort(2 * order[:PAIRS] + 1).astype(np.int64)
    pos = np.arange(HALF, dtype=np.int64)
    angle = 2 * np.pi * ((pos[:, None] * freq[None, :]) % L) / L
    fwd = np.concatenate([np.cos(angle), np.sin(angle)], 1) / np.sqrt(L / 2)
    lag = np.arange(BANK, dtype=np.int64)
    both = np.concatenate([freq, freq])
    inv = np.cos(2 * np.pi * ((both[:, None] * lag[None, :]) % L) / L)
    return (fwd.reshape(HALF // P, P, 2 * PAIRS).transpose(1, 0, 2).copy(), inv.reshape(4, P, BANK).transpose(1, 0, 2).copy())


def feed_forward(nc, x2, out, w_chunks, b_rows, ag_in, consts):
    NT = x2.shape[0] // P
    CHUNKS = w_chunks.shape[0]
    KC = KT // (CHUNKS // NBANK)
    with ExitStack() as st:
        def sb(name, shape, dt):
            return st.enter_context(nc.sbuf_tensor(f"{name}_f", shape, dt))

        def sem(name):
            return st.enter_context(nc.semaphore(f"{name}_f"))

        w_hi, w_lo = sb("w_hi", [P, KT, L], F16), sb("w_lo", [P, KT, L], F16)
        b_stack = sb("b_stack", [P, 2, L], F16)
        ag_t = sb("ag_t", [P, KT, 2 * AG], F16)
        xn = [sb(f"xn{i}", [P, L], F32) for i in range(2)]
        x_hi = [sb(f"x_hi{i}", [P, KT, P], F16) for i in range(2)]
        x_lo = [sb(f"x_lo{i}", [P, KT, P], F16) for i in range(2)]
        y = [sb(f"y{i}", [P, L], F32) for i in range(2)]
        ag_raw = y[0][:, 0:KT * AG].rearrange("p (k c) -> p k c", k=KT)
        b_raw = y[0]
        chunk = [sb("chunk0", [P, KC, BANK], F32)[:], y[1][:].rearrange("p (k c) -> p k c", k=KC)]
        ag_sumsq, ag_total = sb("ag_sumsq", [P, 2], F32), sb("ag_total", [P, 2], F32)
        ag_scale, ag_iscale = sb("ag_scale", [P, 2], F32), sb("ag_iscale", [P, 2], F32)
        stats, mv = sb("stats", [P, NBANK, 6], F32), sb("mv", [P, R, 2], F32)
        rs, nb_ = sb("rs", [P, R], F32), sb("nb", [P, R], F32)
        var_eps, nmean = sb("var_eps", [P, R], F32), sb("nmean", [P, R], F32)
        tmp, tmp2 = sb("tmp", [P, 2], F32), sb("tmp2", [P, 1], F32)
        ag, ag2 = sb("ag", [P, AG], F32), sb("ag2", [P, AG], F32)
        nmax = sb("nmax", [P, 1], F32)
        probs = sb("probs", [P, EXPERTS], F32)
        top, top_i = sb("top", [P, 8], F32), sb("top_i", [P, 8], U32)
        top_f = sb("top_f", [P, 2], F32)
        pair, wtop = sb("pair", [P, 1], F32), sb("wtop", [P, 2], F32)
        dense, dense2 = sb("dense", [P, EXPERTS], F32), sb("dense2", [P, EXPERTS], F32)
        h, h_rest = sb("h", [P, ER], F32), sb("h_rest", [P, ER], F32)
        h_parts = sb("h_parts", [P, 4, ER], BF16)
        h_t = sb("h_t", [P, 2, P], BF16)
        ident, ident16 = consts["ident"], consts["ident_bf16"]
        expert_ids, columns = consts["expert_ids"], consts["columns"]
        w_scale, w_iscale = consts["w_scale"], consts["w_iscale"]

        def pb(name, shape, dt):
            return st.enter_context(nc.psum_tensor(f"{name}_f", shape, dt))

        ps_y = [pb(f"ps_y{j}", [P, BANK], F32) for j in range(NBANK)]
        ps_a, ps_h = pb("ps_a", [P, BANK], F32), pb("ps_h", [P, 2, BANK], BF16)
        ps_t = [pb(f"ps_t{i}", [P, BANK], F32) for i in range(2)]

        w_loaded = [sem(f"w_loaded{i}") for i in range(2)]
        w_hi_done, w_split = sem("w_hi_done"), sem("w_split")
        ag_loaded, ag_squared, ag_summed, ag_scaled = sem("ag_loaded"), sem("ag_squared"), sem("ag_summed"), sem("ag_scaled")
        ag_hi_done, ag_split = sem("ag_hi_done"), sem("ag_split")
        b_loaded, b_hi_done, b_split = sem("b_loaded"), sem("b_hi_done"), sem("b_split")
        x_loaded = [sem(f"x_loaded{i}") for i in range(2)]
        stored = [sem(f"stored{i}") for i in range(2)]
        t_filled, hi_done, t_free = sem("t_filled"), sem("hi_done"), sem("t_free")
        a_done, a_read, nmax_ready, exp_done, h_ready = sem("a_done"), sem("a_read"), sem("nmax_ready"), sem("exp_done"), sem("h_ready")
        ht_done, ht_copied = sem("ht_done"), sem("ht_copied")
        bank_done, evacuated = sem("bank_done"), sem("evacuated")
        mv_ready, ln_ready, out_ready, dve_step, pool_step = sem("mv_ready"), sem("ln_ready"), sem("out_ready"), sem("dve_step"), sem("pool_step")

        def tiles(eng, slot, chain, links):
            for t in (-1, 0, 1):
                slot(t, t // 2, t % 2)
                if chain:
                    chain.mark()
            start = chain.base - 2 * links if chain else 0
            with eng.Fori(1, (NT - 2) // 2) as m:
                for parity in range(2):
                    t = 2 * m + parity
                    if chain:
                        chain.base, chain.count = t * links + start, 0
                    slot(t, m, parity)
                    if chain:
                        assert chain.count == links, (chain.count, links)
            if chain:
                chain.base, chain.count = start + (NT - 2) * links, 0
            for t in (NT - 2, NT - 1):
                slot(t, t // 2, t % 2)

        def first(t):
            return isinstance(t, int) and t == 0

        def chunk_at(c):
            k = KC * (c % (CHUNKS // NBANK))
            j = c // (CHUNKS // NBANK)
            return slice(None), slice(k, k + KC), slice(j * BANK, (j + 1) * BANK)

        with nc.Block() as block:
            @block.sync
            def _(sp):
                def load(t, half, parity):
                    if is_batch(t, NT):
                        after(sp, evacuated, NBANK * (t - 1))
                        sp.dma_start(xn[parity][:], x2[bass.ds(t * P, P), :]).then_inc(x_loaded[parity], 16)

                def slot(t, half, parity):
                    if isinstance(t, int) and t == -1:
                        sp.dma_start(ag_raw, ag_in).then_inc(ag_loaded, 16)
                        load(0, 0, 0)
                        for c in range(CHUNKS):
                            after(sp, w_split, c - 1)
                            sp.dma_start(chunk[c % 2].rearrange("p k c -> p (k c)"), w_chunks[c]).then_inc(w_loaded[c % 2], 16)
                            if c == 1:
                                sp.wait_ge(ag_split, 2)
                                for i in range(2):
                                    sp.dma_start(b_raw[i * ER:(i + 1) * ER, :], b_rows).then_inc(b_loaded, 16)
                            if c == 3:
                                load(1, 0, 1)
                        return
                    load(t + 2, half + 1, parity)
                    sp.wait_ge(out_ready, t + 1)
                    sp.dma_start(out[bass.ds(t * P, P), :], y[parity][:]).then_inc(stored[parity], 16)

                tiles(sp, slot, None, 0)
                for i in range(2):
                    sp.wait_ge(stored[i], 16 * (NT // 2))

            @block.gpsimd
            def _(pool):
                g = nc.gpsimd
                chain = Chain(nc, pool, pool_step, consts["pad"])

                def slot(t, half, parity):
                    if not is_batch(t, NT):
                        pool.wait_ge(ag_squared, 2)
                        g.partition_all_reduce(ag_total[:], ag_sumsq[:], P, bass.bass_isa.ReduceOp.add).then_inc(ag_summed, 1)
                        return
                    pool.wait_ge(mv_ready, t + 1)
                    after(pool, out_ready, t)
                    g.tensor_tensor(var_eps[:, 0:1], mv[:, 0, 1:2], columns[:, EPS_AT, 0:1], ALU.add)
                    chain.link(g.tensor_tensor(nmean[:, 0:1], mv[:, 0, 0:1], columns[:, MINUS_ONE, 0:1], ALU.mult))
                    chain.link(g.tensor_tensor(rs[:, 0:1], var_eps[:, 0:1], columns[:, MINUS_HALF, 0:1], ALU.pow))
                    g.tensor_tensor(nb_[:, 0:1], nmean[:, 0:1], rs[:, 0:1], ALU.mult).then_inc(ln_ready, 1)

                tiles(pool, slot, chain, 2)

            @block.scalar
            def _(act):
                def chunk_hi(c):
                    act.wait_ge(w_loaded[c % 2], 16 * (c // 2 + 1))
                    nc.scalar.activation(w_hi[chunk_at(c)], chunk[c % 2], ACT.Copy, scale=w_scale[:]).then_inc(w_hi_done, 1)

                def slot(t, half, parity):
                    cur, nxt = is_batch(t, NT), is_batch(t + 1, NT)
                    if not cur:
                        act.wait_ge(ag_loaded, 16)
                        for i, cols in enumerate((slice(0, ER), slice(ER, AG))):
                            nc.scalar.activation(x_lo[1][:, :, cols], ag_raw[:, :, cols], ACT.Square,
                                                 accum_out=ag_sumsq[:, i:i + 1]).then_inc(ag_squared, 1)
                    if cur:
                        act.wait_ge(nmax_ready, t + 1)
                        nc.scalar.activation(probs[:], ag[:, ER:AG], ACT.Exp, bias=nmax[:]).then_inc(exp_done, 1)
                        if first(t):
                            for c in range(4, 8):
                                chunk_hi(c)
                        act.wait_ge(ht_done, t + 1)
                        nc.scalar.activation(h_t[:], ps_h[:, :, 0:P], ACT.Copy).then_inc(ht_copied, 1)
                        if first(t):
                            for c in range(8, CHUNKS):
                                chunk_hi(c)
                    if nxt:
                        for q in range(4):
                            act.wait_ge(t_filled, 4 * (t + 1) + q + 1)
                            nc.scalar.activation(x_hi[1 - parity][:, 4 * q:4 * q + 4, :],
                                                 ps_t[q % 2][:].rearrange("p (k c) -> p k c", k=4), ACT.Copy).then_inc(hi_done, 1)
                    if not cur:
                        act.wait_ge(ag_scaled, 1)
                        for i, cols in enumerate((slice(0, ER), slice(ER, AG))):
                            nc.scalar.activation(ag_t[:, :, cols], ag_raw[:, :, cols], ACT.Copy, scale=ag_scale[:, i:i + 1]).then_inc(ag_hi_done, 1)
                        chunk_hi(0)
                        chunk_hi(1)
                        act.wait_ge(b_loaded, 32)
                        nc.scalar.activation(b_stack[:, 0], b_raw[:], ACT.Copy, scale=w_scale[:]).then_inc(b_hi_done, 1)
                        nc.scalar.activation(b_stack[0:ER, 1], b_raw[0:ER, :], ACT.Copy, scale=w_scale[0:ER, :]).then_inc(b_hi_done, 1)
                        chunk_hi(2)
                        chunk_hi(3)
                    if cur:
                        act.wait_ge(ln_ready, t + 1)
                        nc.scalar.activation(y[parity][:], y[parity][:], ACT.Identity, bias=nb_[:, 0:1], scale=rs[:, 0:1]).then_inc(out_ready, 1)

                tiles(act, slot, None, 0)

            @block.vector
            def _(dve):
                v = nc.vector
                chain = Chain(nc, dve, dve_step, consts["pad"])

                def chunk_lo(c):
                    dve.wait_ge(w_hi_done, c + 1)
                    v.scalar_tensor_tensor(w_lo[chunk_at(c)], chunk[c % 2], w_scale[:], w_hi[chunk_at(c)], ALU.mult,
                                           ALU.subtract).then_inc(w_split, 1)

                def slot(t, half, parity):
                    cur, nxt = is_batch(t, NT), is_batch(t + 1, NT)

                    def bank_out(j):
                        if j == 0:
                            after(dve, stored[parity], 16 * half)
                        dve.wait_ge(bank_done, NBANK * t + j + 1)
                        at = slice(j * BANK, (j + 1) * BANK)
                        v.scalar_tensor_tensor(y[parity][:, at], ps_y[j][:], w_iscale[:], xn[parity][:, at], ALU.mult,
                                               ALU.add).then_inc(evacuated, 1)

                    def low_half(q):
                        if nxt:
                            dve.wait_ge(hi_done, 4 * (t + 1) + q + 1)
                            v.tensor_tensor(x_lo[1 - parity][:, 4 * q:4 * q + 4, :], ps_t[q % 2][:].rearrange("p (k c) -> p k c", k=4),
                                            x_hi[1 - parity][:, 4 * q:4 * q + 4, :], ALU.subtract).then_inc(t_free, 1)

                    def bank_stats(j):
                        dve.wait_ge(evacuated, NBANK * t + j + 1)
                        return v.bn_stats(stats[:, j], y[parity][:, j * BANK:(j + 1) * BANK])

                    if not cur:
                        dve.wait_ge(ag_summed, 1)
                        scale_steps(nc, chain, ag_scale[:], ag_iscale[:], ag_total[:], tmp[:])
                        v.memset(nmax[:], 0.0).then_inc(ag_scaled, 1)
                        for q in range(4):
                            low_half(q)
                        for i, cols in enumerate((slice(0, ER), slice(ER, AG))):
                            dve.wait_ge(ag_hi_done, i + 1)
                            v.scalar_tensor_tensor(ag_t[:, :, AG + cols.start:AG + cols.stop], ag_raw[:, :, cols], ag_scale[:, i:i + 1],
                                                   ag_t[:, :, cols], ALU.mult, ALU.subtract).then_inc(ag_split, 1)
                        chunk_lo(0)
                        chunk_lo(1)
                        dve.wait_ge(b_hi_done, 2)
                        v.scalar_tensor_tensor(b_stack[ER:P, 1], b_raw[ER:P, :], w_scale[ER:P, :], b_stack[ER:P, 0], ALU.mult,
                                               ALU.subtract).then_inc(b_split, 1)
                        chunk_lo(2)
                        chunk_lo(3)
                        return
                    dve.wait_ge(a_done, t + 1)
                    chain.link(v.tensor_copy(ag2[:], ps_a[:, AG:2 * AG]))
                    v.tensor_tensor(ag[:], ps_a[:, 0:AG], ag2[:], ALU.add).then_inc(a_read, 1)
                    dve.wait_ge(a_read, t + 1)
                    v.tensor_scalar(ag[:, 0:ER], ag[:, 0:ER], ag_iscale[:, 0:1], None, ALU.mult)
                    chain.link(v.tensor_scalar(ag[:, ER:AG], ag[:, ER:AG], ag_iscale[:, 1:2], None, ALU.mult))
                    chain.link(v.tensor_reduce(tmp2[:], ag[:, ER:AG], AX.X, ALU.max))
                    v.tensor_scalar(nmax[:], tmp2[:], -1.0, None, ALU.mult).then_inc(nmax_ready, 1)
                    dve.wait_ge(exp_done, t + 1)
                    chain.settle()
                    chain.link(v.max(top[:], probs[:]))
                    chain.settle()
                    chain.link(v.max_index(top_i[:], top[:], probs[:]))
                    v.tensor_tensor(pair[:], top[:, 0:1], top[:, 1:2], ALU.add)
                    chain.link(v.tensor_copy(top_f[:], top_i[:, 0:2]))
                    chain.link(v.reciprocal(pair[:], pair[:]))
                    chain.link(v.tensor_scalar(wtop[:], top[:, 0:2], pair[:], 2.0, ALU.mult, ALU.mult))
                    v.tensor_scalar(dense[:], expert_ids[:], top_f[:, 0:1], wtop[:, 0:1], ALU.is_equal, ALU.mult)
                    chain.link(v.tensor_scalar(dense2[:], expert_ids[:], top_f[:, 1:2], wtop[:, 1:2], ALU.is_equal, ALU.mult))
                    chain.link(v.tensor_tensor(dense[:], dense[:], dense2[:], ALU.add))
                    chain.link(v.tensor_tensor(h[:].rearrange("p (e r) -> p e r", e=EXPERTS), ag[:, 0:ER].rearrange("p (e r) -> p e r", e=EXPERTS),
                                               dense[:].unsqueeze(2).to_broadcast([P, EXPERTS, RANK]), ALU.mult))
                    after(dve, ht_done, t)
                    chain.link(v.tensor_copy(h_parts[:, 0], h[:]))
                    chain.link(v.tensor_tensor(h_rest[:], h[:], h_parts[:, 0], ALU.subtract))
                    v.tensor_copy(h_parts[:, 3], h_parts[:, 0])
                    chain.link(v.tensor_copy(h_parts[:, 1], h_rest[:]))
                    v.tensor_tensor(h_parts[:, 2], h_rest[:], h_parts[:, 1], ALU.subtract).then_inc(h_ready, 1)
                    if first(t):
                        for c in range(4, CHUNKS):
                            chunk_lo(c)
                    bank_out(0)
                    bank_out(1)
                    bank_stats(0)
                    low_half(0)
                    low_half(1)
                    bank_stats(1)
                    bank_out(2)
                    low_half(2)
                    low_half(3)
                    bank_stats(2)
                    bank_out(3)
                    chain.link(bank_stats(3))
                    after(dve, ln_ready, t)
                    chain.settle()
                    v.bn_aggr(mv[:, 0], stats[:].rearrange("p a b -> p (a b)")).then_inc(mv_ready, 1)

                tiles(dve, slot, chain, 15)

            @block.tensor
            def _(pe):
                def slot(t, half, parity):
                    cur, nxt = is_batch(t, NT), is_batch(t + 1, NT)
                    other = 1 - parity

                    def transposed_bank(q):
                        if nxt:
                            if q == 0:
                                pe.wait_ge(x_loaded[other], 16 * (half + parity + 1))
                            after(pe, t_free, 4 * (t + 1) + q - 1)
                            for i in range(4):
                                k = 4 * q + i
                                ins = nc.tensor.transpose(ps_t[q % 2][:, i * P:(i + 1) * P], xn[other][:, k * P:(k + 1) * P], ident[:])
                            ins.then_inc(t_filled, 1)

                    if not cur:
                        for q in range(4):
                            transposed_bank(q)
                        return

                    def main(j):
                        after(pe, evacuated, NBANK * (t - 1) + j + 1)
                        for k in range(KT):
                            if first(t) and k % KC == 0:
                                pe.wait_ge(w_split, j * (CHUNKS // NBANK) + k // KC + 1)
                            for xx, ww in ((x_hi, w_hi), (x_hi, w_lo), (x_lo, w_hi)):
                                nc.tensor.matmul(ps_y[j][:], xx[parity][:, k], ww[:, k, j * BANK:(j + 1) * BANK],
                                                 start=(k == 0 and xx is x_hi and ww is w_hi), stop=False)

                    def lora(j):
                        nc.tensor.matmul(ps_y[j][:], h_t[:, 0], b_stack[:, 0, j * BANK:(j + 1) * BANK], start=False, stop=False)
                        nc.tensor.matmul(ps_y[j][:], h_t[:, 1], b_stack[:, 1, j * BANK:(j + 1) * BANK], start=False,
                                         stop=True).then_inc(bank_done, 1)

                    pe.wait_ge(t_free, 4 * (t + 1))
                    after(pe, a_read, t)
                    if first(t):
                        pe.wait_ge(ag_split, 2)
                    for k in range(KT):
                        nc.tensor.matmul(ps_a[:, 0:2 * AG], x_hi[parity][:, k], ag_t[:, k, :], start=(k == 0), stop=False)
                        ins = nc.tensor.matmul(ps_a[:, 0:AG], x_lo[parity][:, k], ag_t[:, k, 0:AG], start=False, stop=(k == KT - 1))
                    ins.then_inc(a_done, 1)
                    main(0)
                    pe.wait_ge(h_ready, t + 1)
                    after(pe, ht_copied, t)
                    for i in range(2):
                        ins = nc.tensor.transpose(ps_h[:, i, 0:P], h_parts[:, 2 * i:2 * i + 2].rearrange("p a b -> p (a b)"), ident16[:])
                    ins.then_inc(ht_done, 1)
                    main(1)
                    if first(t):
                        pe.wait_ge(b_split, 1)
                    pe.wait_ge(ht_copied, t + 1)
                    lora(0)
                    lora(1)
                    transposed_bank(0)
                    transposed_bank(1)
                    main(2)
                    lora(2)
                    transposed_bank(2)
                    transposed_bank(3)
                    main(3)
                    lora(3)

                tiles(pe, slot, None, 0)


def setup(nc, consts):
    with ExitStack() as st:
        loaded, made = st.enter_context(nc.semaphore("ident_loaded")), st.enter_context(nc.semaphore("ident_made"))
        with nc.Block() as block:
            @block.sync
            def _(sp):
                sp.dma_start(consts["ident"][:], consts["ident_dram"]).then_inc(loaded, 16)
                sp.dma_start(consts["expert_ids"][:], consts["expert_dram"]).then_inc(loaded, 16)

            @block.vector
            def _(dve):
                for at, value in ((EPS4_AT, EPS / 4), (EPS_AT, EPS), (MINUS_ONE, -1.0), (MINUS_HALF, -0.5)):
                    nc.vector.memset(consts["columns"][:, at], value)
                dve.wait_ge(loaded, 32)
                nc.vector.tensor_copy(consts["ident_bf16"][:], consts["ident"][:]).then_inc(made, 1)
                dve.wait_ge(made, 1)


def autocorrelation(nc, x, z, forward_dram, inverse_dram, consts):
    nb = x.shape[0] // C
    TOP = 7
    BITS = L.bit_length() - 1
    with ExitStack() as st:
        def sb(name, shape, dt):
            return st.enter_context(nc.sbuf_tensor(f"{name}_c", shape, dt))

        def sem(name):
            return st.enter_context(nc.semaphore(f"{name}_c"))

        rows = sb("rows", [P, R, L], F32)
        x_t = sb("x_t", [P, KT, C], F32)
        table = [sb(f"table{i}", [P, KT, P], F32) for i in range(2)]
        lags = sb("lags", [P, KT, BANK], F32)
        power = sb("power", [P, KT, C], F32)
        corr = sb("corr", [P, R, L], F32)
        turn = [sb(f"turn{i}", [P, 2 * L], F32) for i in range(2)]
        acc = sb("acc", [P, L], F32)
        top, top_i = sb("top", [P, 8], F32), sb("top_i", [P, 8], U32)
        bit_u, bit, nbit = sb("bit_u", [P, BITS, 8], U32), sb("bit", [P, BITS, 8], F32), sb("nbit", [P, BITS, 8], F32)
        ntop, total, weight = sb("ntop", [P, 1], F32), sb("total", [P, 1], F32), sb("weight", [P, 8], F32)
        ident = consts["ident"]
        ps_t = [st.enter_context(nc.psum_tensor(f"ps_t{i}_c", [P, BANK], F32)) for i in range(2)]
        ps_f = [st.enter_context(nc.psum_tensor(f"ps_f{i}_c", [P, BANK], F32)) for i in range(2)]
        ps_c = [st.enter_context(nc.psum_tensor(f"ps_c{i}_c", [P, BANK], F32)) for i in range(2)]

        x_loaded, lags_loaded = sem("x_loaded"), sem("lags_loaded")
        table_loaded = [sem(f"table_loaded{i}") for i in range(2)]
        stored = sem("stored")
        t_filled, t_copied, fwd_done, squared = sem("t_filled"), sem("t_copied"), sem("fwd_done"), sem("squared")
        corr_done, corr_copied, ntop_ready, exp_done = sem("corr_done"), sem("corr_copied"), sem("ntop_ready"), sem("exp_done")
        z_ready, dve_step = sem("z_ready"), sem("dve_step")
        NBNK = R * NBANK

        def every_batch(eng, batch):
            batch(0)
            with eng.Fori(1, nb) as n:
                batch(n)

        with nc.Block() as block:
            @block.sync
            def _(sp):
                def batch(n):
                    after(sp, z_ready, R * n)
                    sp.dma_start(rows[:], x[bass.ds(n * C, C), :].rearrange("(r p) l -> p r l", p=P)).then_inc(x_loaded, 16)
                    for m in range(KT):
                        after(sp, fwd_done, KT * n + max(m - 1, 0))
                        sp.dma_start(table[m % 2][:], forward_dram[m]).then_inc(table_loaded[m % 2], 16)
                    for c in range(NBANK):
                        after(sp, corr_done, NBNK * n + R * c)
                        sp.dma_start(lags[:], inverse_dram[c]).then_inc(lags_loaded, 16)
                    for r in range(R):
                        sp.wait_ge(z_ready, R * n + r + 1)
                        sp.dma_start(z[bass.ds(n * C + r * P, P), :], acc[:]).then_inc(stored, 16)

                every_batch(sp, batch)
                sp.wait_ge(stored, 16 * R * nb)

            @block.gpsimd
            def _(pool):
                pool.wait_ge(z_ready, 1)

            @block.tensor
            def _(pe):
                def batch(n):
                    pe.wait_ge(x_loaded, 16 * (n + 1))
                    for q in range(NBNK):
                        after(pe, t_copied, NBNK * n + max(q - 1, 0))
                        for i in range(4):
                            k = 4 * (q % 4) + i
                            ins = nc.tensor.transpose(ps_t[q % 2][:, i * P:(i + 1) * P], rows[:, q // 4, k * P:(k + 1) * P], ident[:])
                        ins.then_inc(t_filled, 1)
                    pe.wait_ge(t_copied, NBNK * (n + 1))
                    for m in range(KT):
                        pe.wait_ge(table_loaded[m % 2], 16 * (KT // 2 * n + m // 2 + 1))
                        after(pe, squared, KT * n + max(m - 1, 0))
                        for k in range(KT):
                            ins = nc.tensor.matmul(ps_f[m % 2][:, 0:C], table[m % 2][:, k, :], x_t[:, k, :], start=(k == 0), stop=(k == KT - 1))
                        ins.then_inc(fwd_done, 1)
                    pe.wait_ge(squared, KT * (n + 1))
                    for c in range(NBANK):
                        pe.wait_ge(lags_loaded, 16 * (NBANK * n + c + 1))
                        for r in range(R):
                            after(pe, corr_copied, NBNK * n + max(R * c + r - 1, 0))
                            for m in range(KT):
                                ins = nc.tensor.matmul(ps_c[r][:], power[:, m, r * P:(r + 1) * P], lags[:, m, :], start=(m == 0), stop=(m == KT - 1))
                            ins.then_inc(corr_done, 1)

                every_batch(pe, batch)

            @block.scalar
            def _(act):
                def batch(n):
                    for q in range(NBNK):
                        act.wait_ge(t_filled, NBNK * n + q + 1)
                        r, kk = q // 4, 4 * (q % 4)
                        nc.scalar.activation(x_t[:, kk:kk + 4, r * P:(r + 1) * P], ps_t[q % 2][:].rearrange("p (k c) -> p k c", k=4),
                                             ACT.Copy).then_inc(t_copied, 1)
                    for m in range(KT):
                        act.wait_ge(fwd_done, KT * n + m + 1)
                        nc.scalar.activation(power[:, m], ps_f[m % 2][:, 0:C], ACT.Square).then_inc(squared, 1)
                    after(act, z_ready, R * n)
                    for c in range(NBANK):
                        for r in range(R):
                            act.wait_ge(corr_done, NBNK * n + R * c + r + 1)
                            nc.scalar.activation(corr[:, r, c * BANK:(c + 1) * BANK], ps_c[r][:], ACT.Copy).then_inc(corr_copied, 1)
                    for r in range(R):
                        act.wait_ge(ntop_ready, R * n + r + 1)
                        nc.scalar.activation(weight[:, 0:TOP], top[:, 0:TOP], ACT.Exp, bias=ntop[:], accum_out=total[:]).then_inc(exp_done, 1)

                every_batch(act, batch)

            @block.vector
            def _(dve):
                v = nc.vector
                chain = Chain(nc, dve, dve_step, consts["pad"])
                HEAD, LAG = 8, 2 * BITS + 3
                def batch(n):
                    for r in range(R):
                        chain.base, chain.count = (n * R + r) * (HEAD + TOP * LAG), 0
                        if r == 0:
                            dve.wait_ge(corr_copied, NBNK * (n + 1))
                        chain.settle()
                        chain.link(v.max(top[:], corr[:, r]))
                        chain.settle()
                        chain.link(v.max_index(top_i[:], top[:], corr[:, r]))
                        v.tensor_scalar(ntop[:], top[:, 0:1], -1.0, None, ALU.mult).then_inc(ntop_ready, 1)
                        for b in range(BITS):
                            ins = v.tensor_scalar(bit_u[:, b], top_i[:], b, 1, ALU.logical_shift_right, ALU.bitwise_and)
                        chain.link(ins)
                        chain.link(v.tensor_copy(bit[:], bit_u[:]))
                        chain.link(v.tensor_scalar(nbit[:], bit[:], -1.0, 1.0, ALU.mult, ALU.add))
                        dve.wait_ge(exp_done, R * n + r + 1)
                        chain.link(v.reciprocal(total[:], total[:]))
                        chain.link(v.tensor_scalar(weight[:, 0:TOP], weight[:, 0:TOP], total[:], None, ALU.mult))
                        after(dve, stored, 16 * (R * n + r))
                        chain.link(v.tensor_copy(acc[:], rows[:, r]))
                        assert chain.count == HEAD, chain.count
                        chain.settle()
                        with dve.Fori(0, TOP) as lag:
                            chain.base, chain.count = (n * R + r) * (HEAD + TOP * LAG) + HEAD + lag * LAG, 0
                            v.tensor_copy(turn[0][:, 0:L], rows[:, r])
                            chain.link(v.tensor_copy(turn[0][:, L:2 * L], rows[:, r]))
                            for i in range(BITS):
                                b = BITS - 1 - i
                                step, width = 1 << b, L + (1 << b) - 1
                                a, c = turn[i % 2], turn[1 - i % 2]
                                chain.link(v.tensor_scalar(c[:, 0:width], a[:, step:step + width], bit[:, b, bass.ds(lag, 1)], None, ALU.mult))
                                chain.link(v.scalar_tensor_tensor(c[:, 0:width], a[:, 0:width], nbit[:, b, bass.ds(lag, 1)],
                                                                  c[:, 0:width], ALU.mult, ALU.add))
                            chain.link(v.scalar_tensor_tensor(acc[:], turn[BITS % 2][:, 0:L], weight[:, bass.ds(lag, 1)], acc[:],
                                                              ALU.mult, ALU.add))
                            chain.link(v.tensor_copy(ntop[:], total[:]))
                            assert chain.count == LAG, chain.count
                        v.tensor_copy(ntop[:], total[:]).then_inc(z_ready, 1)

                every_batch(dve, batch)


def correlation_tables():
    j = np.arange(L, dtype=np.int64)
    cosine = np.cos(2 * np.pi * np.minimum(j, L - j) / L)
    sine = np.sin(2 * np.pi * j / L)
    freq = np.concatenate([np.arange(L // 2 + 1), np.arange(1, L // 2)]).astype(np.int64)
    is_sine = j > L // 2
    phase = (j[:, None] * freq[None, :]) % L
    fwd = np.where(is_sine[None, :], sine[phase], cosine[phase]) / np.sqrt(L / 2)
    once = (freq == 0) | (freq == L // 2)
    inv = cosine[phase.T] * np.where(once, 0.5, 1.0)[:, None]
    fwd = fwd.reshape(KT, P, KT, P).transpose(2, 1, 0, 3)
    inv = inv.reshape(KT, P, NBANK, BANK).transpose(2, 1, 0, 3)
    return np.ascontiguousarray(fwd, np.float32), np.ascontiguousarray(inv, np.float32)


def guard_flag(nc, consts, flag):
    with ExitStack() as st:
        def sb(name, shape):
            return st.enter_context(nc.sbuf_tensor(name, shape, F32))

        n = consts["g_lags"].shape[1]
        bound, most, most_all = sb("bound", [P, n]), sb("most", [P, 1]), sb("most_all", [P, 1])
        found, reduced, step = [st.enter_context(nc.semaphore(x)) for x in ("most_found", "reduced", "flag_step")]
        with nc.Block() as block:
            @block.gpsimd
            def _(pool):
                pool.wait_ge(found, 1)
                nc.gpsimd.partition_all_reduce(most_all[:], most[:], P, bass.bass_isa.ReduceOp.max).then_inc(reduced, 1)

            @block.vector
            def _(dve):
                nc.vector.scalar_tensor_tensor(bound[:], consts["g_energy"][:], L / 32.0, consts["g_lags"][:], ALU.mult,
                                               ALU.add).then_inc(step, 1)
                dve.wait_ge(step, 1)
                nc.vector.tensor_reduce(most[:], bound[:], AX.X, ALU.max).then_inc(found, 1)
                dve.wait_ge(reduced, 1)
                nc.vector.tensor_scalar(flag[:], most_all[:], -GUARD_GAP, None, ALU.is_gt).then_inc(step, 1)
                dve.wait_ge(step, 2)


def decoder_layer(nc, x, ctx_in, w_chunks, ag_in, b_rows, fwd_dram, inv_dram, ident_dram, expert_dram, forward_dram,
                  inverse_dram, out):
    rows = x.shape[0]
    x2 = nc.dram_tensor("x2_scratch", (rows, L), F32, kind="Internal").ap()
    z = nc.dram_tensor("z_scratch", (rows, L), F32, kind="Internal").ap()
    w_rows = w_chunks.rearrange("c p o -> (c p) o")
    with ExitStack() as st:
        def sb(name, shape, dt):
            return st.enter_context(nc.sbuf_tensor(name, shape, dt))

        consts = dict(
            ident=sb("ident", [P, P], F32), ident_bf16=sb("ident_bf16", [P, P], BF16),
            columns=sb("columns", [P, 4, R], F32), pad=sb("pad", [P, 1], F32), expert_ids=sb("expert_ids", [P, EXPERTS], F32),
            g_lags=sb("g_lags", [P, rows // P], F32), g_energy=sb("g_energy", [P, rows // P], F32),
            w_scale=sb("w_scale", [P, 1], F32), w_iscale=sb("w_iscale", [P, 1], F32),
            fwd_dram=fwd_dram, inv_dram=inv_dram, ident_dram=ident_dram, expert_dram=expert_dram)
        flag = sb("flag", [P, 1], I32)
        setup(nc, consts)
        attention_pass(nc, x, ctx_in, x2, w_rows, b_rows, consts, EPS4_AT, "fast")
        guard_flag(nc, consts, flag)
        some_row_needs_it = nc.values_load(flag[0:1, 0:1], min_val=0, max_val=1)
        with nc.If(some_row_needs_it):
            autocorrelation(nc, x, z, forward_dram, inverse_dram, consts)
            attention_pass(nc, z, ctx_in, x2, w_rows, b_rows, consts, EPS_AT, "full")
        feed_forward(nc, x2, out, w_chunks, b_rows, ag_in, consts)


def kernel(x, ctx_4096, L0_ffn_W_base, L0_ffn_gate_W, L0_ffn_A, L0_ffn_B):
    import ml_dtypes
    import concourse.bacc as bacc
    from concourse.bass_utils import run_bass_kernel_spmd

    shape = x.shape
    fwd, inv = guard_tables()
    forward, inverse = correlation_tables()
    arrays = {
        "x": np.ascontiguousarray(x).reshape(-1, L),
        "ctx_in": np.ascontiguousarray(ctx_4096).reshape(-1, L),
        "w_chunks": np.ascontiguousarray(
            L0_ffn_W_base.reshape(NBANK, BANK, KT // 4, 4, P).transpose(0, 2, 4, 3, 1)).reshape(KT, P, L),
        "ag_in": np.ascontiguousarray(
            np.concatenate([L0_ffn_A.reshape(ER, L), L0_ffn_gate_W]).reshape(AG, KT, P).transpose(2, 1, 0)),
        "b_rows": np.ascontiguousarray(np.transpose(L0_ffn_B, (0, 2, 1))).reshape(ER, L),
        "fwd_dram": fwd.astype(ml_dtypes.bfloat16),
        "inv_dram": inv.astype(ml_dtypes.bfloat16),
        "forward_dram": forward,
        "inverse_dram": inverse,
        "ident_dram": np.eye(P, dtype=np.float32),
        "expert_dram": np.tile(np.arange(EXPERTS, dtype=np.float32), (P, 1)),
    }
    nc = bacc.Bacc("TRN2", target_bir_lowering=False, num_devices=1)
    aps = {n: nc.dram_tensor(n, a.shape, mybir.dt.from_np(a.dtype), kind="ExternalInput").ap() for n, a in arrays.items()}
    out = nc.dram_tensor("out", arrays["x"].shape, F32, kind="ExternalOutput").ap()
    decoder_layer(nc, out=out, **aps)
    r = run_bass_kernel_spmd(nc, [arrays], core_ids=[0])
    return r.results[0]["out"].reshape(shape)
```

```python
from contextlib import ExitStack

import numpy as np

import concourse.bass as bass
from concourse import mybir

F32 = mybir.dt.float32
F16 = mybir.dt.float16
BF16 = mybir.dt.bfloat16
I32 = mybir.dt.int32
U32 = mybir.dt.uint32
ALU = mybir.AluOpType
ACT = mybir.ActivationFunctionType
AX = mybir.AxisListType

P = 128
L = 2048
C = 256
R = C // P
KT = L // P
BANK = 512
NBANK = L // BANK
EPS = 1e-5
EXPERTS, RANK = 8, 8
ER = EXPERTS * RANK
AG = ER + EXPERTS
EPS4_AT, EPS_AT, MINUS_ONE, MINUS_HALF = range(4)
GUARD_GAP = 110.0
PAIRS = 256
HALF = L // 2
KC = 2
PREFETCHED = 3


def after(eng, sem, value):
    if isinstance(value, int) and value <= 0:
        return
    eng.wait_ge(sem, value)


class Chain:

    def __init__(self, nc, eng, sem, pad):
        self.eng, self.sem, self.base, self.count = eng, sem, 0, 0
        self.pad_memset, self.pad = nc.vector.memset, pad[:]

    def link(self, instruction):
        self.count += 1
        instruction.then_inc(self.sem, 1)
        self.eng.wait_ge(self.sem, self.base + self.count)

    def settle(self):
        self.pad_memset(self.pad, 0.0)

    def mark(self):
        done, self.count = self.count, 0
        self.base = self.base + done
        return done


def batch_slots(eng, chain, nb, slot, links):
    for n in (-2, -1, 0, 1):
        slot(n, n // 2, n % 2)
        if chain:
            chain.mark()
    if nb > 4:
        start = chain.base - 2 * links if chain else 0
        with eng.Fori(1, (nb - 2) // 2) as m:
            for parity in range(2):
                n = 2 * m + parity
                if chain:
                    chain.base, chain.count = n * links + start, 0
                slot(n, m, parity)
                if chain:
                    assert chain.count == links, (chain.count, links)
        if chain:
            chain.base, chain.count = start + (nb - 2) * links, 0
    for n in (nb - 2, nb - 1):
        slot(n, n // 2, n % 2)
        if chain:
            chain.mark()


def is_batch(n, nb):
    return not isinstance(n, int) or 0 <= n < nb


def scale_steps(nc, chain, scale, inverse, total, tmp):
    v = nc.vector
    chain.link(v.tensor_scalar(tmp.bitcast(U32), total.bitcast(U32), 24, None, ALU.logical_shift_right))
    v.tensor_scalar(scale.bitcast(I32), tmp.bitcast(I32), -float(1 << 23), float(204 << 23), ALU.mult, ALU.add)
    chain.link(v.tensor_scalar(inverse.bitcast(I32), tmp.bitcast(I32), float(1 << 23), float(50 << 23), ALU.mult, ALU.add))


def chunk_rows(w_chunks, c):
    at = c * KC * BANK
    return w_chunks[at // L, :, at % L:at % L + KC * BANK]


def wait_stored(eng, stored, nb):
    for per_tile in stored:
        for sem in per_tile:
            eng.wait_ge(sem, 16 * (nb // 2))


def attention_pass(nc, src, ctx_in, x2_out, w_chunks, b_rows, ag_in, consts, stored, eps_column, tag):
    nb = src.shape[0] // C
    w_rows = w_chunks.rearrange("c p o -> (c p) o")
    PIECES = 2 * R
    with ExitStack() as st:
        def sb(name, shape, dt):
            return st.enter_context(nc.sbuf_tensor(f"{name}_{tag}", shape, dt))

        def sem(name):
            return st.enter_context(nc.semaphore(f"{name}_{tag}"))

        x2buf = [sb(f"x2buf{i}", [P, R, L], F32) for i in (1, 0)][::-1]
        xbuf = [sb(f"xbuf{i}", [P, R, L], F32) for i in range(2)]
        cbuf = sb("cbuf", [P, R, L], F32)
        v_hi = [sb(f"v_hi{i}", [P, R, L], F16) for i in range(2)]
        v_lo = [sb(f"v_lo{i}", [P, R, L], F16) for i in range(2)]
        q_hi, q_lo = sb("q_hi", [P, KT, C], F16), sb("q_lo", [P, KT, C], F16)
        k_both = sb("k_both", [P, KT, 2, C], F16)
        p_hi, p_lo = sb("p_hi", [P, R, C], F16), sb("p_lo", [P, R, C], F16)
        expd = sb("expd", [P, R, C], F32)
        u_rows = sb("u_rows", [P, R, HALF], BF16)
        u_t = sb("u_t", [P, HALF // P, C], BF16)
        power = sb("power", [P, 4, C], BF16)
        fwd = sb("fwd", [P, HALF // P, 2 * PAIRS], BF16)
        inv = sb("inv", [P, 4, BANK], BF16)
        junk, junk_w = sb("junk", [P, HALF], BF16), sb("junk_w", [P, HALF], BF16)
        stats = sb("stats", [P, R, NBANK, 6], F32)
        stats2 = sb("stats2", [P, R, NBANK, 6], F32)
        mv1 = sb("mv1", [P, R, 2], F32)
        mv2 = sb("mv2", [P, R, 2], F32)
        rs1, nb1 = sb("rs1", [P, R], F32), sb("nb1", [P, R], F32)
        rs2, nb2 = sb("rs2", [P, R], F32), sb("nb2", [P, R], F32)
        tmp, tmp2 = sb("tmp", [P, R], F32), sb("tmp2", [P, R], F32)
        var_eps = [sb(f"var_eps{i}", [P, R], F32) for i in range(2)]
        nmean = [sb(f"nmean{i}", [P, R], F32) for i in range(2)]
        mean_sq = sb("mean_sq", [P, R], F32)
        pool_pad = [sb(f"pool_pad{i}", [P, R], F32) for i in range(2)]
        w_tile = consts["xn0"]
        w_sumsq = sb("w_sumsq", [P, 2 * (L // P + 1)], F32)
        w_total, w_total_all = sb("w_total", [P, 1], F32), sb("w_total_all", [P, 1], F32)
        sumsq = [sb(f"sumsq{i}", [P, PIECES], F32) for i in range(2)]
        sumall = [sb(f"sumall{i}", [P, PIECES], F32) for i in range(2)]
        scale = [sb(f"scale{i}", [P, 1], F32) for i in range(2)]
        iscale = [sb(f"iscale{i}", [P, 1], F32) for i in range(2)]
        lscale = [sb(f"lscale{i}", [P, 1], F32) for i in range(2)]
        rowmax, nmax = sb("rowmax", [P, R], F32), sb("nmax", [P, R], F32)
        psum_e, rinv = sb("psum_e", [P, R], F32), sb("rinv", [P, R], F32)
        gmax = sb("gmax", [P, R], F32)
        ident = consts["ident"]
        ident16, ident_f16 = consts["ident_bf16"], consts["ident_f16"]
        g_lags, g_energy, columns = consts["g_lags"], consts["g_energy"], consts["columns"]

        ps_t = [st.enter_context(nc.psum_tensor(f"ps_t{i}_{tag}", [P, BANK], F32)) for i in range(3)]
        ps_c = [st.enter_context(nc.psum_tensor(f"ps_c{i}_{tag}", [P, BANK], F32)) for i in range(2)]
        ps_s = [st.enter_context(nc.psum_tensor(f"ps_s{i}_{tag}", [P, BANK], F32)) for i in range(R)]
        ps_g = [st.enter_context(nc.psum_tensor(f"ps_g_{tag}", [P, BANK], F32)), ps_s[0]]

        x_loaded = [[sem(f"x_loaded{i}{r}") for r in range(R)] for i in range(2)]
        c_loaded = [sem(f"c_loaded{r}") for r in range(R)]
        prefetched = sem("prefetched")
        tables_loaded = sem("tables_loaded")
        folded, ln1_ready = sem("folded"), sem("ln1_ready")
        x1_ready = [sem(f"x1_ready{r}") for r in range(R)]
        sumsq_done, sumall_done, scale_ready = sem("sumsq_done"), sem("sumall_done"), sem("scale_ready")
        t_filled, hi_done, t_free = sem("t_filled"), sem("hi_done"), sem("t_free")
        sim_done, nmax_ready, exp_done, p_ready = sem("sim_done"), sem("nmax_ready"), sem("exp_done"), sem("p_ready")
        vhi_done, vlo_done = sem("vhi_done"), sem("vlo_done")
        fwd_done, sq_done, inv_done = sem("fwd_done"), sem("sq_done"), sem("inv_done")
        g_free = [sem(f"g_free{r}") for r in range(R)]
        context_done, ctx_added = sem("context_done"), sem("ctx_added")
        ln2_ready, x2_ready, c_scaled = sem("ln2_ready"), sem("x2_ready"), sem("c_scaled")
        dve_step, pool_step = sem("dve_step"), sem("pool_step")
        evac_even, evac_odd = sem("evac_even"), sem("evac_odd")
        w_cleared = sem("w_cleared")
        w_loaded, w_squared, w_summed, w_reduced = sem("w_loaded"), sem("w_squared"), sem("w_summed"), sem("w_reduced")
        mv1_ready, mv2_ready, mv1_free = sem("mv1_ready"), sem("mv2_ready"), sem("mv1_free")

        ORDER = "k0 k1 k2 q0 k3 q1 k4 q2 k5 q3 k6 q4 k7 q5 u0 q6 u1 q7".split()
        SHORT = [name for name in ORDER if name[0] != "q"]
        TQ, TB = KT // 4 * R, len(ORDER)
        EVAC = len(SHORT) // 2

        def bank_at(p):
            kind, i = ORDER[p][0], int(ORDER[p][1])
            return (kind, i, 0) if kind == "u" else (kind, i // 4, 4 * (i % 4))

        def emptied(p):
            if ORDER[p][0] == "q":
                return t_free, TQ, int(ORDER[p][1]) + 1
            e = SHORT.index(ORDER[p])
            return (evac_even, evac_odd)[e % 2], EVAC, e // 2 + 1

        W_TILES = L // P + 1
        assert nb == L // P
        CG = R * NBANK

        def bank_of_halves(p):
            kind, r, kk = bank_at(p)
            bank = ps_t[p % 3][:]
            if kind == "k":
                return (k_both[:, kk:kk + 4, :, r * P:(r + 1) * P],
                        bank.bitcast(F16).rearrange("p (k h c) -> p k h c", k=4, h=2))
            return u_t[:, :, r * P:(r + 1) * P], bank.bitcast(BF16).rearrange("p (k c) -> p k c", c=P)

        with nc.Block() as block:
            @block.sync
            def _(sp):
                def load_context(n):
                    if is_batch(n, nb):
                        for r in range(R):
                            after(sp, vlo_done, R * (n - 1) + r + 1)
                            sp.dma_start(cbuf[:, r], ctx_in[bass.ds(n * C + r * P, P), :]).then_inc(c_loaded[r], 16)

                def load_weights(n):
                    if is_batch(n, W_TILES):
                        after(sp, w_squared, 2 * n)
                        if isinstance(n, int) and n == 0:
                            sp.dma_start(w_tile[0:ER, :], b_rows).then_inc(w_loaded, 16)
                        else:
                            sp.dma_start(w_tile[:], w_rows[bass.ds((n - 1) * P, P), :]).then_inc(w_loaded, 16)

                def store(n, parity):
                    if is_batch(n, nb):
                        for r in range(R):
                            sp.wait_ge(x2_ready, R * n + r + 1)
                            sp.dma_start(x2_out[bass.ds(n * C + r * P, P), :], x2buf[parity][:, r]).then_inc(stored[parity][r], 16)

                def load_x(n, parity):
                    if is_batch(n, nb):
                        for r in range(R):
                            after(sp, ctx_added, CG * (n - 2) + NBANK * (r + 1))
                            sp.dma_start(xbuf[parity][:, r], src[bass.ds(n * C + r * P, P), :]).then_inc(x_loaded[parity][r], 16)

                def slot(n, half, parity):
                    if isinstance(n, int) and n == -2:
                        load_context(0)
                        load_x(0, 0)
                        load_weights(0)
                        sp.dma_start(fwd[:], consts["fwd_dram"]).then_inc(tables_loaded, 16)
                        sp.dma_start(inv[:], consts["inv_dram"]).then_inc(tables_loaded, 16)
                    else:
                        load_context(n + 2)
                        load_weights(n + 2)
                        store(n - 1, 1 - parity)
                        load_x(n + 2, parity)

                batch_slots(sp, None, nb, slot, 0)
                sp.wait_ge(stored[0][0], 16)
                sp.wait_ge(w_squared, 2 * W_TILES)
                sp.dma_start(consts["xn0"][:], x2_out[0:P, :]).then_inc(prefetched, 16)
                sp.dma_start(consts["ag_raw"][:], ag_in.rearrange("p k c -> p (k c)")).then_inc(prefetched, 16)
                for c in range(PREFETCHED):
                    sp.dma_start(consts["chunks"][c][:].rearrange("p k c -> p (k c)"), chunk_rows(w_chunks, c)).then_inc(prefetched, 16)
                store(nb - 1, (nb - 1) % 2)
                for r in range(R):
                    sp.wait_ge(stored[0][r], 16 * (nb // 2))
                sp.wait_ge(prefetched, 16 * (PREFETCHED + 2))

            @block.gpsimd
            def _(pool):
                g = nc.gpsimd
                chain = Chain(nc, pool, pool_step, consts["pad"])

                def settle(i):
                    g.tensor_tensor(pool_pad[i][:], columns[:, MINUS_ONE], columns[:, MINUS_ONE], ALU.mult)

                def norm_steps(i, mv, eps_at, rstd, nbias, ready):
                    g.tensor_tensor(var_eps[i][:], mv[:, :, 1], columns[:, eps_at], ALU.add)
                    chain.link(g.tensor_tensor(nmean[i][:], mv[:, :, 0], columns[:, MINUS_ONE], ALU.mult))
                    chain.link(g.tensor_tensor(rstd, var_eps[i][:], columns[:, MINUS_HALF], ALU.pow))
                    g.tensor_tensor(nbias, nmean[i][:], rstd, ALU.mult).then_inc(ready, 1)

                def slot(n, half, parity):
                    cur, nxt, n2 = is_batch(n, nb), is_batch(n + 1, nb), is_batch(n + 2, nb)
                    other = 1 - parity

                    def fold(r):
                        if n2:
                            pool.wait_ge(x_loaded[parity][r], 16 * (half + 2))
                            g.tensor_tensor(u_rows[:, r], xbuf[parity][:, r, 0:HALF], xbuf[parity][:, r, HALF:L],
                                            ALU.subtract).then_inc(folded, 1)

                    def value_low(r, i):
                        if n2:
                            at = slice(i * HALF, (i + 1) * HALF)
                            pool.wait_ge(c_scaled, R * (n + 2) + r + 1)
                            ins = g.tensor_tensor(v_lo[parity][:, r, at], cbuf[:, r, at], v_hi[parity][:, r, at], ALU.subtract)
                            if i == 1:
                                ins.then_inc(vlo_done, 1)

                    def reduce_context():
                        if n2:
                            pool.wait_ge(sumsq_done, PIECES * (n + 3))
                            settle(0)
                            g.partition_all_reduce(sumall[parity][:], sumsq[parity][:], P,
                                                   bass.bass_isa.ReduceOp.add).then_inc(sumall_done, 1)

                    reduce_context()
                    if n2:
                        after(pool, t_filled, TB * (n + 1) + ORDER.index("u1") + 1)
                    fold(0)
                    if cur:
                        pool.wait_ge(mv2_ready, n + 1)
                        after(pool, x2_ready, R * n)
                        norm_steps(1, mv2, EPS_AT, rs2[:], nb2[:], ln2_ready)
                    fold(1)
                    value_low(0, 0)
                    if n2:
                        pool.wait_ge(mv1_ready, n + 3)
                        for r in range(R):
                            after(pool, x1_ready[r], n + 2)
                        g.tensor_tensor(mean_sq[:], mv1[:, :, 0], mv1[:, :, 0], ALU.mult)
                        norm_steps(0, mv1, eps_column, rs1[:], nb1[:], ln1_ready)
                        pool.wait_ge(ln1_ready, n + 3)
                        g.tensor_tensor(g_energy[:, bass.ds((n + 2) * R, R)], mean_sq[:], mv1[:, :, 1], ALU.add).then_inc(mv1_free, 1)
                    value_low(0, 1)
                    value_low(1, 0)
                    value_low(1, 1)
                    if cur and not (isinstance(n, int) and n == nb - 1):
                        pool.wait_ge(ln2_ready, n + 1)
                        settle(1)
                        for r in range(R):
                            g.tensor_scalar(x2buf[parity][:, r], x2buf[parity][:, r], rs2[:, r:r + 1], nb2[:, r:r + 1], ALU.mult,
                                            ALU.add).then_inc(x2_ready, 1)
                    if isinstance(n, int) and n == nb - 1:
                        pool.wait_ge(w_summed, 1)
                        g.partition_all_reduce(w_total_all[:], w_total[:], P, bass.bass_isa.ReduceOp.add).then_inc(w_reduced, 1)

                batch_slots(pool, chain, nb, slot, 4)

            @block.scalar
            def _(act):
                def slot(n, half, parity):
                    cur, nxt, n2 = is_batch(n, nb), is_batch(n + 1, nb), is_batch(n + 2, nb)
                    other = 1 - parity

                    def emptied_bank(p):
                        if nxt and (ORDER[p][0] == "q" or emptied(p)[0] is evac_even):
                            act.wait_ge(t_filled, TB * (n + 1) + p + 1)
                            kind, r, kk = bank_at(p)
                            if kind == "q":
                                bank = ps_t[p % 3][:].rearrange("p (k c) -> p k c", k=4)
                                nc.scalar.activation(q_hi[:, kk:kk + 4, r * P:(r + 1) * P], bank, ACT.Copy).then_inc(hi_done, 1)
                            else:
                                dst, bank = bank_of_halves(p)
                                nc.scalar.activation(dst, bank, ACT.Copy).then_inc(evac_even, 1)

                    def square_context(i):
                        if n2:
                            r, at = i // 2, i % 2 * HALF
                            act.wait_ge(c_loaded[r], 16 * (n + 3))
                            after(act, sumsq_done, PIECES * (n + 2) + i)
                            nc.scalar.activation(junk[:], cbuf[:, r, at:at + HALF], ACT.Square,
                                                 accum_out=sumsq[parity][:, i:i + 1]).then_inc(sumsq_done, 1)

                    def square_weights(i):
                        if is_batch(n + 2, W_TILES):
                            at = slice(i * HALF, (i + 1) * HALF)
                            act.wait_ge(w_loaded, 16 * (n + 3))
                            after(act, w_squared, 2 * (n + 2) + i)
                            if isinstance(n, int) and n == -2:
                                act.wait_ge(w_cleared, 1)
                                nc.scalar.activation(junk_w[0:ER, :], w_tile[0:ER, at], ACT.Square,
                                                     accum_out=w_sumsq[0:ER, i:i + 1]).then_inc(w_squared, 1)
                            else:
                                nc.scalar.activation(junk_w[:], w_tile[:, at], ACT.Square,
                                                     accum_out=w_sumsq[:, bass.ds(2 * (n + 2) + i, 1)]).then_inc(w_squared, 1)

                    def normalise1():
                        if n2:
                            act.wait_ge(ln1_ready, n + 3)
                            act.wait_ge(folded, R * (n + 2) + 1)
                            nc.scalar.activation(xbuf[parity][:, 0], xbuf[parity][:, 0], ACT.Identity, bias=nb1[:, 0:1],
                                                 scale=rs1[:, 0:1]).then_inc(x1_ready[0], 1)

                    def softmax_exp(r):
                        if nxt:
                            after(act, p_ready, R * n + r + 1)
                            act.wait_ge(nmax_ready, R * (n + 1) + r + 1)
                            nc.scalar.activation(expd[:, r], ps_s[r][:, 0:C], ACT.Exp, bias=nmax[:, r:r + 1],
                                                 scale=lscale[other][:], accum_out=psum_e[:, r:r + 1]).then_inc(exp_done, 1)

                    for j in range(CG):
                        emptied_bank(2 * j)
                        emptied_bank(2 * j + 1)
                        if 1 <= j <= PIECES:
                            square_context(j - 1)
                        if j >= 6 and not (isinstance(n, int) and n == -2):
                            square_weights(j - 6)
                    for p in range(2 * CG, TB):
                        emptied_bank(p)
                    def value_high(r):
                        if n2:
                            after(act, context_done, CG * (n + 1))
                            act.wait_ge(scale_ready, n + 3)
                            nc.scalar.activation(v_hi[parity][:, r], cbuf[:, r], ACT.Copy, scale=scale[parity][:]).then_inc(vhi_done, 1)

                    def guard_squares(m):
                        if nxt:
                            after(act, inv_done, R * (n + 1))
                            act.wait_ge(fwd_done, 4 * (n + 1) + m + 1)
                            nc.scalar.activation(power[:, m], ps_t[m % 3][:, 0:C], ACT.Square).then_inc(sq_done, 1)

                    value_high(0)
                    guard_squares(0)
                    value_high(1)
                    for m in range(1, 4):
                        guard_squares(m)
                    softmax_exp(0)
                    if isinstance(n, int) and n == -2:
                        square_weights(0)
                        square_weights(1)
                    normalise1()
                    softmax_exp(1)

                batch_slots(act, None, nb, slot, 0)

            @block.vector
            def _(dve):
                v = nc.vector
                chain = Chain(nc, dve, dve_step, consts["pad"])
                v.memset(w_sumsq[:], 0.0).then_inc(w_cleared, 1)

                def slot(n, half, parity):
                    cur, nxt, n2 = is_batch(n, nb), is_batch(n + 1, nb), is_batch(n + 2, nb)
                    other = 1 - parity

                    def x2_stats(j):
                        dve.wait_ge(ctx_added, CG * n + j + 1)
                        r, b = j // NBANK, j % NBANK
                        return v.bn_stats(stats2[:, r, b], x2buf[parity][:, r, b * BANK:(b + 1) * BANK])

                    def emptied_bank(p):
                        if nxt and ORDER[p][0] == "q":
                            kind, r, kk = bank_at(p)
                            at = (slice(None), slice(kk, kk + 4), slice(r * P, (r + 1) * P))
                            bank = ps_t[p % 3][:].rearrange("p (k c) -> p k c", k=4)
                            dve.wait_ge(hi_done, TQ * (n + 1) + int(ORDER[p][1]) + 1)
                            v.tensor_tensor(q_lo[at], bank, q_hi[at], ALU.subtract).then_inc(t_free, 1)
                        elif nxt and emptied(p)[0] is evac_odd:
                            dve.wait_ge(t_filled, TB * (n + 1) + p + 1)
                            dst, bank = bank_of_halves(p)
                            v.tensor_copy(dst, bank).then_inc(evac_odd, 1)

                    def guard_lags(r):
                        if cur:
                            dve.wait_ge(inv_done, R * n + r + 1)
                            chain.link(v.tensor_reduce(gmax[:, r:r + 1], ps_g[r][:, 1:BANK], AX.X, ALU.max, apply_absolute_value=True))
                            v.tensor_tensor(g_lags[:, bass.ds(n * R + r, 1)], gmax[:, r:r + 1], ps_g[r][:, 0:1],
                                            ALU.subtract).then_inc(g_free[r], 1)

                    for j in range(CG):
                        emptied_bank(2 * j)
                        emptied_bank(2 * j + 1)
                        if cur:
                            r, b = j // NBANK, j % NBANK
                            if b == 0:
                                after(dve, stored[parity][r], 16 * half)
                            dve.wait_ge(context_done, CG * n + j + 1)
                            v.scalar_tensor_tensor(x2buf[parity][:, r, b * BANK:(b + 1) * BANK], ps_c[j % 2][:], iscale[parity][:],
                                                   xbuf[parity][:, r, b * BANK:(b + 1) * BANK], ALU.mult,
                                                   ALU.add).then_inc(ctx_added, 1)
                            if j:
                                x2_stats(j - 1)
                        if j == 0:
                            guard_lags(1)
                    for p in range(2 * CG, TB):
                        emptied_bank(p)
                    if cur:
                        chain.link(x2_stats(CG - 1))
                        after(dve, ln2_ready, n)
                        chain.settle()
                        chain.link(v.bn_aggr(mv2[:, 0], stats2[:, 0].rearrange("p a b -> p (a b)")))
                        chain.settle()
                        v.bn_aggr(mv2[:, 1], stats2[:, 1].rearrange("p a b -> p (a b)")).then_inc(mv2_ready, 1)

                    def scale_context(r):
                        if n2:
                            dve.wait_ge(vhi_done, R * (n + 2) + r + 1)
                            v.tensor_scalar(cbuf[:, r], cbuf[:, r], scale[parity][:], None, ALU.mult).then_inc(c_scaled, 1)

                    def softmax_max(r):
                        if nxt:
                            dve.wait_ge(sim_done, R * (n + 1) + r + 1)
                            dve.wait_ge(scale_ready, n + 2)
                            chain.link(v.tensor_reduce(rowmax[:, r:r + 1], ps_s[r][:, 0:C], AX.X, ALU.max))
                            v.tensor_scalar(nmax[:, r:r + 1], rowmax[:, r:r + 1], iscale[other][:], -(C ** -0.5), ALU.mult,
                                            ALU.mult).then_inc(nmax_ready, 1)

                    def softmax_norm(r):
                        if nxt:
                            dve.wait_ge(exp_done, R * (n + 1) + r + 1)
                            chain.link(v.reciprocal(rinv[:, r:r + 1], psum_e[:, r:r + 1]))
                            chain.link(v.tensor_scalar(p_hi[:, r], expd[:, r], rinv[:, r:r + 1], None, ALU.mult))
                            v.scalar_tensor_tensor(p_lo[:, r], expd[:, r], rinv[:, r:r + 1], p_hi[:, r], ALU.mult,
                                                   ALU.subtract).then_inc(p_ready, 1)

                    def x_stats(r):
                        if n2:
                            dve.wait_ge(x_loaded[parity][r], 16 * (half + 2))
                            for b in range(NBANK):
                                ins = v.bn_stats(stats[:, r, b], xbuf[parity][:, r, b * BANK:(b + 1) * BANK])
                            chain.link(ins)
                            if r == 0:
                                after(dve, mv1_free, n + 2)
                            chain.settle()
                            ins = v.bn_aggr(mv1[:, r], stats[:, r].rearrange("p a b -> p (a b)"))
                            if r == 0:
                                chain.link(ins)
                            else:
                                ins.then_inc(mv1_ready, 1)

                    if n2:
                        dve.wait_ge(sumall_done, n + 3)
                        chain.link(v.tensor_reduce(tmp[:, 0:1], sumall[parity][:], AX.X, ALU.add))
                        scale_steps(nc, chain, scale[parity][:], iscale[parity][:], tmp[:, 0:1], tmp2[:, 0:1])
                        v.tensor_scalar(lscale[parity][:], iscale[parity][:], C ** -0.5, None, ALU.mult).then_inc(scale_ready, 1)
                    x_stats(0)
                    scale_context(0)
                    softmax_max(0)
                    x_stats(1)
                    softmax_norm(0)
                    guard_lags(0)
                    scale_context(1)
                    softmax_max(1)
                    softmax_norm(1)
                    if n2:
                        dve.wait_ge(ln1_ready, n + 3)
                        dve.wait_ge(folded, R * (n + 2) + 2)
                        v.tensor_scalar(xbuf[parity][:, 1], xbuf[parity][:, 1], rs1[:, 1:2], nb1[:, 1:2], ALU.mult,
                                        ALU.add).then_inc(x1_ready[1], 1)
                    if isinstance(n, int) and n == nb - 1:
                        dve.wait_ge(ln2_ready, n + 1)
                        for r in range(R):
                            v.tensor_scalar(x2buf[parity][:, r], x2buf[parity][:, r], rs2[:, r:r + 1], nb2[:, r:r + 1], ALU.mult,
                                            ALU.add).then_inc(x2_ready, 1)
                        dve.wait_ge(w_squared, 2 * W_TILES)
                        v.tensor_reduce(w_total[:], w_sumsq[:], AX.X, ALU.add).then_inc(w_summed, 1)
                        dve.wait_ge(w_reduced, 1)
                        scale_steps(nc, chain, consts["w_scale"][:], consts["w_iscale"][:], w_total_all[:], tmp[:, 0:1])

                batch_slots(dve, chain, nb, slot, 16)

            @block.tensor
            def _(pe):
                def slot(n, half, parity):
                    cur, nxt = is_batch(n, nb), is_batch(n + 1, nb)
                    other = 1 - parity

                    def transposed_bank(p):
                        if not nxt:
                            return
                        if p >= 3:
                            emptied_by, counts, count = emptied(p - 3)
                            pe.wait_ge(emptied_by, counts * (n + 1) + count)
                        bank = ps_t[p % 3]
                        kind, r, kk = bank_at(p)
                        if kind == "q":
                            if kk == 0:
                                pe.wait_ge(x1_ready[r], n + 2)
                            for i in range(4):
                                ins = nc.tensor.transpose(bank[:, i * P:(i + 1) * P], xbuf[other][:, r, (kk + i) * P:(kk + i + 1) * P], ident[:])
                        elif kind == "k":
                            if kk == 0:
                                pe.wait_ge(vlo_done, R * (n + 1) + r + 1)
                            out = bank[:].bitcast(F16)
                            for i in range(8):
                                half_rows = (v_hi, v_lo)[i % 2][other]
                                ins = nc.tensor.transpose(out[:, i * P:(i + 1) * P], half_rows[:, r, (kk + i // 2) * P:(kk + i // 2 + 1) * P],
                                                          ident_f16[:])
                        else:
                            pe.wait_ge(folded, R * (n + 1) + r + 1)
                            out = bank[:].bitcast(BF16)
                            for i in range(HALF // P):
                                ins = nc.tensor.transpose(out[:, i * P:(i + 1) * P], u_rows[:, r, i * P:(i + 1) * P], ident16[:])
                        ins.then_inc(t_filled, 1)

                    def context(j):
                        if j == 0:
                            pe.wait_ge(p_ready, R * (n + 1))
                        after(pe, ctx_added, CG * n + j - 1)
                        r, b = j // NBANK, j % NBANK
                        terms = [(p_hi, v_hi), (p_hi, v_lo), (p_lo, v_hi)]
                        for i in range(3 * R):
                            pp, vv = terms[i % 3]
                            d = i // 3
                            ins = nc.tensor.matmul(ps_c[j % 2][:], pp[:, d, r * P:(r + 1) * P], vv[parity][:, d, b * BANK:(b + 1) * BANK],
                                                   start=(i == 0), stop=(i == 3 * R - 1))
                        ins.then_inc(context_done, 1)

                    def logits(r):
                        after(pe, exp_done, R * n + r + 1)
                        terms = [(q_hi, 0), (q_hi, 1), (q_lo, 0)]
                        for i in range(3 * KT):
                            qq, part = terms[i % 3]
                            k = i // 3
                            ins = nc.tensor.matmul(ps_s[r][:, 0:C], qq[:, k, r * P:(r + 1) * P], k_both[:, k, part, :],
                                                   start=(i == 0), stop=(i == 3 * KT - 1))
                        ins.then_inc(sim_done, 1)

                    for p in range(3):
                        transposed_bank(p)
                    for j in range(CG):
                        if cur:
                            context(j)
                        for p in (2 * j + 3, 2 * j + 4):
                            if p < TB:
                                transposed_bank(p)
                    if nxt:
                        for p in (ORDER.index("k6"), ORDER.index("k7"), ORDER.index("q3")):
                            emptied_by, counts, count = emptied(p)
                            pe.wait_ge(emptied_by, counts * (n + 1) + count)
                        after(pe, g_free[1], n + 1)
                        logits(0)
                        pe.wait_ge(t_free, TQ * (n + 2))
                        for evac in (evac_even, evac_odd):
                            pe.wait_ge(evac, EVAC * (n + 2))
                        if isinstance(n, int) and n == -1:
                            pe.wait_ge(tables_loaded, 32)
                        for m in range(4):
                            if m == 3:
                                pe.wait_ge(sq_done, 4 * (n + 1) + 1)
                            for k in range(HALF // P):
                                ins = nc.tensor.matmul(ps_t[m % 3][:, 0:C], fwd[:, k, m * P:(m + 1) * P], u_t[:, k, :],
                                                       start=(k == 0), stop=(k == HALF // P - 1))
                            ins.then_inc(fwd_done, 1)
                        logits(1)
                        pe.wait_ge(sq_done, 4 * (n + 2))
                        for r in range(R):
                            if r == 0:
                                after(pe, g_free[0], n + 1)
                            else:
                                pe.wait_ge(exp_done, R * (n + 1) + 1)
                            for m in range(4):
                                ins = nc.tensor.matmul(ps_g[r][:], power[:, m, r * P:(r + 1) * P], inv[:, m, :],
                                                       start=(m == 0), stop=(m == 3))
                            ins.then_inc(inv_done, 1)

                batch_slots(pe, None, nb, slot, 0)


def guard_tables():
    order = (np.arange(L // 4) * 197 + 61) % (L // 4)
    freq = np.sort(2 * order[:PAIRS] + 1).astype(np.int64)
    pos = np.arange(HALF, dtype=np.int64)
    angle = 2 * np.pi * ((pos[:, None] * freq[None, :]) % L) / L
    fwd = np.concatenate([np.cos(angle), np.sin(angle)], 1) / np.sqrt(L / 2)
    lag = np.arange(BANK, dtype=np.int64)
    both = np.concatenate([freq, freq])
    inv = np.cos(2 * np.pi * ((both[:, None] * lag[None, :]) % L) / L)
    return (fwd.reshape(HALF // P, P, 2 * PAIRS).transpose(1, 0, 2).copy(), inv.reshape(4, P, BANK).transpose(1, 0, 2).copy())


def feed_forward(nc, x2, out, w_chunks, b_rows, consts, x2_stored):
    NT = x2.shape[0] // P
    CHUNKS = NBANK * KT // KC
    GPSIMD_CHUNKS = range(7, CHUNKS, 4)
    ALL, LATER = PREFETCHED + 4, PREFETCHED + 2
    buffer_of = [c % ALL if c < 2 * ALL else (c - 2 * ALL) % LATER for c in range(CHUNKS)]
    rounds = [buffer_of[:c + 1].count(buffer_of[c]) for c in range(CHUNKS)]
    last_user = [max([b for b in range(c) if buffer_of[b] == buffer_of[c]], default=None) for c in range(CHUNKS)]
    with ExitStack() as st:
        def sb(name, shape, dt):
            return st.enter_context(nc.sbuf_tensor(f"{name}_f", shape, dt))

        def sem(name):
            return st.enter_context(nc.semaphore(f"{name}_f"))

        xn1, x_hi1, x_lo1 = sb("xn1", [P, L], F32), sb("x_hi1", [P, KT, P], F16), sb("x_lo1", [P, KT, P], F16)
        w_hi, w_lo = sb("w_hi", [P, KT, L], F16), sb("w_lo", [P, KT, L], F16)
        b_stack = sb("b_stack", [P, 2, L], F16)
        ag_t = sb("ag_t", [P, KT, 2 * AG], F16)
        xn = [consts["xn0"], xn1]
        x_hi, x_lo = [sb("x_hi0", [P, KT, P], F16), x_hi1], [sb("x_lo0", [P, KT, P], F16), x_lo1]
        y = [sb(f"y{i}", [P, L], F32) for i in range(2)]
        ag_raw = consts["ag_raw"][:].rearrange("p (k c) -> p k c", k=KT)
        b_raw = y[0]
        chunk = [c[:] for c in consts["chunks"]]
        chunk += [rows[:, i * KC * BANK:(i + 1) * KC * BANK].rearrange("p (k c) -> p k c", k=KC) for rows in (y[1], xn1) for i in range(2)]
        ag_sumsq, ag_total = sb("ag_sumsq", [P, 2], F32), sb("ag_total", [P, 2], F32)
        ag_scale, ag_iscale = sb("ag_scale", [P, 2], F32), sb("ag_iscale", [P, 2], F32)
        stats, mv = sb("stats", [P, NBANK, 6], F32), sb("mv", [P, R, 2], F32)
        rs, nb_ = sb("rs", [P, R], F32), sb("nb", [P, R], F32)
        var_eps, nmean = sb("var_eps", [P, R], F32), sb("nmean", [P, R], F32)
        tmp, tmp2 = sb("tmp", [P, 2], F32), sb("tmp2", [P, 1], F32)
        ag = sb("ag", [P, AG], F32)
        nmax = sb("nmax", [P, 1], F32)
        probs = sb("probs", [P, EXPERTS], F32)
        top, top_i = sb("top", [P, 8], F32), sb("top_i", [P, 8], U32)
        top_f = sb("top_f", [P, 2], F32)
        pair, wtop = sb("pair", [P, 1], F32), sb("wtop", [P, 2], F32)
        dense, dense2 = sb("dense", [P, EXPERTS], F32), sb("dense2", [P, EXPERTS], F32)
        h = sb("h", [P, ER], F32)
        h_parts = consts["ag_raw"][:, 0:2 * ER].bitcast(BF16).rearrange("p (a b) -> p a b", a=4)
        h_t = consts["ag_raw"][:, P:2 * P].bitcast(BF16).rearrange("p (a b) -> p a b", a=2)
        ident, ident16 = consts["ident"], consts["ident_bf16"]
        expert_ids, columns = consts["expert_ids"], consts["columns"]
        w_scale, w_iscale = consts["w_scale"], consts["w_iscale"]

        def pb(name, shape, dt):
            return st.enter_context(nc.psum_tensor(f"{name}_f", shape, dt))

        ps_y = [pb(f"ps_y{j}", [P, BANK], F32) for j in range(NBANK)]
        ps_a, ps_h = pb("ps_a", [P, BANK], F32), pb("ps_h", [P, 2, BANK], BF16)
        ps_t = [pb(f"ps_t{i}", [P, BANK], F32) for i in range(2)]

        w_loaded = [sem(f"w_loaded{i}") for i in range(ALL)]
        w_hi_done, w_split, w_split_pool = sem("w_hi_done"), sem("w_split"), sem("w_split_pool")
        ag_squared, ag_summed, ag_scaled = sem("ag_squared"), sem("ag_summed"), sem("ag_scaled")
        ag_hi_done, ag_split = sem("ag_hi_done"), sem("ag_split")
        b_loaded, b_hi_done, b_split = sem("b_loaded"), sem("b_hi_done"), sem("b_split")
        x_loaded = [sem(f"x_loaded{i}") for i in range(2)]
        stored = [sem(f"stored{i}") for i in range(2)]
        t_filled, hi_done, t_free = sem("t_filled"), sem("hi_done"), sem("t_free")
        a_done, a_read, nmax_ready, exp_done, h_ready = sem("a_done"), sem("a_read"), sem("nmax_ready"), sem("exp_done"), sem("h_ready")
        ht_done, ht_copied = sem("ht_done"), sem("ht_copied")
        bank_done, evacuated = sem("bank_done"), sem("evacuated")
        mv_ready, ln_ready, out_ready, dve_step, pool_step = sem("mv_ready"), sem("ln_ready"), sem("out_ready"), sem("dve_step"), sem("pool_step")

        def tiles(eng, slot, chain, links):
            for t in (-1, 0, 1):
                slot(t, t // 2, t % 2)
                if chain:
                    chain.mark()
            start = chain.base - 2 * links if chain else 0
            with eng.Fori(1, (NT - 2) // 2) as m:
                for parity in range(2):
                    t = 2 * m + parity
                    if chain:
                        chain.base, chain.count = t * links + start, 0
                    slot(t, m, parity)
                    if chain:
                        assert chain.count == links, (chain.count, links)
            if chain:
                chain.base, chain.count = start + (NT - 2) * links, 0
            for t in (NT - 2, NT - 1):
                slot(t, t // 2, t % 2)

        def first(t):
            return isinstance(t, int) and t == 0

        def chunk_at(c):
            k = KC * (c % (CHUNKS // NBANK))
            j = c // (CHUNKS // NBANK)
            return slice(None), slice(k, k + KC), slice(j * BANK, (j + 1) * BANK)

        def wait_split(eng, c):
            if c in GPSIMD_CHUNKS:
                eng.wait_ge(w_split_pool, GPSIMD_CHUNKS.index(c) + 1)
            else:
                eng.wait_ge(w_split, len([b for b in range(c + 1) if b not in GPSIMD_CHUNKS]))

        with nc.Block() as block:
            @block.sync
            def _(sp):
                def load(t, half, parity):
                    if is_batch(t, NT):
                        after(sp, evacuated, NBANK * (t - 1))
                        sp.dma_start(xn[parity][:], x2[bass.ds(t * P, P), :]).then_inc(x_loaded[parity], 16)

                def slot(t, half, parity):
                    if isinstance(t, int) and t == -1:
                        for c in range(PREFETCHED, CHUNKS):
                            if last_user[c] is not None:
                                wait_split(sp, last_user[c])
                            if c == LATER:
                                wait_stored(sp, x2_stored, NT // R)
                            sp.dma_start(chunk[buffer_of[c]].rearrange("p k c -> p (k c)"), chunk_rows(w_chunks, c)).then_inc(w_loaded[buffer_of[c]], 16)
                            if c == 12:
                                sp.wait_ge(ag_squared, 2)
                                for i in range(2):
                                    sp.dma_start(b_raw[i * ER:(i + 1) * ER, :], b_rows).then_inc(b_loaded, 16)
                            if c == 18:
                                for last in range(2 * ALL - 2, 2 * ALL):
                                    wait_split(sp, last)
                                load(1, 0, 1)
                        return
                    load(t + 2, half + 1, parity)
                    sp.wait_ge(out_ready, t + 1)
                    sp.dma_start(out[bass.ds(t * P, P), :], y[parity][:]).then_inc(stored[parity], 16)

                tiles(sp, slot, None, 0)
                for i in range(2):
                    sp.wait_ge(stored[i], 16 * (NT // 2))

            @block.gpsimd
            def _(pool):
                g = nc.gpsimd
                chain = Chain(nc, pool, pool_step, consts["pad"])

                def slot(t, half, parity):
                    if not is_batch(t, NT):
                        pool.wait_ge(ag_squared, 2)
                        g.partition_all_reduce(ag_total[:], ag_sumsq[:], P, bass.bass_isa.ReduceOp.add).then_inc(ag_summed, 1)
                        for c in GPSIMD_CHUNKS:
                            pool.wait_ge(w_hi_done, c + 1)
                            chain.link(g.tensor_scalar(chunk[buffer_of[c]], chunk[buffer_of[c]], w_scale[:], 1.0, ALU.mult, ALU.mult))
                            g.tensor_tensor(w_lo[chunk_at(c)], chunk[buffer_of[c]], w_hi[chunk_at(c)], ALU.subtract).then_inc(w_split_pool, 1)
                        return
                    pool.wait_ge(mv_ready, t + 1)
                    after(pool, out_ready, t)
                    g.tensor_tensor(var_eps[:, 0:1], mv[:, 0, 1:2], columns[:, EPS_AT, 0:1], ALU.add)
                    chain.link(g.tensor_tensor(nmean[:, 0:1], mv[:, 0, 0:1], columns[:, MINUS_ONE, 0:1], ALU.mult))
                    chain.link(g.tensor_tensor(rs[:, 0:1], var_eps[:, 0:1], columns[:, MINUS_HALF, 0:1], ALU.pow))
                    g.tensor_tensor(nb_[:, 0:1], nmean[:, 0:1], rs[:, 0:1], ALU.mult).then_inc(ln_ready, 1)

                tiles(pool, slot, chain, 2)

            @block.scalar
            def _(act):
                def chunk_hi(c):
                    after(act, w_loaded[buffer_of[c]], 16 * (rounds[c] - (buffer_of[c] < PREFETCHED)))
                    nc.scalar.activation(w_hi[chunk_at(c)], chunk[buffer_of[c]], ACT.Copy, scale=w_scale[:]).then_inc(w_hi_done, 1)

                def slot(t, half, parity):
                    cur, nxt = is_batch(t, NT), is_batch(t + 1, NT)

                    def high_half(q):
                        if nxt:
                            act.wait_ge(t_filled, 4 * (t + 1) + q + 1)
                            nc.scalar.activation(x_hi[1 - parity][:, 4 * q:4 * q + 4, :],
                                                 ps_t[q % 2][:].rearrange("p (k c) -> p k c", k=4), ACT.Copy).then_inc(hi_done, 1)

                    def chunks_hi(*chunks):
                        if first(t) or not cur:
                            for c in chunks:
                                chunk_hi(c)

                    if not cur:
                        for i, cols in enumerate((slice(0, ER), slice(ER, AG))):
                            nc.scalar.activation(y[0][:, 0:KT * AG].rearrange("p (k c) -> p k c", k=KT)[:, :, cols], ag_raw[:, :, cols],
                                                 ACT.Square, accum_out=ag_sumsq[:, i:i + 1]).then_inc(ag_squared, 1)
                        high_half(0)
                        high_half(1)
                        chunk_hi(0)
                        high_half(2)
                        high_half(3)
                        chunks_hi(1, 2)
                        act.wait_ge(ag_scaled, 1)
                        for i, cols in enumerate((slice(0, ER), slice(ER, AG))):
                            nc.scalar.activation(ag_t[:, :, cols], ag_raw[:, :, cols], ACT.Copy, scale=ag_scale[:, i:i + 1]).then_inc(ag_hi_done, 1)
                        chunks_hi(*range(3, 12))
                        return
                    chunks_hi(12)
                    act.wait_ge(nmax_ready, t + 1)
                    nc.scalar.activation(probs[:], ag[:, ER:AG], ACT.Exp, bias=nmax[:]).then_inc(exp_done, 1)
                    chunks_hi(*range(13, 20))
                    act.wait_ge(ht_done, t + 1)
                    nc.scalar.activation(h_t, ps_h[:, :, 0:P], ACT.Copy).then_inc(ht_copied, 1)
                    high_half(0)
                    high_half(1)
                    chunks_hi(*range(20, 24))
                    chunks_hi(*range(24, 28))
                    high_half(2)
                    high_half(3)
                    chunks_hi(*range(28, CHUNKS))
                    if first(t):
                        act.wait_ge(b_loaded, 32)
                        nc.scalar.activation(b_stack[:, 0], b_raw[:], ACT.Copy, scale=w_scale[:]).then_inc(b_hi_done, 1)
                        nc.scalar.activation(b_stack[0:ER, 1], b_raw[0:ER, :], ACT.Copy, scale=w_scale[0:ER, :]).then_inc(b_hi_done, 1)
                    if cur:
                        act.wait_ge(ln_ready, t + 1)
                        nc.scalar.activation(y[parity][:], y[parity][:], ACT.Identity, bias=nb_[:, 0:1], scale=rs[:, 0:1]).then_inc(out_ready, 1)

                tiles(act, slot, None, 0)

            @block.vector
            def _(dve):
                v = nc.vector
                chain = Chain(nc, dve, dve_step, consts["pad"])

                def chunk_lo(c):
                    if c in GPSIMD_CHUNKS:
                        return
                    dve.wait_ge(w_hi_done, c + 1)
                    v.scalar_tensor_tensor(w_lo[chunk_at(c)], chunk[buffer_of[c]], w_scale[:], w_hi[chunk_at(c)], ALU.mult,
                                           ALU.subtract).then_inc(w_split, 1)

                def slot(t, half, parity):
                    cur, nxt = is_batch(t, NT), is_batch(t + 1, NT)

                    def bank_out(j):
                        if j == 0:
                            after(dve, stored[parity], 16 * half)
                        dve.wait_ge(bank_done, NBANK * t + j + 1)
                        at = slice(j * BANK, (j + 1) * BANK)
                        v.scalar_tensor_tensor(y[parity][:, at], ps_y[j][:], w_iscale[:], xn[parity][:, at], ALU.mult,
                                               ALU.add).then_inc(evacuated, 1)

                    def low_half(q):
                        if nxt:
                            dve.wait_ge(hi_done, 4 * (t + 1) + q + 1)
                            v.tensor_tensor(x_lo[1 - parity][:, 4 * q:4 * q + 4, :], ps_t[q % 2][:].rearrange("p (k c) -> p k c", k=4),
                                            x_hi[1 - parity][:, 4 * q:4 * q + 4, :], ALU.subtract).then_inc(t_free, 1)

                    def bank_stats(j):
                        dve.wait_ge(evacuated, NBANK * t + j + 1)
                        return v.bn_stats(stats[:, j], y[parity][:, j * BANK:(j + 1) * BANK])

                    if not cur:
                        dve.wait_ge(ag_summed, 1)
                        scale_steps(nc, chain, ag_scale[:], ag_iscale[:], ag_total[:], tmp[:])
                        v.memset(nmax[:], 0.0).then_inc(ag_scaled, 1)
                        low_half(0)
                        low_half(1)
                        chunk_lo(0)
                        low_half(2)
                        low_half(3)
                        chunk_lo(1)
                        chunk_lo(2)
                        for i, cols in enumerate((slice(0, ER), slice(ER, AG))):
                            dve.wait_ge(ag_hi_done, i + 1)
                            v.scalar_tensor_tensor(ag_t[:, :, AG + cols.start:AG + cols.stop], ag_raw[:, :, cols], ag_scale[:, i:i + 1],
                                                   ag_t[:, :, cols], ALU.mult, ALU.subtract).then_inc(ag_split, 1)
                        for c in range(3, 12):
                            chunk_lo(c)
                        return
                    dve.wait_ge(a_done, t + 1)
                    chain.link(v.tensor_copy(ag[:], ps_a[:, AG:2 * AG]))
                    v.tensor_tensor(ag[:], ps_a[:, 0:AG], ag[:], ALU.add).then_inc(a_read, 1)
                    dve.wait_ge(a_read, t + 1)
                    v.tensor_scalar(ag[:, 0:ER], ag[:, 0:ER], ag_iscale[:, 0:1], None, ALU.mult)
                    chain.link(v.tensor_scalar(ag[:, ER:AG], ag[:, ER:AG], ag_iscale[:, 1:2], None, ALU.mult))
                    chain.link(v.tensor_reduce(tmp2[:], ag[:, ER:AG], AX.X, ALU.max))
                    v.tensor_scalar(nmax[:], tmp2[:], -1.0, None, ALU.mult).then_inc(nmax_ready, 1)
                    dve.wait_ge(exp_done, t + 1)
                    chain.settle()
                    chain.link(v.max(top[:], probs[:]))
                    chain.settle()
                    chain.link(v.max_index(top_i[:], top[:], probs[:]))
                    v.tensor_tensor(pair[:], top[:, 0:1], top[:, 1:2], ALU.add)
                    chain.link(v.tensor_copy(top_f[:], top_i[:, 0:2]))
                    chain.link(v.reciprocal(pair[:], pair[:]))
                    chain.link(v.tensor_scalar(wtop[:], top[:, 0:2], pair[:], 2.0, ALU.mult, ALU.mult))
                    v.tensor_scalar(dense[:], expert_ids[:], top_f[:, 0:1], wtop[:, 0:1], ALU.is_equal, ALU.mult)
                    chain.link(v.tensor_scalar(dense2[:], expert_ids[:], top_f[:, 1:2], wtop[:, 1:2], ALU.is_equal, ALU.mult))
                    chain.link(v.tensor_tensor(dense[:], dense[:], dense2[:], ALU.add))
                    chain.link(v.tensor_tensor(h[:].rearrange("p (e r) -> p e r", e=EXPERTS), ag[:, 0:ER].rearrange("p (e r) -> p e r", e=EXPERTS),
                                               dense[:].unsqueeze(2).to_broadcast([P, EXPERTS, RANK]), ALU.mult))
                    after(dve, ht_done, t)
                    chain.link(v.tensor_copy(h_parts[:, 0], h[:]))
                    chain.link(v.tensor_tensor(h[:], h[:], h_parts[:, 0], ALU.subtract))
                    v.tensor_copy(h_parts[:, 3], h_parts[:, 0])
                    chain.link(v.tensor_copy(h_parts[:, 1], h[:]))
                    v.tensor_tensor(h_parts[:, 2], h[:], h_parts[:, 1], ALU.subtract).then_inc(h_ready, 1)
                    if first(t):
                        for c in range(12, CHUNKS):
                            if c in (20, 28):
                                low_half((c - 20) // 4)
                                low_half((c - 20) // 4 + 1)
                            chunk_lo(c)
                        dve.wait_ge(b_hi_done, 2)
                        v.scalar_tensor_tensor(b_stack[ER:P, 1], b_raw[ER:P, :], w_scale[ER:P, :], b_stack[ER:P, 0], ALU.mult,
                                               ALU.subtract).then_inc(b_split, 1)
                    bank_out(0)
                    bank_out(1)
                    bank_stats(0)
                    if not first(t):
                        low_half(0)
                        low_half(1)
                    bank_stats(1)
                    bank_out(2)
                    if not first(t):
                        low_half(2)
                        low_half(3)
                    bank_stats(2)
                    bank_out(3)
                    chain.link(bank_stats(3))
                    after(dve, ln_ready, t)
                    chain.settle()
                    v.bn_aggr(mv[:, 0], stats[:].rearrange("p a b -> p (a b)")).then_inc(mv_ready, 1)

                tiles(dve, slot, chain, 15)

            @block.tensor
            def _(pe):
                def slot(t, half, parity):
                    cur, nxt = is_batch(t, NT), is_batch(t + 1, NT)
                    other = 1 - parity

                    def transposed_bank(q):
                        if nxt:
                            if q == 0:
                                after(pe, x_loaded[other], 16 * (half + 1))
                            after(pe, t_free, 4 * (t + 1) + q - 1)
                            for i in range(4):
                                k = 4 * q + i
                                ins = nc.tensor.transpose(ps_t[q % 2][:, i * P:(i + 1) * P], xn[other][:, k * P:(k + 1) * P], ident[:])
                            ins.then_inc(t_filled, 1)

                    if not cur:
                        for q in range(4):
                            transposed_bank(q)
                        return

                    def main(j):
                        after(pe, evacuated, NBANK * (t - 1) + j + 1)
                        for k in range(KT):
                            if first(t) and k % KC == 0:
                                wait_split(pe, j * (CHUNKS // NBANK) + k // KC)
                            for xx, ww in ((x_hi, w_hi), (x_hi, w_lo), (x_lo, w_hi)):
                                nc.tensor.matmul(ps_y[j][:], xx[parity][:, k], ww[:, k, j * BANK:(j + 1) * BANK],
                                                 start=(k == 0 and xx is x_hi and ww is w_hi), stop=False)

                    def lora(j):
                        nc.tensor.matmul(ps_y[j][:], h_t[:, 0], b_stack[:, 0, j * BANK:(j + 1) * BANK], start=False, stop=False)
                        nc.tensor.matmul(ps_y[j][:], h_t[:, 1], b_stack[:, 1, j * BANK:(j + 1) * BANK], start=False,
                                         stop=True).then_inc(bank_done, 1)

                    pe.wait_ge(t_free, 4 * (t + 1))

                    def experts():
                        after(pe, a_read, t)
                        if first(t):
                            pe.wait_ge(ag_split, 2)
                        for k in range(KT):
                            nc.tensor.matmul(ps_a[:, 0:2 * AG], x_hi[parity][:, k], ag_t[:, k, :], start=(k == 0), stop=False)
                            ins = nc.tensor.matmul(ps_a[:, 0:AG], x_lo[parity][:, k], ag_t[:, k, 0:AG], start=False, stop=(k == KT - 1))
                        ins.then_inc(a_done, 1)

                    def transposed_h():
                        pe.wait_ge(h_ready, t + 1)
                        after(pe, ht_copied, t)
                        for i in range(2):
                            ins = nc.tensor.transpose(ps_h[:, i, 0:P], h_parts[:, 2 * i:2 * i + 2].rearrange("p a b -> p (a b)"), ident16[:])
                        ins.then_inc(ht_done, 1)

                    if first(t):
                        main(0)
                        experts()
                        main(1)
                        transposed_h()
                    else:
                        experts()
                        main(0)
                        transposed_h()
                        main(1)
                    def loras(*banks):
                        if first(t):
                            pe.wait_ge(b_split, 1)
                        pe.wait_ge(ht_copied, t + 1)
                        for j in banks:
                            lora(j)

                    if not first(t):
                        loras(0, 1)
                    transposed_bank(0)
                    transposed_bank(1)
                    main(2)
                    if not first(t):
                        loras(2)
                    transposed_bank(2)
                    transposed_bank(3)
                    main(3)
                    loras(*(range(NBANK) if first(t) else (3,)))

                tiles(pe, slot, None, 0)


def setup(nc, consts):
    with ExitStack() as st:
        ident_ready = st.enter_context(nc.semaphore("ident_ready"))
        with nc.Block() as block:
            @block.sync
            def _(sp):
                sp.dma_start(consts["ident"][:], consts["ident_dram"]).then_inc(ident_ready, 16)
                sp.dma_start(consts["expert_ids"][:], consts["expert_dram"]).then_inc(ident_ready, 16)

            @block.vector
            def _(dve):
                for at, value in ((EPS4_AT, EPS / 4), (EPS_AT, EPS), (MINUS_ONE, -1.0), (MINUS_HALF, -0.5)):
                    nc.vector.memset(consts["columns"][:, at], value)
                dve.wait_ge(ident_ready, 32)
                nc.vector.tensor_copy(consts["ident_f16"][:], consts["ident"][:])
                nc.vector.tensor_copy(consts["ident_bf16"][:], consts["ident"][:]).then_inc(ident_ready, 1)
                dve.wait_ge(ident_ready, 33)


def autocorrelation(nc, x, z, forward_dram, inverse_dram, consts, stored_before):
    nb = x.shape[0] // C
    TOP = 7
    BITS = L.bit_length() - 1
    with ExitStack() as st:
        def sb(name, shape, dt):
            return st.enter_context(nc.sbuf_tensor(f"{name}_c", shape, dt))

        def sem(name):
            return st.enter_context(nc.semaphore(f"{name}_c"))

        rows = sb("rows", [P, R, L], F32)
        x_t = sb("x_t", [P, KT, C], F32)
        table = [sb(f"table{i}", [P, KT, P], F32) for i in range(2)]
        lags = sb("lags", [P, KT, BANK], F32)
        power = sb("power", [P, KT, C], F32)
        corr = sb("corr", [P, R, L], F32)
        turn = [sb(f"turn{i}", [P, 2 * L], F32) for i in range(2)]
        acc = sb("acc", [P, L], F32)
        top, top_i = sb("top", [P, 8], F32), sb("top_i", [P, 8], U32)
        bit_u, bit, nbit = sb("bit_u", [P, BITS, 8], U32), sb("bit", [P, BITS, 8], F32), sb("nbit", [P, BITS, 8], F32)
        ntop, total, weight = sb("ntop", [P, 1], F32), sb("total", [P, 1], F32), sb("weight", [P, 8], F32)
        ident = consts["ident"]
        ps_t = [st.enter_context(nc.psum_tensor(f"ps_t{i}_c", [P, BANK], F32)) for i in range(2)]
        ps_f = [st.enter_context(nc.psum_tensor(f"ps_f{i}_c", [P, BANK], F32)) for i in range(2)]
        ps_c = [st.enter_context(nc.psum_tensor(f"ps_c{i}_c", [P, BANK], F32)) for i in range(2)]

        x_loaded, lags_loaded = sem("x_loaded"), sem("lags_loaded")
        table_loaded = [sem(f"table_loaded{i}") for i in range(2)]
        stored = sem("stored")
        t_filled, t_copied, fwd_done, squared = sem("t_filled"), sem("t_copied"), sem("fwd_done"), sem("squared")
        corr_done, corr_copied, ntop_ready, exp_done = sem("corr_done"), sem("corr_copied"), sem("ntop_ready"), sem("exp_done")
        z_ready, dve_step = sem("z_ready"), sem("dve_step")
        NBNK = R * NBANK

        def every_batch(eng, batch):
            batch(0)
            with eng.Fori(1, nb) as n:
                batch(n)

        with nc.Block() as block:
            @block.sync
            def _(sp):
                def batch(n):
                    after(sp, z_ready, R * n)
                    sp.dma_start(rows[:], x[bass.ds(n * C, C), :].rearrange("(r p) l -> p r l", p=P)).then_inc(x_loaded, 16)
                    for m in range(KT):
                        after(sp, fwd_done, KT * n + max(m - 1, 0))
                        sp.dma_start(table[m % 2][:], forward_dram[m]).then_inc(table_loaded[m % 2], 16)
                    for c in range(NBANK):
                        after(sp, corr_done, NBNK * n + R * c)
                        sp.dma_start(lags[:], inverse_dram[c]).then_inc(lags_loaded, 16)
                    for r in range(R):
                        sp.wait_ge(z_ready, R * n + r + 1)
                        sp.dma_start(z[bass.ds(n * C + r * P, P), :], acc[:]).then_inc(stored, 16)

                wait_stored(sp, stored_before, nb)
                every_batch(sp, batch)
                sp.wait_ge(stored, 16 * R * nb)

            @block.gpsimd
            def _(pool):
                pool.wait_ge(z_ready, 1)

            @block.tensor
            def _(pe):
                def batch(n):
                    pe.wait_ge(x_loaded, 16 * (n + 1))
                    for q in range(NBNK):
                        after(pe, t_copied, NBNK * n + max(q - 1, 0))
                        for i in range(4):
                            k = 4 * (q % 4) + i
                            ins = nc.tensor.transpose(ps_t[q % 2][:, i * P:(i + 1) * P], rows[:, q // 4, k * P:(k + 1) * P], ident[:])
                        ins.then_inc(t_filled, 1)
                    pe.wait_ge(t_copied, NBNK * (n + 1))
                    for m in range(KT):
                        pe.wait_ge(table_loaded[m % 2], 16 * (KT // 2 * n + m // 2 + 1))
                        after(pe, squared, KT * n + max(m - 1, 0))
                        for k in range(KT):
                            ins = nc.tensor.matmul(ps_f[m % 2][:, 0:C], table[m % 2][:, k, :], x_t[:, k, :], start=(k == 0), stop=(k == KT - 1))
                        ins.then_inc(fwd_done, 1)
                    pe.wait_ge(squared, KT * (n + 1))
                    for c in range(NBANK):
                        pe.wait_ge(lags_loaded, 16 * (NBANK * n + c + 1))
                        for r in range(R):
                            after(pe, corr_copied, NBNK * n + max(R * c + r - 1, 0))
                            for m in range(KT):
                                ins = nc.tensor.matmul(ps_c[r][:], power[:, m, r * P:(r + 1) * P], lags[:, m, :], start=(m == 0), stop=(m == KT - 1))
                            ins.then_inc(corr_done, 1)

                every_batch(pe, batch)

            @block.scalar
            def _(act):
                def batch(n):
                    for q in range(NBNK):
                        act.wait_ge(t_filled, NBNK * n + q + 1)
                        r, kk = q // 4, 4 * (q % 4)
                        nc.scalar.activation(x_t[:, kk:kk + 4, r * P:(r + 1) * P], ps_t[q % 2][:].rearrange("p (k c) -> p k c", k=4),
                                             ACT.Copy).then_inc(t_copied, 1)
                    for m in range(KT):
                        act.wait_ge(fwd_done, KT * n + m + 1)
                        nc.scalar.activation(power[:, m], ps_f[m % 2][:, 0:C], ACT.Square).then_inc(squared, 1)
                    after(act, z_ready, R * n)
                    for c in range(NBANK):
                        for r in range(R):
                            act.wait_ge(corr_done, NBNK * n + R * c + r + 1)
                            nc.scalar.activation(corr[:, r, c * BANK:(c + 1) * BANK], ps_c[r][:], ACT.Copy).then_inc(corr_copied, 1)
                    for r in range(R):
                        act.wait_ge(ntop_ready, R * n + r + 1)
                        nc.scalar.activation(weight[:, 0:TOP], top[:, 0:TOP], ACT.Exp, bias=ntop[:], accum_out=total[:]).then_inc(exp_done, 1)

                every_batch(act, batch)

            @block.vector
            def _(dve):
                v = nc.vector
                chain = Chain(nc, dve, dve_step, consts["pad"])
                HEAD, LAG = 8, 2 * BITS + 3
                def batch(n):
                    for r in range(R):
                        chain.base, chain.count = (n * R + r) * (HEAD + TOP * LAG), 0
                        if r == 0:
                            dve.wait_ge(corr_copied, NBNK * (n + 1))
                        chain.settle()
                        chain.link(v.max(top[:], corr[:, r]))
                        chain.settle()
                        chain.link(v.max_index(top_i[:], top[:], corr[:, r]))
                        v.tensor_scalar(ntop[:], top[:, 0:1], -1.0, None, ALU.mult).then_inc(ntop_ready, 1)
                        for b in range(BITS):
                            ins = v.tensor_scalar(bit_u[:, b], top_i[:], b, 1, ALU.logical_shift_right, ALU.bitwise_and)
                        chain.link(ins)
                        chain.link(v.tensor_copy(bit[:], bit_u[:]))
                        chain.link(v.tensor_scalar(nbit[:], bit[:], -1.0, 1.0, ALU.mult, ALU.add))
                        dve.wait_ge(exp_done, R * n + r + 1)
                        chain.link(v.reciprocal(total[:], total[:]))
                        chain.link(v.tensor_scalar(weight[:, 0:TOP], weight[:, 0:TOP], total[:], None, ALU.mult))
                        after(dve, stored, 16 * (R * n + r))
                        chain.link(v.tensor_copy(acc[:], rows[:, r]))
                        assert chain.count == HEAD, chain.count
                        chain.settle()
                        with dve.Fori(0, TOP) as lag:
                            chain.base, chain.count = (n * R + r) * (HEAD + TOP * LAG) + HEAD + lag * LAG, 0
                            v.tensor_copy(turn[0][:, 0:L], rows[:, r])
                            chain.link(v.tensor_copy(turn[0][:, L:2 * L], rows[:, r]))
                            for i in range(BITS):
                                b = BITS - 1 - i
                                step, width = 1 << b, L + (1 << b) - 1
                                a, c = turn[i % 2], turn[1 - i % 2]
                                chain.link(v.tensor_scalar(c[:, 0:width], a[:, step:step + width], bit[:, b, bass.ds(lag, 1)], None, ALU.mult))
                                chain.link(v.scalar_tensor_tensor(c[:, 0:width], a[:, 0:width], nbit[:, b, bass.ds(lag, 1)],
                                                                  c[:, 0:width], ALU.mult, ALU.add))
                            chain.link(v.scalar_tensor_tensor(acc[:], turn[BITS % 2][:, 0:L], weight[:, bass.ds(lag, 1)], acc[:],
                                                              ALU.mult, ALU.add))
                            chain.link(v.tensor_copy(ntop[:], total[:]))
                            assert chain.count == LAG, chain.count
                        v.tensor_copy(ntop[:], total[:]).then_inc(z_ready, 1)

                every_batch(dve, batch)


def correlation_tables():
    j = np.arange(L, dtype=np.int64)
    cosine = np.cos(2 * np.pi * np.minimum(j, L - j) / L)
    sine = np.sin(2 * np.pi * j / L)
    freq = np.concatenate([np.arange(L // 2 + 1), np.arange(1, L // 2)]).astype(np.int64)
    is_sine = j > L // 2
    phase = (j[:, None] * freq[None, :]) % L
    fwd = np.where(is_sine[None, :], sine[phase], cosine[phase]) / np.sqrt(L / 2)
    once = (freq == 0) | (freq == L // 2)
    inv = cosine[phase.T] * np.where(once, 0.5, 1.0)[:, None]
    fwd = fwd.reshape(KT, P, KT, P).transpose(2, 1, 0, 3)
    inv = inv.reshape(KT, P, NBANK, BANK).transpose(2, 1, 0, 3)
    return np.ascontiguousarray(fwd, np.float32), np.ascontiguousarray(inv, np.float32)


def guard_flag(nc, consts, flag):
    with ExitStack() as st:
        bound, most, most_all = consts["g_lags"], consts["most"], consts["most_all"]
        reduced, step = [st.enter_context(nc.semaphore(x)) for x in ("reduced", "flag_step")]
        with nc.Block() as block:
            @block.gpsimd
            def _(pool):
                pool.wait_ge(step, 2)
                nc.gpsimd.partition_all_reduce(most_all[:], most[:], P, bass.bass_isa.ReduceOp.max).then_inc(reduced, 1)

            @block.vector
            def _(dve):
                nc.vector.scalar_tensor_tensor(bound[:], consts["g_energy"][:], L / 32.0, consts["g_lags"][:], ALU.mult,
                                               ALU.add).then_inc(step, 1)
                dve.wait_ge(step, 1)
                nc.vector.tensor_reduce(most[:], bound[:], AX.X, ALU.max).then_inc(step, 1)
                dve.wait_ge(reduced, 1)
                nc.vector.tensor_scalar(flag[:], most_all[:], -GUARD_GAP, None, ALU.is_gt).then_inc(step, 1)
                dve.wait_ge(step, 3)


def x2_in_place(nc, stored, nb):
    with nc.Block() as block:
        @block.sync
        def _(sp):
            wait_stored(sp, stored, nb)


def decoder_layer(nc, x, ctx_in, w_chunks, ag_in, b_rows, fwd_dram, inv_dram, ident_dram, expert_dram, forward_dram,
                  inverse_dram, out):
    rows = x.shape[0]
    x2 = nc.dram_tensor("x2_scratch", (rows, L), F32, kind="Internal").ap()
    z = nc.dram_tensor("z_scratch", (rows, L), F32, kind="Internal").ap()
    with ExitStack() as st:
        def sb(name, shape, dt):
            return st.enter_context(nc.sbuf_tensor(name, shape, dt))

        def stored_sems(tag):
            return [[st.enter_context(nc.semaphore(f"stored{i}{r}_{tag}")) for r in range(R)] for i in range(2)]

        nb = rows // C
        consts = dict(
            ident=sb("ident", [P, P], F32), ident_bf16=sb("ident_bf16", [P, P], BF16),
            ident_f16=sb("ident_f16", [P, P], F16),
            columns=sb("columns", [P, 4, R], F32), pad=sb("pad", [P, 1], F32), expert_ids=sb("expert_ids", [P, EXPERTS], F32),
            g_lags=sb("g_lags", [P, rows // P], F32), g_energy=sb("g_energy", [P, rows // P], F32),
            xn0=sb("xn0", [P, L], F32), ag_raw=sb("ag_raw", [P, KT * AG], F32),
            chunks=[sb(f"chunk{c}", [P, KC, BANK], F32) for c in range(PREFETCHED)],
            most=sb("most", [P, 1], F32), most_all=sb("most_all", [P, 1], F32),
            w_scale=sb("w_scale", [P, 1], F32), w_iscale=sb("w_iscale", [P, 1], F32),
            fwd_dram=fwd_dram, inv_dram=inv_dram, ident_dram=ident_dram, expert_dram=expert_dram)
        flag = sb("flag", [P, 1], I32)
        setup(nc, consts)
        stored, stored_again = stored_sems("fast"), stored_sems("full")
        attention_pass(nc, x, ctx_in, x2, w_chunks, b_rows, ag_in, consts, stored, EPS4_AT, "fast")
        guard_flag(nc, consts, flag)
        some_row_needs_it = nc.values_load(flag[0:1, 0:1], min_val=0, max_val=1)
        with nc.If(some_row_needs_it):
            autocorrelation(nc, x, z, forward_dram, inverse_dram, consts, stored)
            attention_pass(nc, z, ctx_in, x2, w_chunks, b_rows, ag_in, consts, stored_again, EPS_AT, "full")
            x2_in_place(nc, stored_again, nb)
        feed_forward(nc, x2, out, w_chunks, b_rows, consts, stored)


def kernel(x, ctx_4096, L0_ffn_W_base, L0_ffn_gate_W, L0_ffn_A, L0_ffn_B):
    import ml_dtypes
    import concourse.bacc as bacc
    from concourse.bass_utils import run_bass_kernel_spmd

    shape = x.shape
    fwd, inv = guard_tables()
    forward, inverse = correlation_tables()
    arrays = {
        "x": np.ascontiguousarray(x).reshape(-1, L),
        "ctx_in": np.ascontiguousarray(ctx_4096).reshape(-1, L),
        "w_chunks": np.ascontiguousarray(
            L0_ffn_W_base.reshape(NBANK, BANK, KT // 4, 4, P).transpose(0, 2, 4, 3, 1)).reshape(KT, P, L),
        "ag_in": np.ascontiguousarray(
            np.concatenate([L0_ffn_A.reshape(ER, L), L0_ffn_gate_W]).reshape(AG, KT, P).transpose(2, 1, 0)),
        "b_rows": np.ascontiguousarray(np.transpose(L0_ffn_B, (0, 2, 1))).reshape(ER, L),
        "fwd_dram": fwd.astype(ml_dtypes.bfloat16),
        "inv_dram": inv.astype(ml_dtypes.bfloat16),
        "forward_dram": forward,
        "inverse_dram": inverse,
        "ident_dram": np.eye(P, dtype=np.float32),
        "expert_dram": np.tile(np.arange(EXPERTS, dtype=np.float32), (P, 1)),
    }
    nc = bacc.Bacc("TRN2", target_bir_lowering=False, num_devices=1)
    aps = {n: nc.dram_tensor(n, a.shape, mybir.dt.from_np(a.dtype), kind="ExternalInput").ap() for n, a in arrays.items()}
    out = nc.dram_tensor("out", arrays["x"].shape, F32, kind="ExternalOutput").ap()
    decoder_layer(nc, out=out, **aps)
    r = run_bass_kernel_spmd(nc, [arrays], core_ids=[0])
    return r.results[0]["out"].reshape(shape)
```
